# Optimizing a Trainium2 kernel written in Bass

```python
import numpy as np
import jax
import jax.numpy as jnp

def _softmax(x, axis=-1):
    return jax.nn.softmax(x, axis=axis)

def _gelu(x):
    return jax.nn.gelu(x, approximate=True)

def _silu(x):
    return jax.nn.silu(x)

def _sigmoid(x):
    return jax.nn.sigmoid(x)

def _layernorm(x, axis=-1, eps=1e-05):
    m = jnp.mean(x, axis=axis, keepdims=True)
    v = jnp.var(x, axis=axis, keepdims=True)
    return (x - m) / jnp.sqrt(v + eps)

def _scatter_add(tgt, idx, src, axis=0):
    return tgt.at[idx].add(src)

def _segment_sum(src, seg, n):
    return jax.ops.segment_sum(src, seg, n)
kernel_name = 'mk_sandwich_d2_jaxref_r8_14a604'

def setup_inputs(seed: int=0):
    np.random.seed(seed)
    _w = jnp.asarray

    def _L0_attn_setup():
        import jax, jax.numpy as jnp
        import numpy as np
        EMB = 512
        HEADS = 32
        SCALE = 4
        D = EMB // HEADS
        HKV = HEADS // SCALE
        B, S = (2, 256)
        key = jax.random.key(seed)
        ks = jax.random.split(key, 7)
        std = 0.02
        return {'x': jax.random.normal(ks[0], (B, S, EMB), jnp.float32), 'Wq': jax.random.normal(ks[1], (EMB, D, HEADS), jnp.float32) * std, 'bq': jnp.zeros((D, HEADS), jnp.float32), 'Wk': jax.random.normal(ks[2], (EMB, D, HKV), jnp.float32) * std, 'bk': jnp.zeros((D, HKV), jnp.float32), 'Wv': jax.random.normal(ks[3], (EMB, D, HKV), jnp.float32) * std, 'bv': jnp.zeros((D, HKV), jnp.float32)}
    _L0_attn_in = _L0_attn_setup()

    def _L0_ffn_setup():
        import jax, jax.numpy as jnp
        import numpy as np
        HID, INT, LAT, NE, K = (512, 1024, 256, 8, 2)
        LN_EPS = 1e-05

        def _layernorm(x, gamma, beta):
            mu = jnp.mean(x, axis=-1, keepdims=True)
            var = jnp.var(x, axis=-1, keepdims=True)
            return (x - mu) * jax.lax.rsqrt(var + LN_EPS) * gamma + beta
        key = jax.random.key(seed)
        ks = jax.random.split(key, 8)
        s = lambda d: 1.0 / np.sqrt(d)
        return {'hidden_states': jax.random.normal(ks[0], (4, 256, HID), jnp.float32), 'gate_w': jax.random.normal(ks[1], (HID, NE), jnp.float32) * s(HID), 'up_w': jax.random.normal(ks[2], (HID, INT), jnp.float32) * s(HID), 'down_w': jax.random.normal(ks[3], (INT, HID), jnp.float32) * s(INT), 'fc1_w': jax.random.normal(ks[4], (HID, LAT), jnp.float32) * s(HID), 'fc2_w': jax.random.normal(ks[5], (LAT, HID), jnp.float32) * s(LAT), 'expert_w': jax.random.normal(ks[6], (LAT, LAT), jnp.float32), 'ln_gamma': jnp.ones((HID,), jnp.float32), 'ln_beta': jnp.zeros((HID,), jnp.float32)}
    _L0_ffn_in = _L0_ffn_setup()

    def _L1_attn_setup():
        import jax, jax.numpy as jnp
        import numpy as np
        B, S, E, H = (2, 256, 512, 32)
        D = E // H
        ROPE_BASE = 10000.0
        MASK_VAL = -66504.0

        def _rope(x, cos, sin):
            x1, x2 = jnp.split(x, 2, axis=-1)
            return jnp.concatenate([x1 * cos - x2 * sin, x2 * cos + x1 * sin], axis=-1)
        key = jax.random.key(seed)
        k1, k2, k3, k4, k5 = jax.random.split(key, 5)
        return {'hidden_states': jax.random.normal(k1, (B, S, E), dtype=jnp.float32), 'qkv_w': jax.random.normal(k2, (E, 3 * E), dtype=jnp.float32) * 0.02, 'qkv_b': jax.random.normal(k3, (3 * E,), dtype=jnp.float32) * 0.02, 'out_w': jax.random.normal(k4, (E, E), dtype=jnp.float32) * 0.02, 'out_b': jax.random.normal(k5, (E,), dtype=jnp.float32) * 0.02}
    _L1_attn_in = _L1_attn_setup()

    def _L1_ffn_setup():
        import jax, jax.numpy as jnp
        import numpy as np
        IMAGE_START_POS = 34
        Q_START = IMAGE_START_POS + 72 + 1
        Q_END = -1
        LORA_ALPHA = 32
        LORA_RANK = 16
        SCALING = LORA_ALPHA / LORA_RANK
        key = jax.random.key(seed)
        ks = jax.random.split(key, 7)
        B_, S, D, O, E, R = (4, 256, 512, 512, 8, LORA_RANK)
        s = 0.02
        return {'x': jax.random.normal(ks[0], (B_, S, D), jnp.float32), 'W': jax.random.normal(ks[1], (O, D), jnp.float32) * s, 'b': jax.random.normal(ks[2], (O,), jnp.float32) * s, 'A': jax.random.normal(ks[3], (E, R, D), jnp.float32) * s, 'B': jax.random.normal(ks[4], (E, O, R), jnp.float32) * s, 'router_W': jax.random.normal(ks[5], (E, D), jnp.float32) * s, 'router_b': jax.random.normal(ks[6], (E,), jnp.float32) * s}
    _L1_ffn_in = _L1_ffn_setup()
    _d = {'L0_attn_x': _L0_attn_in['x'], 'L0_attn_Wq': _L0_attn_in['Wq'], 'L0_attn_bq': _L0_attn_in['bq'], 'L0_attn_Wk': _L0_attn_in['Wk'], 'L0_attn_bk': _L0_attn_in['bk'], 'L0_attn_Wv': _L0_attn_in['Wv'], 'L0_attn_bv': _L0_attn_in['bv'], 'L0_ffn_gate_w': _L0_ffn_in['gate_w'], 'L0_ffn_up_w': _L0_ffn_in['up_w'], 'L0_ffn_down_w': _L0_ffn_in['down_w'], 'L0_ffn_fc1_w': _L0_ffn_in['fc1_w'], 'L0_ffn_fc2_w': _L0_ffn_in['fc2_w'], 'L0_ffn_expert_w': _L0_ffn_in['expert_w'], 'L0_ffn_ln_gamma': _L0_ffn_in['ln_gamma'], 'L0_ffn_ln_beta': _L0_ffn_in['ln_beta'], 'L1_attn_qkv_w': _L1_attn_in['qkv_w'], 'L1_attn_qkv_b': _L1_attn_in['qkv_b'], 'L1_attn_out_w': _L1_attn_in['out_w'], 'L1_attn_out_b': _L1_attn_in['out_b'], 'L1_ffn_W': _L1_ffn_in['W'], 'L1_ffn_b': _L1_ffn_in['b'], 'L1_ffn_A': _L1_ffn_in['A'], 'L1_ffn_B': _L1_ffn_in['B'], 'L1_ffn_router_W': _L1_ffn_in['router_W'], 'L1_ffn_router_b': _L1_ffn_in['router_b']}
    _x0 = _d['L0_attn_x']
    _d['L0_attn_x'] = jax.random.normal(jax.random.fold_in(jax.random.key(seed), 1), (2, 1024, 512), dtype=_x0.dtype)
    del _x0
    return _d

def reference(L0_attn_x, L0_attn_Wq, L0_attn_bq, L0_attn_Wk, L0_attn_bk, L0_attn_Wv, L0_attn_bv, L0_ffn_gate_w, L0_ffn_up_w, L0_ffn_down_w, L0_ffn_fc1_w, L0_ffn_fc2_w, L0_ffn_expert_w, L0_ffn_ln_gamma, L0_ffn_ln_beta, L1_attn_qkv_w, L1_attn_qkv_b, L1_attn_out_w, L1_attn_out_b, L1_ffn_W, L1_ffn_b, L1_ffn_A, L1_ffn_B, L1_ffn_router_W, L1_ffn_router_b):

    def _L0_attn_ref(x, Wq, bq, Wk, bk, Wv, bv):
        import jax, jax.numpy as jnp
        import numpy as np
        EMB = 512
        HEADS = 32
        SCALE = 4
        D = EMB // HEADS
        HKV = HEADS // SCALE
        B, S = (2, 256)
        q = jnp.einsum('bse,edh->bsdh', x, Wq) + bq
        k = jnp.einsum('bse,edh->bsdh', x, Wk) + bk
        v = jnp.einsum('bse,edh->bsdh', x, Wv) + bv
        k = jnp.repeat(k, SCALE, axis=-1)
        v = jnp.repeat(v, SCALE, axis=-1)
        scores = jnp.einsum('bsdh,bseh->bsde', q, k) / np.float32(np.sqrt(D))
        attn = jax.nn.softmax(scores, axis=-1)
        out = jnp.einsum('bsde,bseh->bsdh', attn, v)
        return out.reshape(x.shape[:-1] + (EMB,))

    def _L0_ffn_ref(hidden_states, gate_w, up_w, down_w, fc1_w, fc2_w, expert_w, ln_gamma, ln_beta):
        import jax, jax.numpy as jnp
        import numpy as np
        HID, INT, LAT, NE, K = (512, 1024, 256, 8, 2)
        LN_EPS = 1e-05

        def _layernorm(x, gamma, beta):
            mu = jnp.mean(x, axis=-1, keepdims=True)
            var = jnp.var(x, axis=-1, keepdims=True)
            return (x - mu) * jax.lax.rsqrt(var + LN_EPS) * gamma + beta
        logits = jnp.einsum('bsh,he->bse', hidden_states, gate_w)
        routing_weights, selected_experts = jax.lax.top_k(logits, K)
        h = jax.nn.relu(jnp.einsum('bsh,hi->bsi', hidden_states, up_w)) ** 2
        shared_out = jnp.einsum('bsi,ih->bsh', h, down_w)
        x_latent = jnp.einsum('bsh,hl->bsl', hidden_states, fc1_w)
        expert_out = jnp.einsum('bsl,lm->bsm', x_latent, expert_w)
        moe_out = expert_out * jnp.sum(routing_weights, axis=-1, keepdims=True)
        routed_out = jnp.einsum('bsl,lh->bsh', moe_out, fc2_w)
        return _layernorm(shared_out + routed_out, ln_gamma, ln_beta)

    def _L1_attn_ref(hidden_states, qkv_w, qkv_b, out_w, out_b):
        import jax, jax.numpy as jnp
        import numpy as np
        B, S, E, H = (2, 256, 512, 32)
        D = E // H
        ROPE_BASE = 10000.0
        MASK_VAL = -66504.0

        def _rope(x, cos, sin):
            x1, x2 = jnp.split(x, 2, axis=-1)
            return jnp.concatenate([x1 * cos - x2 * sin, x2 * cos + x1 * sin], axis=-1)
        b, s, e = hidden_states.shape
        qkv = hidden_states @ qkv_w + qkv_b
        q, k, v = jnp.split(qkv, 3, axis=-1)
        q = q.reshape(b, s, H, D)
        k = k.reshape(b, s, H, D)
        v = v.reshape(b, s, H, D)
        half = D // 2
        inv_freq = 1.0 / ROPE_BASE ** (jnp.arange(0, half, dtype=jnp.float32) / half)
        ang = jnp.arange(s, dtype=jnp.float32)[:, None] * inv_freq[None, :]
        cos = jnp.cos(ang)[None, :, None, :]
        sin = jnp.sin(ang)[None, :, None, :]
        q = _rope(q, cos, sin)
        k = _rope(k, cos, sin)
        scale = 1.0 / jnp.sqrt(jnp.asarray(D, dtype=hidden_states.dtype))
        scores = jnp.einsum('bqhd,bkhd->bhqk', q, k) * scale
        causal = jnp.tril(jnp.ones((s, s), dtype=scores.dtype))
        scores = scores + (1.0 - causal) * MASK_VAL
        probs = jax.nn.softmax(scores, axis=-1)
        ctx = jnp.einsum('bhqk,bkhd->bqhd', probs, v).reshape(b, s, e)
        return ctx @ out_w + out_b

    def _L1_ffn_ref(x, W, b, A, B, router_W, router_b):
        import jax, jax.numpy as jnp
        import numpy as np
        IMAGE_START_POS = 34
        Q_START = IMAGE_START_POS + 72 + 1
        Q_END = -1
        LORA_ALPHA = 32
        LORA_RANK = 16
        SCALING = LORA_ALPHA / LORA_RANK
        x_q = x[:, Q_START:Q_END, :]
        q = x_q.mean(axis=1)
        logits = q @ router_W.T + router_b
        routing = jax.nn.softmax(logits, axis=-1)
        base = x @ W.T + b
        t = jnp.einsum('bsd,erd->bser', x, A)
        lora = jnp.einsum('bser,eor,be->bso', t, B, routing) * SCALING
        return base + lora
    x = L0_attn_x
    x = x + _layernorm(_L0_attn_ref(_layernorm(x, axis=-1), L0_attn_Wq, L0_attn_bq, L0_attn_Wk, L0_attn_bk, L0_attn_Wv, L0_attn_bv), axis=-1)
    x = x + _layernorm(_L0_ffn_ref(_layernorm(x, axis=-1), L0_ffn_gate_w, L0_ffn_up_w, L0_ffn_down_w, L0_ffn_fc1_w, L0_ffn_fc2_w, L0_ffn_expert_w, L0_ffn_ln_gamma, L0_ffn_ln_beta), axis=-1)
    x = x + _layernorm(_L1_attn_ref(_layernorm(x, axis=-1), L1_attn_qkv_w, L1_attn_qkv_b, L1_attn_out_w, L1_attn_out_b), axis=-1)
    x = x + _layernorm(_L1_ffn_ref(_layernorm(x, axis=-1), L1_ffn_W, L1_ffn_b, L1_ffn_A, L1_ffn_B, L1_ffn_router_W, L1_ffn_router_b), axis=-1)
    return x

_drawn_inputs = setup_inputs


def setup_inputs(seed=0):
    import zlib

    import numpy as np

    out = dict(_drawn_inputs(seed))
    spreads = {'L0_attn_bq': (0.0, 0.1),
     'L0_attn_bk': (0.0, 0.1),
     'L0_attn_bv': (0.0, 0.1),
     'L0_ffn_ln_gamma': (1.0, 0.2),
     'L0_ffn_ln_beta': (0.0, 0.1)}
    factors = {'L1_ffn_b': 2.933, 'L1_ffn_router_W': 8.0, 'L1_ffn_router_b': 64.0}
    for name, (base, spread) in spreads.items():
        noise = np.random.default_rng([zlib.crc32(name.encode()), seed]).standard_normal(out[name].shape)
        drawn = base * np.exp(spread * noise) if base else spread * noise
        out[name] = jnp.asarray(drawn.astype(out[name].dtype))
    for name, factor in factors.items():
        out[name] = (out[name] * factor).astype(out[name].dtype)
    return out
```

```python
from contextlib import ExitStack

import concourse.bass as bass
import numpy as np
from concourse import mybir

F32 = mybir.dt.float32
BF16 = mybir.dt.bfloat16
ALU = mybir.AluOpType
ACT = mybir.ActivationFunctionType
X_AXIS = mybir.AxisListType.X

P = 128
NB, S, E = 2, 1024, 512
TILES = NB * S // P
BT = S // P
KC = E // P
D0, G0, R0 = 16, 8, 4
I0 = D0 * G0
INT, LAT, NE = 1024, 256, 8
H, HD = 32, 16
HALF = HD // 2
VW = 32
QH = 4
QUADS = NB * H // QH
BQ = H // QH
NEX, RANK = 8, 16
EPS = 1e-5
MASK = -66504.0
SCALE3 = HD ** -0.5
GT = 4
GR = GT * P
COPIES = 6
Q_PARTS = (0, 0, 0, 1, 1, 2)
K_PARTS = (0, 1, 2, 0, 1, 0)
KR = COPIES * HD
KM = KR + 3


class Chain:

    def __init__(self, eng, sem):
        self.eng, self.sem, self.base, self.k = eng, sem, 0, 0

    def begin(self, base):
        self.base, self.k = base, 0

    def mark(self, ins):
        ins.then_inc(self.sem, 1)
        self.k += 1
        return self.k

    def need(self, k=None):
        self.eng.wait_ge(self.sem, self.base + (self.k if k is None else k))

    def link(self, ins):
        self.mark(ins)
        self.need()

    def need_apart(self, passed):
        wait_apart(self.eng, self.sem, self.base + self.k, passed)


def wait_apart(eng, sem, count, passed):
    eng.wait_ge(sem, count)
    eng.sem_inc(passed, 1)


def layers(nc, ins, out):
    with ExitStack() as whole:
        def at(stack, make, name, shape, dt=F32):
            return stack.enter_context(make(name, shape, dt))

        def sem(name):
            return whole.enter_context(nc.semaphore(name))

        def sb(name, shape, dt=F32, stack=whole):
            return at(stack, nc.sbuf_tensor, name, shape, dt)

        xs = sb("xs", [P, TILES, E])
        ident = sb("ident", [P, P])
        psum = whole.enter_context(nc.psum_tensor("psum", [P, 8, 512], F32))

        q_scr = nc.dram_tensor("q_scr", [3, NB * E, S], BF16).ap()
        k_scr = nc.dram_tensor("k_scr", [3, NB * E, S], BF16).ap()
        v_scr = nc.dram_tensor("v_scr", [TILES, P, H * VW], F32).ap()

        x_in = [sem(f"x_in{c}") for c in range(4)]
        const_in = sem("const_in")
        passed_v = sem("passed_v")
        passed_p = sem("passed_p")

        def finish_stats(dve, act_var, act_sd, chain, st, tmp, n, count, var_at, sd_at):
            nc.vector.tensor_tensor(tmp[:, 0, 0:n], st[:, 0:n, 1], st[:, 0:n, 4], ALU.add)
            nc.vector.tensor_tensor(tmp[:, 1, 0:n], st[:, 0:n, 1], st[:, 0:n, 4], ALU.subtract)
            chain.link(nc.vector.tensor_tensor(tmp[:, 2, 0:n], st[:, 0:n, 2], st[:, 0:n, 5], ALU.add))
            nc.vector.tensor_scalar(tmp[:, 0, 0:n], tmp[:, 0, 0:n], 0.5, None, ALU.mult)
            chain.link(nc.vector.scalar_tensor_tensor(out=tmp[:, 3, 0:n], in0=tmp[:, 1, 0:n], scalar=0.25,
                                                      in1=tmp[:, 1, 0:n], op0=ALU.mult, op1=ALU.mult))
            nc.vector.scalar_tensor_tensor(out=tmp[:, 4, 0:n], in0=tmp[:, 2, 0:n], scalar=1.0 / count,
                                           in1=tmp[:, 3, 0:n], op0=ALU.mult, op1=ALU.add).then_inc(act_var, 1)
            dve.wait_ge(act_sd, sd_at)
            chain.link(nc.vector.reciprocal(tmp[:, 5, 0:n], tmp[:, 4, 0:n]))

        def root(act, act_var, act_sd, tmp, n, var_at):
            act.wait_ge(act_var, var_at)
            nc.scalar.activation(tmp[:, 4, 0:n], tmp[:, 4, 0:n], ACT.Sqrt,
                                 bias=eps[:, 0:1]).then_inc(act_sd, 1)

        eps = sb("eps", [P, 1])

        b_stack = whole.enter_context(ExitStack())
        mixed = sb("mixed", [P, TILES, I0], stack=b_stack)
        mixed_st = sb("mixed_st", [P, TILES, 6], stack=b_stack)
        up = sb("up", [P, KC, INT], stack=b_stack)
        down = sb("down", [P, INT // P, E], stack=b_stack)
        fc1 = sb("fc1", [P, KC, LAT], stack=b_stack)
        lat_out = sb("lat_out", [P, LAT // P, E], stack=b_stack)
        gate = sb("gate", [P, KC, NE], stack=b_stack)
        w3 = sb("w3", [P, KC, 3 * E], stack=b_stack)
        b3 = sb("b3", [P, 3 * E], stack=b_stack)
        gamma = sb("gamma", [P, E], stack=b_stack)
        beta = sb("beta", [P, E], stack=b_stack)
        rope_c = sb("rope_c", [P, BT, HD], stack=b_stack)
        rope_s = sb("rope_s", [P, BT, HD], stack=b_stack)
        w_b = sem("w_b")
        W_B = 16 * 10

        with ExitStack() as sa:
            wq0 = sb("wq0", [P, KC, I0 * R0], stack=sa)
            w0 = sb("w0", [P, KC, 3 * I0], stack=sa)
            bq0 = sb("bq0", [P, I0 * R0], stack=sa)
            b0 = sb("b0", [P, 3 * I0], stack=sa)
            expert_t = sb("expert_t", [P, LAT // P, LAT], stack=sa)
            fc2 = sb("fc2", [P, LAT // P, E], stack=sa)
            st = sb("a_st", [P, TILES, 6], stack=sa)
            tmp = sb("a_tmp", [P, 6, TILES], stack=sa)
            xn = sb("a_xn", [P, 2, E], stack=sa)
            xt = sb("a_xt", [P, 2, E], stack=sa)
            qkv = sb("a_qkv", [P, 2, 3 * I0], stack=sa)
            prod = sb("a_prod", [P, 2, D0 * D0 * G0], stack=sa)
            prov = sb("a_prov", [P, 2, D0 * D0 * G0], stack=sa)
            sc = sb("a_sc", [P, 2, D0 * D0], stack=sa)
            pr = sb("a_pr", [P, 2, D0 * D0], stack=sa)
            mx = sb("a_mx", [P, D0], stack=sa)
            ls = sb("a_ls", [P, 4, D0], stack=sa)
            av = sb("a_av", [P, I0], stack=sa)

            w_a = sem("w_a")
            a_w0 = sem("a_w0")
            a_var = sem("a_var")
            a_sd = sem("a_sd")
            a_xn = sem("a_xn")
            a_tp = sem("a_tp")
            a_xt = sem("a_xt")
            a_pq = sem("a_pq")
            a_qkv = sem("a_qkv")
            a_p1 = sem("a_p1")
            a_s = sem("a_s")
            a_p = sem("a_p")
            a_p2 = sem("a_p2")
            a_v = sem("a_v")
            a_ef = sem("a_ef")
            a_efc = sem("a_efc")
            DP = 4
            SPLIT = DP * D0 * G0

            with nc.Block() as block:
                @block.sync
                def _(sp):
                    for c in range(4):
                        sp.dma_start(xs[:, 4 * c:4 * c + 4, :],
                                     ins["x"][512 * c:512 * c + 512, :].rearrange("(t p) e -> p t e", p=P)
                                     ).then_inc(x_in[c], 16)
                        if c == 0:
                            sp.dma_start(ident[:, :], ins["ident"]).then_inc(const_in, 16)
                            sp.dma_start(wq0[:, :, :], ins["wq0"].rearrange("(k p) n -> p k n", p=P)).then_inc(w_a, 16)
                            sp.dma_start(w0[:, :, I0:2 * I0],
                                         ins["wk0"].rearrange("(k p) n -> p k n", p=P)).then_inc(w_a, 16)
                            sp.dma_start(w0[:, :, 2 * I0:3 * I0],
                                         ins["wv0"].rearrange("(k p) n -> p k n", p=P)).then_inc(w_a, 16)
                            sp.dma_start(bq0[:, :], ins["bq0"].partition_broadcast(P)).then_inc(w_a, 16)
                            sp.dma_start(b0[:, I0:2 * I0], ins["bk0"].partition_broadcast(P)).then_inc(w_a, 16)
                            sp.dma_start(b0[:, 2 * I0:3 * I0], ins["bv0"].partition_broadcast(P)).then_inc(w_a, 16)
                    sp.dma_start(expert_t[:, :, :],
                                 ins["expert_t"].rearrange("(k p) n -> p k n", p=P)).then_inc(w_a, 16)
                    sp.dma_start(fc2[:, :, :], ins["fc2"].rearrange("(k p) n -> p k n", p=P)).then_inc(w_a, 16)
                    for dst, name in ((up, "up"), (down, "down"), (fc1, "fc1"), (gate, "gate"), (w3, "w3"),
                                      (rope_c, "rope_c"), (rope_s, "rope_s")):
                        sp.dma_start(dst[:, :, :], ins[name].rearrange("(k p) n -> p k n", p=P)).then_inc(w_b, 16)
                    sp.dma_start(b3[:, :], ins["b3"].partition_broadcast(P)).then_inc(w_b, 16)
                    sp.dma_start(gamma[:, :], ins["gamma"].partition_broadcast(P)).then_inc(w_b, 16)
                    sp.dma_start(beta[:, :], ins["beta"].partition_broadcast(P)).then_inc(w_b, 16)

                @block.vector
                def _(dve):
                    ch = Chain(dve, a_v)
                    ch.link(nc.vector.memset(eps[:, :], EPS))
                    for c in range(4):
                        dve.wait_ge(x_in[c], 16)
                        for t in range(4 * c, 4 * c + 4):
                            i = nc.vector.bn_stats(st[:, t, :], xs[:, t, :])
                    ch.link(i)
                    dve.wait_ge(w_a, 16 * 8)
                    nc.vector.tensor_reduce(w0[:, :, 0:I0], wq0[:, :, :].rearrange("p k (i r) -> p k i r", r=R0),
                                            X_AXIS, ALU.add)
                    nc.vector.tensor_reduce(b0[:, 0:I0], bq0[:, :].rearrange("p (i r) -> p i r", r=R0),
                                            X_AXIS, ALU.add).then_inc(a_w0, 1)
                    finish_stats(dve, a_var, a_sd, ch, st, tmp, TILES, E, 1, 1)
                    head = ch.k

                    def normalise(n, u):
                        nc.vector.tensor_scalar(xn[:, u, :], tile_of(xs, n), col_of(tmp, 0, n), col_of(tmp, 5, n),
                                                ALU.subtract, ALU.mult).then_inc(a_xn, 1)

                    def tile_of(a, n):
                        return a[:, bass.ds(n, 1), :].rearrange("p o e -> p (o e)")

                    def col_of(a, row, n):
                        return a[:, row, bass.ds(n, 1)]

                    def evacuate(n, u):
                        dve.wait_ge(a_pq, n + 1)
                        nc.vector.tensor_tensor(qkv[:, u, :], psum[:, 2 + u, 0:3 * I0], b0[:, :],
                                                ALU.add).then_inc(a_qkv, 1)

                    def weigh(n, u):
                        dve.wait_ge(a_p1, n + 1)
                        s2 = sc[:, u, :].rearrange("p (d e) -> p d e", d=D0)
                        ch.link(nc.vector.tensor_reduce(sc[:, u, :], prod[:, u, :].rearrange("p (i g) -> p i g", g=G0),
                                                        X_AXIS, ALU.add))
                        ch.link(nc.vector.tensor_reduce(mx[:, :], s2, X_AXIS, ALU.max))
                        nc.vector.tensor_tensor(s2, s2, mx[:, :].rearrange("p (d o) -> p d o", o=1)
                                                .broadcast_to([P, D0, D0]), ALU.subtract).then_inc(a_s, 1)

                    def share(n, u):
                        dve.wait_ge(a_p, n + 1)
                        p2 = pr[:, u, :].rearrange("p (d e) -> p d e", d=D0)
                        ch.mark(nc.vector.tensor_reduce(ls[:, u, :], p2, X_AXIS, ALU.add))
                        v3 = qkv[:, u, 2 * I0:3 * I0].rearrange("p (e g) -> p g e", g=G0)
                        for d in range(DP):
                            last = nc.vector.tensor_tensor(
                                prov[:, u, d * D0 * G0:(d + 1) * D0 * G0].rearrange("p (g e) -> p g e", g=G0),
                                p2[:, d:d + 1, :].broadcast_to([P, G0, D0]), v3, ALU.mult)
                        ch.need()
                        ch.link(nc.vector.reciprocal(ls[:, 2 + u, :], ls[:, u, :]))

                    def collect(n, u):
                        dve.wait_ge(a_p2, n + 1)
                        ch.link(nc.vector.tensor_reduce(av[:, :], prov[:, u, :].rearrange("p (i e) -> p i e", e=D0),
                                                        X_AXIS, ALU.add))
                        o = tile_of(mixed, n)
                        ch.mark(nc.vector.tensor_tensor(
                            o.rearrange("p (d g) -> p d g", g=G0), av[:, :].rearrange("p (d g) -> p d g", g=G0),
                            ls[:, 2 + u, :].rearrange("p (d o) -> p d o", o=1).broadcast_to([P, D0, G0]), ALU.mult))
                        ch.need_apart(passed_v)
                        nc.vector.bn_stats(tile_of(mixed_st, n), o)

                    FIRST_LINKS, LINKS = 4, 6

                    def step(n, u):
                        left = TILES - n if isinstance(n, int) else TILES
                        ch.begin(head + FIRST_LINKS + n * LINKS)
                        if left > 3:
                            normalise(n + 3, 1 - u)
                        if left > 1:
                            weigh(n + 1, 1 - u)
                        collect(n, u)
                        if left > 2:
                            evacuate(n + 2, u)
                        if left > 1:
                            share(n + 1, 1 - u)
                            assert ch.k == LINKS, ch.k

                    normalise(0, 0)
                    normalise(1, 1)
                    ch.begin(head)
                    evacuate(0, 0)
                    normalise(2, 0)
                    weigh(0, 0)
                    evacuate(1, 1)
                    share(0, 0)
                    assert ch.k == FIRST_LINKS, ch.k
                    with dve.Fori(0, TILES // 2 - 2) as it:
                        for u in range(2):
                            step(it * 2 + u, u)
                    for n in range(TILES - 4, TILES):
                        step(n, n % 2)

                @block.gpsimd
                def _(pool):
                    def scores(n, u):
                        pool.wait_ge(a_qkv, n + 1)
                        q = qkv[:, u, 0:I0].rearrange("p (d o g) -> p d o g", d=D0, o=1).broadcast_to([P, D0, D0, G0])
                        k = qkv[:, u, I0:2 * I0].rearrange("p (o e g) -> p o e g", o=1, e=D0)\
                            .broadcast_to([P, D0, D0, G0])
                        nc.gpsimd.tensor_tensor(prod[:, u, :].rearrange("p (d e g) -> p d e g", d=D0, e=D0), q, k,
                                                ALU.mult).then_inc(a_p1, 1)

                    def context(n, u):
                        pool.wait_ge(a_p, n + 1)
                        n_d = D0 - DP
                        p = pr[:, u, DP * D0:].rearrange("p (d o e) -> p d o e", d=n_d, o=1)\
                            .broadcast_to([P, n_d, G0, D0])
                        v = qkv[:, u, 2 * I0:3 * I0].rearrange("p (o e g) -> p o g e", o=1, g=G0)\
                            .broadcast_to([P, n_d, G0, D0])
                        nc.gpsimd.tensor_tensor(prov[:, u, SPLIT:].rearrange("p (d g e) -> p d g e", d=n_d, g=G0), p, v,
                                                ALU.mult).then_inc(a_p2, 1)

                    scores(0, 0)
                    scores(1, 1)
                    context(0, 0)
                    with pool.Fori(0, TILES // 2 - 1) as it:
                        for u in range(2):
                            context(it * 2 + (u + 1), 1 - u)
                            scores(it * 2 + (u + 2), u)
                    context(TILES - 1, 1)

                @block.scalar
                def _(act):
                    root(act, a_var, a_sd, tmp, TILES, 1)

                    def copy_xt(n, u):
                        act.wait_ge(a_tp, n + 1)
                        nc.scalar.activation(xt[:, u, :], psum[:, u, :], ACT.Copy).then_inc(a_xt, 1)

                    def exps(n, u):
                        act.wait_ge(a_s, n + 1)
                        nc.scalar.activation(pr[:, u, :], sc[:, u, :], ACT.Exp,
                                             scale=D0 ** -0.5).then_inc(a_p, 1)

                    copy_xt(0, 0)
                    copy_xt(1, 1)
                    copy_xt(2, 0)
                    exps(0, 0)
                    with act.Fori(0, TILES // 2 - 2) as it:
                        for u in range(2):
                            copy_xt(it * 2 + (u + 3), 1 - u)
                            exps(it * 2 + (u + 1), 1 - u)
                    copy_xt(TILES - 1, 1)
                    for n in range(TILES - 3, TILES):
                        exps(n, n % 2)
                    act.wait_ge(a_ef, 1)
                    nc.scalar.activation(lat_out[:, :, :].rearrange("p k n -> p (k n)"),
                                         psum[:, 4:6, :].rearrange("p k n -> p (k n)"), ACT.Copy).then_inc(a_efc, 1)

                @block.tensor
                def _(pe):
                    pe.wait_ge(const_in, 16)
                    pe.wait_ge(a_w0, 1)

                    def project(n, u):
                        pe.wait_ge(a_xn, n + 1)
                        for c in range(KC):
                            last = nc.tensor.transpose(psum[:, u, c * P:(c + 1) * P], xn[:, u, c * P:(c + 1) * P],
                                                       ident[:, :])
                        last.then_inc(a_tp, 1)
                        pe.wait_ge(a_xt, n + 1)
                        for c in range(KC):
                            last = nc.tensor.matmul(psum[:, 2 + u, 0:3 * I0], xt[:, u, c * P:(c + 1) * P],
                                                    w0[:, c, :], start=(c == 0), stop=(c == KC - 1))
                        last.then_inc(a_pq, 1)

                    with pe.Fori(0, TILES // 2) as it:
                        for u in range(2):
                            project(it * 2 + u, u)
                    for lc in range(LAT // P):
                        for mc in range(LAT // P):
                            last = nc.tensor.matmul(psum[:, 4 + lc, :], expert_t[:, mc, lc * P:(lc + 1) * P],
                                                    fc2[:, mc, :], start=(mc == 0), stop=(mc == LAT // P - 1))
                    last.then_inc(a_ef, 1)

        with ExitStack() as sbk:
            mtmp = sb("b_mtmp", [P, 6, TILES], stack=sbk)
            st = sb("b_st", [P, GT, 6], stack=sbk)
            tmp = sb("b_tmp", [P, 6, GT], stack=sbk)
            ln = sb("b_ln", [P, 2, I0], stack=sbk)
            rows = sb("b_rows", [P, GT, E], stack=sbk)
            xt = sb("b_xt", [P, KC, GR], stack=sbk)
            hr = sb("b_hr", [P, 2, GR], stack=sbk)
            ht = sb("b_ht", [P, INT // P, GR], stack=sbk)
            lt = sb("b_lt", [P, LAT // P, GR], stack=sbk)
            sh = sb("b_sh", [P, 2, E], stack=sbk)
            top = sb("b_top", [P, GT, 8], stack=sbk)
            rw = sb("b_rw", [P, GT], stack=sbk)
            qk = sb("b_qk", [P, 2 * E], stack=sbk)
            rot = sb("b_rot", [P, 2 * E], stack=sbk)
            rest = sb("b_rest", [P, 2 * E], stack=sbk)
            parts = sb("b_parts", [P, 3, 2 * KC, 2 * P], BF16, stack=sbk)
            v32 = sb("b_v32", [P, H, VW], stack=sbk)

            b_v = sem("b_v")
            b_mv = sem("b_mv")
            b_ms = sem("b_ms")
            b_var = sem("b_var")
            b_sd = sem("b_sd")
            b_xn = sem("b_xn")
            b_tp = sem("b_tp")
            b_xt = sem("b_xt")
            b_up = sem("b_up")
            b_hr = sem("b_hr")
            b_h = sem("b_h")
            b_gate = sem("b_gate")
            b_dn = sem("b_dn")
            b_sh = sem("b_sh")
            b_y = sem("b_y")
            b_qkv = sem("b_qkv")
            b_ev = sem("b_ev")
            b_vs = sem("b_vs")
            b_rot = sem("b_rot")
            b_qk = sem("b_qk")
            b_tq = sem("b_tq")
            b_p1 = sem("b_p1")
            b_r = sem("b_r")
            b_p2 = sem("b_p2")
            b_p3 = sem("b_p3")
            b_vo = sem("b_vo")
            b_qo = sem("b_qo")
            b_c = sem("b_c")
            G = TILES // GT
            N_UP = INT // P
            N_U = N_UP + LAT // P

            with nc.Block() as block:
                @block.sync
                def _(sp):
                    with sp.Fori(0, G) as g:
                        for t in range(GT):
                            sp.wait_ge(b_vs, g * GT + (t + 1))
                            sp.dma_start(v_scr[bass.ds(g * GT + t, 1), :, :].rearrange("o p n -> p (o n)"),
                                         v32[:, :, :].rearrange("p h w -> p (h w)")).then_inc(b_vo, 16)
                            if t % 2 == 1:
                                sp.wait_ge(b_p2, g * GT + (t + 1))
                                sp.wait_ge(b_p3, g * GT + (t + 1))
                                row = (g // 2) * E
                                col = (g % 2) * GR + (t // 2) * 2 * P
                                for j, scr in enumerate((q_scr, k_scr)):
                                    for part in range(3):
                                        sp.dma_start(
                                            scr[part, bass.ds(row, E), bass.ds(col, 2 * P)]
                                            .rearrange("(c p) n -> p c n", p=P),
                                            parts[:, part, j * KC:(j + 1) * KC, :]).then_inc(b_qo, 16)
                    sp.wait_ge(b_qo, TILES // 2 * 6 * 16 + 16)
                    sp.wait_ge(b_vo, (TILES + 1) * 16)

                @block.vector
                def _(dve):
                    ch = Chain(dve, b_v)
                    dve.sem_inc(b_vo, 16)
                    dve.sem_inc(b_tq, 1)
                    dve.wait_ge(w_b, W_B)
                    finish_stats(dve, b_mv, b_ms, ch, mixed_st, mtmp, TILES, I0, 1, 1)
                    head = ch.k

                    def tile_of(a, n):
                        return a[:, bass.ds(n, 1), :].rearrange("p o e -> p (o e)")

                    def finish(g, k):
                        finish_stats(dve, b_var, b_sd, ch, st, tmp, GT, E, None, g * 4 + (k + 1))

                    def scaled(dst, src, t):
                        return nc.vector.tensor_scalar(dst, src, tmp[:, 0, t:t + 1], tmp[:, 5, t:t + 1],
                                                       ALU.subtract, ALU.mult)

                    with dve.Fori(0, G) as g:
                        ch.begin(g * 35 + head)
                        for t in range(GT):
                            n = g * GT + t
                            ch.link(nc.vector.tensor_scalar(ln[:, t % 2, :], tile_of(mixed, n),
                                                            mtmp[:, 0, bass.ds(n, 1)], mtmp[:, 5, bass.ds(n, 1)],
                                                            ALU.subtract, ALU.mult))
                            x3 = tile_of(xs, n).rearrange("p (i r) -> p i r", r=R0)
                            ch.mark(nc.vector.tensor_tensor(
                                x3, x3, ln[:, t % 2, :].rearrange("p (i o) -> p i o", o=1).broadcast_to([P, I0, R0]),
                                ALU.add))
                            ch.need_apart(passed_v)
                            last = nc.vector.bn_stats(st[:, t, :], tile_of(xs, n))
                        ch.link(last)
                        finish(g, 0)
                        for t in range(GT):
                            scaled(rows[:, t, :], tile_of(xs, g * GT + t), t).then_inc(b_xn, 1)
                        wait_apart(dve, b_gate, g + 1, passed_v)
                        for t in range(GT):
                            last = nc.vector.max(top[:, t, :], psum[:, 6, t * NE:(t + 1) * NE])
                        ch.link(last)
                        ch.link(nc.vector.tensor_tensor(rw[:, :], top[:, :, 0], top[:, :, 1], ALU.add))
                        for t in range(GT):
                            dve.wait_ge(b_sh, g * GT + (t + 1))
                            i = nc.vector.scalar_tensor_tensor(
                                out=rows[:, t, :], in0=psum[:, 4 + t % 2, :], scalar=rw[:, t:t + 1],
                                in1=sh[:, t % 2, :], op0=ALU.mult, op1=ALU.add)
                            i.then_inc(b_y, 1)
                            dve.wait_ge(b_y, g * GT + (t + 1))
                            last = nc.vector.bn_stats(st[:, t, :], rows[:, t, :])
                        ch.link(last)
                        finish(g, 1)
                        for t in range(GT):
                            last = scaled(rows[:, t, :], rows[:, t, :], t)
                        ch.link(last)
                        for t in range(GT):
                            last = nc.vector.tensor_tensor(rows[:, t, :], rows[:, t, :], gamma[:, :], ALU.mult)
                        ch.link(last)
                        for t in range(GT):
                            last = nc.vector.tensor_tensor(rows[:, t, :], rows[:, t, :], beta[:, :], ALU.add)
                        ch.link(last)
                        for t in range(GT):
                            last = nc.vector.bn_stats(st[:, t, :], rows[:, t, :])
                        ch.link(last)
                        finish(g, 2)
                        for t in range(GT):
                            last = scaled(rows[:, t, :], rows[:, t, :], t)
                        ch.link(last)
                        for t in range(GT):
                            last = nc.vector.tensor_tensor(tile_of(xs, g * GT + t), tile_of(xs, g * GT + t),
                                                           rows[:, t, :], ALU.add)
                        ch.mark(last)
                        ch.need_apart(passed_v)
                        for t in range(GT):
                            last = nc.vector.bn_stats(st[:, t, :], tile_of(xs, g * GT + t))
                        ch.link(last)
                        finish(g, 3)
                        for t in range(GT):
                            scaled(rows[:, t, :], tile_of(xs, g * GT + t), t).then_inc(b_xn, 1)

                        def split(t):
                            n = g * GT + t
                            dve.wait_ge(b_p1, n + 1)
                            half = slice((t % 2) * P, (t % 2 + 1) * P)
                            pt = psum[:, 0:2, :].rearrange("p b (c n) -> p (b c) n", n=P)
                            r3 = rest[:, :].rearrange("p (c n) -> p c n", n=P)
                            nc.vector.tensor_tensor(r3, pt, parts[:, 0, :, half], ALU.subtract).then_inc(b_r, 1)
                            dve.wait_ge(b_p2, n + 1)
                            nc.vector.tensor_tensor(parts[:, 2, :, half], r3, parts[:, 1, :, half],
                                                    ALU.subtract).then_inc(b_p3, 1)

                        for t in range(GT):
                            n = g * GT + t
                            k0 = 2 + 3 * (t % 2)
                            dve.wait_ge(b_qkv, n + 1)
                            dve.wait_ge(b_tq, n + 1)
                            nc.vector.tensor_tensor(qk[:, :].rearrange("p (j n) -> p j n", j=2), psum[:, k0:k0 + 2, :],
                                                    b3[:, 0:2 * E].rearrange("p (j n) -> p j n", j=2),
                                                    ALU.add).then_inc(b_ev, 1)
                            dve.wait_ge(b_vo, (g * GT + t + 1) * 16)
                            if t == 0:
                                dve.wait_ge(b_c, 2)
                            nc.vector.tensor_tensor(v32[:, :, 0:HD], psum[:, k0 + 2, :].rearrange("p (h w) -> p h w", w=HD),
                                                    b3[:, 2 * E:3 * E].rearrange("p (h w) -> p h w", w=HD),
                                                    ALU.add).then_inc(b_vs, 1)
                            if t:
                                split(t - 1)
                            dve.wait_ge(b_rot, n + 1)
                            q3 = qk[:, :].rearrange("p (h w) -> p h w", w=HD)
                            pos = (g % 2) * GT + t
                            cos = rope_c[:, bass.ds(pos, 1), :].broadcast_to([P, 2 * H, HD])
                            ch.link(nc.vector.tensor_tensor(q3, q3, cos, ALU.mult))
                            nc.vector.tensor_tensor(qk[:, :], qk[:, :], rot[:, :], ALU.add).then_inc(b_qk, 1)
                        split(GT - 1)
                        assert ch.k == 35, ch.k

                @block.gpsimd
                def _(pool):
                    nc.gpsimd.memset(v32[:, :, HD:VW], 0.0).then_inc(b_c, 1)
                    pool.wait_ge(b_c, 1)
                    nc.gpsimd.memset(v32[:, :, HD:HD + 1], 1.0).then_inc(b_c, 1)
                    with pool.Fori(0, G) as g:
                        for j in range(N_UP):
                            pool.wait_ge(b_hr, g * N_U + (j + 1))
                            nc.gpsimd.tensor_tensor(ht[:, j, :], hr[:, j % 2, :], hr[:, j % 2, :],
                                                    ALU.mult).then_inc(b_h, 1)
                        for t in range(GT):
                            pool.wait_ge(b_ev, g * GT + (t + 1))
                            q4 = qk[:, :].rearrange("p (h j w) -> p h j w", j=2, w=HALF)
                            r4 = rot[:, :].rearrange("p (h j w) -> p h j w", j=2, w=HALF)
                            s = rope_s[:, bass.ds((g % 2) * GT + t, 1), :]
                            nc.gpsimd.tensor_tensor(r4[:, :, 0, :], q4[:, :, 1, :],
                                                    s[:, :, 0:HALF].broadcast_to([P, 2 * H, HALF]), ALU.mult)
                            nc.gpsimd.tensor_tensor(r4[:, :, 1, :], q4[:, :, 0, :],
                                                    s[:, :, HALF:HD].broadcast_to([P, 2 * H, HALF]),
                                                    ALU.mult).then_inc(b_rot, 1)

                @block.scalar
                def _(act):
                    act.sem_inc(b_qo, 16)
                    root(act, b_mv, b_ms, mtmp, TILES, 1)
                    with act.Fori(0, G) as g:
                        def copy_xt(first):
                            for t in range(GT):
                                act.wait_ge(b_tp, g * 2 * GT + (first + t + 1))
                                nc.scalar.activation(xt[:, :, t * P:(t + 1) * P],
                                                     psum[:, t % 2, :].rearrange("p (c n) -> p c n", n=P),
                                                     ACT.Copy).then_inc(b_xt, 1)

                        root(act, b_var, b_sd, tmp, GT, g * 4 + 1)
                        copy_xt(0)
                        for j in range(N_U):
                            act.wait_ge(b_up, g * N_U + (j + 1))
                            if j < N_UP:
                                if j >= 2:
                                    act.wait_ge(b_h, g * N_UP + (j - 1))
                                nc.scalar.activation(hr[:, j % 2, :], psum[:, 2 + j % 2, :], ACT.Relu).then_inc(b_hr, 1)
                            else:
                                nc.scalar.activation(lt[:, j - N_UP, :], psum[:, 2 + j % 2, :],
                                                     ACT.Copy).then_inc(b_hr, 1)
                        for t in range(GT):
                            act.wait_ge(b_dn, g * GT + (t + 1))
                            if t >= 2:
                                act.wait_ge(b_y, g * GT + (t - 1))
                            nc.scalar.activation(sh[:, t % 2, :], psum[:, 2 + t % 2, :], ACT.Copy).then_inc(b_sh, 1)
                        for k in range(1, 4):
                            root(act, b_var, b_sd, tmp, GT, g * 4 + (k + 1))
                        copy_xt(GT)
                        for t in range(GT):
                            n = g * GT + t
                            half = slice((t % 2) * P, (t % 2 + 1) * P)
                            act.wait_ge(b_tq, n + 2)
                            if t % 2 == 0:
                                act.wait_ge(b_qo, (g * GT + t) * 3 * 16 + 16)
                            nc.scalar.activation(parts[:, 0, :, half],
                                                 psum[:, 0:2, :].rearrange("p b (c n) -> p (b c) n", n=P),
                                                 ACT.Copy).then_inc(b_p1, 1)
                            act.wait_ge(b_r, n + 1)
                            nc.scalar.activation(parts[:, 1, :, half], rest[:, :].rearrange("p (c n) -> p c n", n=P),
                                                 ACT.Copy).then_inc(b_p2, 1)

                @block.tensor
                def _(pe):
                    pe.wait_ge(w_b, W_B)
                    with pe.Fori(0, G) as g:
                        def turn(first):
                            for t in range(GT):
                                pe.wait_ge(b_xn, g * 2 * GT + (first + t + 1))
                                if t >= 2:
                                    pe.wait_ge(b_xt, g * 2 * GT + (first + t - 1))
                                for c in range(KC):
                                    last = nc.tensor.transpose(psum[:, t % 2, c * P:(c + 1) * P],
                                                               rows[:, t, c * P:(c + 1) * P], ident[:, :])
                                last.then_inc(b_tp, 1)

                        turn(0)
                        pe.wait_ge(b_xt, g * 2 * GT + GT)
                        for j in range(N_U):
                            if j >= 2:
                                pe.wait_ge(b_hr, g * N_U + (j - 1))
                            w = up[:, :, j * P:(j + 1) * P] if j < N_UP else fc1[:, :, (j - N_UP) * P:(j - N_UP + 1) * P]
                            for c in range(KC):
                                last = nc.tensor.matmul(psum[:, 2 + j % 2, :], w[:, c, :], xt[:, c, :],
                                                        start=(c == 0), stop=(c == KC - 1))
                            last.then_inc(b_up, 1)
                        for t in range(GT):
                            for c in range(KC):
                                last = nc.tensor.matmul(psum[:, 6, t * NE:(t + 1) * NE], xt[:, c, t * P:(t + 1) * P],
                                                        gate[:, c, :], start=(c == 0), stop=(c == KC - 1))
                        last.then_inc(b_gate, 1)
                        pe.wait_ge(b_hr, g * N_U + N_U)
                        pe.wait_ge(b_h, g * N_UP + N_UP)
                        for t in range(GT):
                            if t >= 2:
                                pe.wait_ge(b_y, g * GT + (t - 1))
                            for c in range(N_UP):
                                nc.tensor.matmul(psum[:, 2 + t % 2, :], ht[:, c, t * P:(t + 1) * P], down[:, c, :],
                                                 start=(c == 0), stop=(c == N_UP - 1))
                            for c in range(LAT // P):
                                last = nc.tensor.matmul(psum[:, 4 + t % 2, :], lt[:, c, t * P:(t + 1) * P],
                                                        lat_out[:, c, :], start=(c == 0), stop=(c == LAT // P - 1))
                            last.then_inc(b_dn, 1)
                        turn(GT)
                        pe.wait_ge(b_xt, g * 2 * GT + 2 * GT)

                        def turn_qk(t):
                            pe.wait_ge(b_qk, g * GT + (t + 1))
                            if t:
                                pe.wait_ge(b_r, g * GT + t)
                            for c in range(2 * KC):
                                last = nc.tensor.transpose(psum[:, c // KC, (c % KC) * P:(c % KC + 1) * P],
                                                           qk[:, c * P:(c + 1) * P], ident[:, :])
                            last.then_inc(b_tq, 1)

                        for t in range(GT):
                            if t >= 2:
                                pe.wait_ge(b_ev, g * GT + (t - 1))
                                pe.wait_ge(b_vs, g * GT + (t - 1))
                            for j in range(3):
                                for c in range(KC):
                                    last = nc.tensor.matmul(psum[:, 2 + 3 * (t % 2) + j, :], xt[:, c, t * P:(t + 1) * P],
                                                            w3[:, c, j * E:(j + 1) * E],
                                                            start=(c == 0), stop=(c == KC - 1))
                            last.then_inc(b_qkv, 1)
                            if t:
                                turn_qk(t - 1)
                        turn_qk(GT - 1)
        b_stack.close()


        wo = sb("wo", [P, KC, E])
        bo = sb("bo", [P, E])
        w4 = sb("w4", [P, KC, E])
        b4 = sb("b4", [P, E])
        lora_a = sb("lora_a", [P, E])
        lora_b = sb("lora_b", [P, E])
        route_w = sb("route_w", [P, KC, NEX])
        route_b = sb("route_b", [P, NEX])
        own = sb("own", [P, NEX])
        counted = sb("counted", [P, 3, P])
        ctx = sb("ctx", [P, QUADS // 2, BT, P])
        w_d = sem("w_d")
        W_D = 16 * 10

        batches = [(0, j) for j in range(BT // 2)] + [(1, j) for j in range(BT)]
        NBATCH = len(batches)
        PIECES = NBATCH * QH
        RING = BT * QH + 3
        DIAG = BT * QH

        def span(half, j):
            q0 = max(half * 512, j * P)
            return q0, half * 512 + 512 - q0

        def schedule(ahead):
            tiles = 0
            for m in range(NBATCH):
                for h in range(QH):
                    yield "piece", m * QH + h
                    if ahead and tiles < BT * QH and (m * QH + h) * 8 >= tiles * 9 - 8:
                        yield "tile", tiles
                        tiles += 1
                if m:
                    yield "pv", m - 1
                if m == 7:
                    yield "turn", 0
                if ahead and tiles == BT * QH:
                    yield "peak", 0
                    tiles += 1
            assert not ahead or tiles == BT * QH + 1
            yield "pv", NBATCH - 1
            yield "turn", 1

        with ExitStack() as sc_:
            q_stack = sb("q_stack", [P, 4, QH * BT, P], BF16, stack=sc_)
            qs = q_stack[:, :, :, :].rearrange("p u (h t) q -> p u h (t q)", h=QH)
            ks = sb("ks", [P, 4, QH, S], BF16, stack=sc_)
            vs = sb("vs", [P, 4, BT, QH * VW], stack=sc_)
            pt = sb("c_pt", [P, 2 * QH, 512], stack=sc_)
            junk = sb("c_junk", [P, 2, S], BF16, stack=sc_)
            causal = sb("c_causal", [P, S], stack=sc_)
            mx = sb("c_mx", [P, 2, QH * BT], stack=sc_)
            mp = sb("c_mp", [QH * BT, 3, P], BF16, stack=sc_)
            mr = sb("c_mr", [QH * BT, P], stack=sc_)
            ot = sb("c_ot", [P, S], stack=sc_)
            rec = sb("c_rec", [P, 2, BT // 2 * QH], stack=sc_)

            c_in = sem("c_in")
            c_ld = [sem(f"c_ld{u}") for u in range(4)]
            c_one = sem("c_one")
            c_ap = sem("c_ap")
            c_ac = sem("c_ac")
            c_mp = sem("c_mp")
            c_mrow = sem("c_mrow")
            c_v = sem("c_v")
            c_sb = sem("c_sb")
            c_ex = sem("c_ex")
            c_af = sem("c_af")
            c_o = sem("c_o")
            c_oe = sem("c_oe")
            LOADS = 2 * COPIES + 1

            with nc.Block() as block:
                @block.sync
                def _(sp):
                    def load(n, u):
                        for scr, dst, parts_ in ((k_scr, ks, K_PARTS), (q_scr, qs, Q_PARTS)):
                            for c, part in enumerate(parts_):
                                sp.dma_start(dst[c * HD:(c + 1) * HD, u, :, :],
                                             scr[part, bass.ds(n * QH * HD, QH * HD), :]
                                             .rearrange("(h d) s -> d h s", d=HD)).then_inc(c_ld[u], 16)
                        sp.dma_start(vs[:, u, :, :],
                                     v_scr[bass.ds((n // BQ) * BT, BT), :, bass.ds((n % BQ) * QH * VW, QH * VW)]
                                     .rearrange("t p n -> p t n")).then_inc(c_ld[u], 16)

                    load(0, 0)
                    sp.dma_start(causal[:, :], ins["causal"]).then_inc(c_in, 16)
                    for u in range(1, 4):
                        load(u, u)
                    for dst, name in ((wo, "wo"), (w4, "w4"), (route_w, "route_w")):
                        sp.dma_start(dst[:, :, :], ins[name].rearrange("(k p) n -> p k n", p=P)).then_inc(w_d, 16)
                    for dst, name in ((bo, "bo"), (b4, "b4"), (route_b, "route_b")):
                        sp.dma_start(dst[:, :], ins[name].partition_broadcast(P)).then_inc(w_d, 16)
                    for dst, name in ((lora_a, "lora_a"), (lora_b, "lora_b"), (own, "own")):
                        sp.dma_start(dst[:, :], ins[name]).then_inc(w_d, 16)
                    sp.dma_start(counted[:, :, :], ins["counted"].rearrange("p (a n) -> p a n", a=3)).then_inc(w_d, 16)

                    def peaks(n, u):
                        sp.wait_ge(c_mp, n + 1)
                        for j in range(3):
                            sp.dma_start(q_stack[KR + j:KR + j + 1, u, :, :],
                                         mp[:, j, :]).then_inc(c_mrow, 16)

                    peaks(0, 0)
                    with sp.Fori(0, QUADS // 4 - 1) as it:
                        for u in range(4):
                            n = it * 4 + u
                            peaks(n + 1, (u + 1) % 4)
                            sp.wait_ge(c_o, n * 2 + 2)
                            load(n + 4, u)
                    for u in range(3):
                        peaks(QUADS - 4 + u + 1, u + 1)
                    sp.wait_ge(c_mrow, QUADS * 48)

                @block.gpsimd
                def _(pool):
                    nc.gpsimd.memset(ks[KR:KM, :, :, :], 1.0).then_inc(c_one, 1)

                    def mask(n, u):
                        d = 0
                        for m, (half, j) in enumerate(batches):
                            if span(half, j)[0] != j * P:
                                continue
                            for h in range(QH):
                                p = m * QH + h
                                wait_apart(pool, c_ex, n * PIECES + (p + 1), passed_p)
                                blk = pt[:, p % (2 * QH), 0:P]
                                nc.gpsimd.affine_select(out=blk, in_=blk, compare_op=ALU.is_ge, fill=0.0, base=0,
                                                        pattern=[[1, P]], channel_multiplier=-1).then_inc(c_af, 1)
                                d += 1
                        assert d == DIAG

                    with pool.Fori(0, QUADS) as n:
                        mask(n, 0)

                @block.scalar
                def _(act):
                    with act.Fori(0, QUADS) as n:
                        for m, (half, j) in enumerate(batches):
                            w = span(half, j)[1]
                            for h in range(QH):
                                p = m * QH + h
                                act.wait_ge(c_sb, n * PIECES + (p + 1))
                                nc.scalar.activation(pt[:, p % (2 * QH), 0:w], psum[:, 4 + p % 2, 0:w], ACT.Exp,
                                                     scale=SCALE3).then_inc(c_ex, 1)
                            if m == 5 or m == NBATCH - 1:
                                b = int(m != 5)
                                act.wait_ge(c_o, n * 2 + (b + 1))
                                nc.scalar.activation(ot[:, b * 512:(b + 1) * 512], psum[:, 6 + b, :],
                                                     ACT.Copy).then_inc(c_oe, 1)

                @block.vector
                def _(dve):
                    ch = Chain(dve, c_v)
                    dve.wait_ge(c_in, 16)

                    def tile_max(s, slot, par, used):
                        i = s % BT
                        w = (i + 1) * P
                        wait_apart(dve, c_ap, used + 1, passed_v)
                        nc.vector.tensor_tensor_reduce(
                            out=junk[:, slot, 0:w], in0=psum[:, 2 * slot:2 * slot + 2, :].rearrange("p b n -> p (b n)")[:, 0:w],
                            in1=causal[:, S - w:S], scale=1.0, scalar=-3.4e38, op0=ALU.add, op1=ALU.max,
                            accum_out=mx[:, par, s:s + 1]).then_inc(c_ac, 1)

                    def peak_parts(slot, used):
                        dve.wait_ge(c_ap, used + 1)
                        t = psum[0:QH * BT, 2 * slot, 0:P]
                        ch.link(nc.vector.tensor_scalar(mp[:, 0, :], t, -1.0, None, ALU.mult))
                        nc.vector.scalar_tensor_tensor(out=mr[:, :], in0=t, scalar=-1.0, in1=mp[:, 0, :],
                                                       op0=ALU.mult, op1=ALU.subtract).then_inc(c_ac, 1)
                        dve.wait_ge(c_ac, used + 1)
                        ch.link(nc.vector.tensor_copy(mp[:, 1, :], mr[:, :]))
                        nc.vector.tensor_tensor(mp[:, 2, :], mr[:, :], mp[:, 1, :], ALU.subtract).then_inc(c_mp, 1)

                    def context(pair, i, half, slot, used):
                        dve.wait_ge(c_ap, used + 1)
                        c4 = psum[:, 2 * slot, :].rearrange("p (t h w) -> p t h w", h=QH, w=VW)
                        r4 = rec[:, half, :].rearrange("p (t h o) -> p t h o", h=QH, o=1)
                        ch.link(nc.vector.reciprocal(r4, c4[:, :, :, HD:HD + 1]))
                        o = ctx[:, bass.ds(pair, 1), half * 4:half * 4 + 4, i * QH * HD:(i + 1) * QH * HD]\
                            .rearrange("p o t (h d) -> p (o t) h d", d=HD)
                        nc.vector.tensor_tensor(o, c4[:, :, :, 0:HD], r4.broadcast_to([P, 4, QH, HD]),
                                                ALU.mult).then_inc(c_ac, 1)

                    def first():
                        for s in range(QH * BT):
                            tile_max(s, s % 2, 0, s)
                        peak_parts(QH * BT % 2, QH * BT)

                    def step(n, u, pair, ahead, base):
                        ch.begin(CH0 + n * CHN)
                        k = 0
                        for what, a in schedule(ahead):
                            slot = (FIRST + RING * u + k) % 2
                            used = base + k
                            if what == "tile":
                                tile_max(a, slot, (u + 1) % 2, used)
                            elif what == "peak":
                                peak_parts(slot, used)
                            elif what == "turn":
                                context(pair, u % 2, a, slot, used)
                            else:
                                continue
                            k += 1
                        assert ch.k == (CHN if ahead else 2), ch.k

                    CH0, CHN, FIRST = 2, 4, QH * BT + 1
                    first()
                    with dve.Fori(0, QUADS // 4 - 1) as it:
                        for u in range(4):
                            n = it * 4 + u
                            step(n, u, it * 2 + u // 2, True, n * RING + FIRST)
                    for u in range(4):
                        n = QUADS - 4 + u
                        step(n, u, n // 2, u < 3, n * RING + FIRST)

                @block.tensor
                def _(pe):
                    FIRST = QH * BT + 1

                    def score_tile(s, slot, u, used, wait):
                        h, i = divmod(s, BT)
                        if wait:
                            pe.wait_ge(c_ac, used - 1)
                        w = (i + 1) * P
                        for lo in range(0, w, 512):
                            hi = min(w, lo + 512)
                            last = nc.tensor.matmul(psum[:, 2 * slot + lo // 512, 0:hi - lo],
                                                    qs[0:KR, u, h, i * P:(i + 1) * P], ks[0:KR, u, h, lo:hi],
                                                    start=True, stop=True)
                        last.then_inc(c_ap, 1)

                    def peak(slot, par, used):
                        pe.wait_ge(c_ac, used)
                        nc.tensor.transpose(psum[0:QH * BT, 2 * slot, 0:P], mx[:, par, :], ident[:, :]).then_inc(c_ap, 1)

                    def turn(n, half, slot, used):
                        pe.wait_ge(c_ac, used - 1)
                        pe.wait_ge(c_oe, n * 2 + (half + 1))
                        for t in range(4):
                            at_ = (half * 4 + t) * P
                            last = nc.tensor.transpose(psum[:, 2 * slot, t * P:(t + 1) * P], ot[:, at_:at_ + P], ident[:, :])
                        last.then_inc(c_ap, 1)

                    def piece(n, p, u):
                        m, h = divmod(p, QH)
                        half, j = batches[m]
                        q0, w = span(half, j)
                        if p >= 2:
                            pe.wait_ge(c_ex, n * PIECES + (p - 1))
                        nc.tensor.matmul(psum[:, 4 + p % 2, 0:w], ks[0:KM, u, h, j * P:(j + 1) * P],
                                         qs[0:KM, u, h, q0:q0 + w], start=True, stop=True).then_inc(c_sb, 1)

                    diags = [m for m, (half, j) in enumerate(batches) if span(half, j)[0] == j * P]

                    def values(n, m, u):
                        half, j = batches[m]
                        q0, w = span(half, j)
                        pe.wait_ge(c_ex, n * PIECES + (m + 1) * QH)
                        if m in diags:
                            pe.wait_ge(c_af, n * DIAG + (diags.index(m) + 1) * QH)
                        last_j = (BT // 2 if half == 0 else BT) - 1
                        for h in range(QH):
                            last = nc.tensor.matmul(psum[h * VW:(h + 1) * VW, 6 + half, q0 - half * 512:q0 - half * 512 + w],
                                                    vs[:, u, j, h * VW:(h + 1) * VW], pt[:, (m * QH + h) % (2 * QH), 0:w],
                                                    start=(j == 0), stop=(j == last_j), skip_group_check=True)
                        if j == last_j:
                            last.then_inc(c_o, 1)

                    def step(n, u, ahead, base, turns):
                        pe.wait_ge(c_mrow, n * 48 + 48)
                        if ahead:
                            pe.wait_ge(c_ld[(u + 1) % 4], turns)
                        k = 0
                        for what, a in schedule(ahead):
                            slot = (FIRST + RING * u + k) % 2
                            used = base + k
                            if what == "piece":
                                piece(n, a, u)
                            elif what == "pv":
                                values(n, a, u)
                            else:
                                if what == "tile":
                                    score_tile(a, slot, (u + 1) % 4, used, True)
                                elif what == "peak":
                                    peak(slot, (u + 1) % 2, used)
                                else:
                                    turn(n, a, slot, used)
                                k += 1

                    pe.wait_ge(c_ld[0], LOADS * 16)
                    for s in range(QH * BT):
                        score_tile(s, s % 2, 0, s, s >= 2)
                    peak(QH * BT % 2, 0, QH * BT)
                    pe.wait_ge(c_one, 1)
                    with pe.Fori(0, QUADS // 4 - 1) as it:
                        for u in range(4):
                            n = it * 4 + u
                            step(n, u, True, n * RING + FIRST, (it + (1 if u < 3 else 2)) * (LOADS * 16))
                    for u in range(4):
                        n = QUADS - 4 + u
                        step(n, u, u < 3, n * RING + FIRST, QUADS // 4 * LOADS * 16)

        with ExitStack() as sd:
            ctxs = sb("d_ctxs", [P, BQ // 2, BT, P], stack=sd)
            ct = sb("d_ct", [P, 2, KC, P], stack=sd)
            rows = sb("d_rows", [P, BT, E], stack=sd)
            xt = sb("d_xt", [P, KC, S], stack=sd)
            st = sb("d_st", [P, BT, 6], stack=sd)
            tmp = sb("d_tmp", [P, 6, BT], stack=sd)
            mt = sb("d_mt", [P, KC, P], stack=sd)
            lg = sb("d_lg", [P, NEX], stack=sd)
            le = sb("d_le", [P, NEX], stack=sd)
            one = sb("d_one", [P, 8], stack=sd)
            bs = sb("d_bs", [P, E], stack=sd)
            weff = sb("d_weff", [P, KC, E], stack=sd)

            d_cx = sem("d_cx")
            d_tp = sem("d_tp")
            d_xt = sem("d_xt")
            d_ou = sem("d_ou")
            d_used = sem("d_used")
            d_y = sem("d_y")
            d_var = sem("d_var")
            d_sd = sem("d_sd")
            d_xn = sem("d_xn")
            d_mn = sem("d_mn")
            d_mt = sem("d_mt")
            d_lg = sem("d_lg")
            d_le = sem("d_le")
            d_ex = sem("d_ex")
            d_bs = sem("d_bs")
            d_we = sem("d_we")
            d_wf = sem("d_wf")
            d_f = sem("d_f")
            d_fy = sem("d_fy")
            d_o = sem("d_o")
            d_out = sem("d_out")
            d_v = sem("d_v")
            MEAN_ROWS = S - 1 - 107
            CHD = 22

            with nc.Block() as block:
                @block.sync
                def _(sp):
                    sp.sem_inc(d_used, 1)
                    with sp.Fori(0, NB) as b:
                        sp.wait_ge(d_used, b + 1)
                        sp.dma_start(ctxs[:, :, :, :], ctx[:, bass.ds(b * KC, KC), :, :]).then_inc(d_cx, 16)
                        for t in range(BT):
                            sp.wait_ge(d_o, b * BT + (t + 1))
                            sp.dma_start(out[bass.ds(b * S + t * P, P), :], rows[:, t, :]).then_inc(d_out, 16)
                    sp.wait_ge(d_out, TILES * 16 + 16)

                @block.vector
                def _(dve):
                    ch = Chain(dve, d_v)
                    dve.sem_inc(d_out, 16)
                    dve.wait_ge(w_d, W_D)

                    def tile_of(a, n):
                        return a[:, bass.ds(n, 1), :].rearrange("p o e -> p (o e)")

                    with dve.Fori(0, NB) as b:
                        ch.begin(b * CHD)

                        def scaled(dst, src, t):
                            return nc.vector.tensor_scalar(dst, src, tmp[:, 0, t:t + 1], tmp[:, 5, t:t + 1],
                                                           ALU.subtract, ALU.mult)

                        dve.wait_ge(d_out, b * (BT * 16) + 16)
                        for t in range(BT):
                            dve.wait_ge(d_ou, b * BT + (t + 1))
                            nc.vector.tensor_tensor(rows[:, t, :], psum[:, 2 + t % 2, :], bo[:, :],
                                                    ALU.add).then_inc(d_y, 1)
                            dve.wait_ge(d_y, b * BT + (t + 1))
                            last = nc.vector.bn_stats(st[:, t, :], rows[:, t, :])
                        ch.link(last)
                        finish_stats(dve, d_var, d_sd, ch, st, tmp, BT, E, None, b * 3 + 1)
                        for t in range(BT):
                            last = scaled(rows[:, t, :], rows[:, t, :], t)
                        ch.link(last)
                        for t in range(BT):
                            last = nc.vector.tensor_tensor(tile_of(xs, b * BT + t), tile_of(xs, b * BT + t),
                                                           rows[:, t, :], ALU.add)
                        ch.mark(last)
                        ch.need_apart(passed_v)
                        for t in range(BT):
                            last = nc.vector.bn_stats(st[:, t, :], tile_of(xs, b * BT + t))
                        ch.link(last)
                        finish_stats(dve, d_var, d_sd, ch, st, tmp, BT, E, None, b * 3 + 2)
                        for t in range(BT):
                            scaled(rows[:, t, :], tile_of(xs, b * BT + t), t).then_inc(d_xn, 1)
                        dve.wait_ge(d_lg, b + 1)
                        ch.link(nc.vector.tensor_tensor(lg[:, :], psum[:, 2, 0:NEX], route_b[:, :], ALU.add))
                        ch.link(nc.vector.tensor_reduce(one[:, 0:1], lg[:, :], X_AXIS, ALU.max))
                        nc.vector.tensor_scalar(lg[:, :], lg[:, :], one[:, 0:1], None, ALU.subtract).then_inc(d_le, 1)
                        dve.wait_ge(d_ex, b + 1)
                        ch.link(nc.vector.tensor_reduce(one[:, 1:2], le[:, :], X_AXIS, ALU.add))
                        ch.link(nc.vector.reciprocal(one[:, 2:3], one[:, 1:2]))
                        ch.link(nc.vector.tensor_scalar(le[:, :], le[:, :], one[:, 2:3], None, ALU.mult))
                        ch.link(nc.vector.tensor_tensor(lg[:, :], le[:, :], own[:, :], ALU.mult))
                        ch.link(nc.vector.tensor_reduce(one[:, 3:4], lg[:, :], X_AXIS, ALU.add))
                        nc.vector.tensor_scalar(bs[:, :], lora_b[:, :], one[:, 3:4], None, ALU.mult).then_inc(d_bs, 1)
                        dve.wait_ge(d_we, b + 1)
                        for c in range(KC):
                            last = nc.vector.tensor_tensor(weff[:, c, :], psum[:, 4 + c, :], w4[:, c, :], ALU.add)
                        last.then_inc(d_wf, 1)
                        for t in range(BT):
                            dve.wait_ge(d_f, b * BT + (t + 1))
                            nc.vector.tensor_tensor(rows[:, t, :], psum[:, 2 + t % 2, :], b4[:, :],
                                                    ALU.add).then_inc(d_fy, 1)
                            dve.wait_ge(d_fy, b * BT + (t + 1))
                            last = nc.vector.bn_stats(st[:, t, :], rows[:, t, :])
                        ch.link(last)
                        finish_stats(dve, d_var, d_sd, ch, st, tmp, BT, E, None, b * 3 + 3)
                        for t in range(BT):
                            last = scaled(rows[:, t, :], rows[:, t, :], t)
                        ch.link(last)
                        for t in range(BT):
                            nc.vector.tensor_tensor(rows[:, t, :], tile_of(xs, b * BT + t), rows[:, t, :],
                                                    ALU.add).then_inc(d_o, 1)
                        assert ch.k == CHD, ch.k

                @block.scalar
                def _(act):
                    with act.Fori(0, NB) as b:
                        for t in range(BT):
                            act.wait_ge(d_tp, b * 2 * BT + (t + 1))
                            nc.scalar.activation(ct[:, t % 2, :, :].rearrange("p c n -> p (c n)"), psum[:, t % 2, :],
                                                 ACT.Copy).then_inc(d_xt, 1)
                        root(act, d_var, d_sd, tmp, BT, b * 3 + 1)
                        root(act, d_var, d_sd, tmp, BT, b * 3 + 2)
                        for t in range(BT):
                            act.wait_ge(d_tp, b * 2 * BT + (BT + t + 1))
                            nc.scalar.activation(xt[:, :, t * P:(t + 1) * P],
                                                 psum[:, t % 2, :].rearrange("p (c n) -> p c n", n=P),
                                                 ACT.Copy).then_inc(d_xt, 1)
                        act.wait_ge(d_mn, b + 1)
                        for c in range(KC):
                            last = nc.scalar.activation(mt[:, c, :], psum[:, 4 + c, 0:P], ACT.Copy,
                                                        scale=1.0 / MEAN_ROWS)
                        last.then_inc(d_mt, 1)
                        act.wait_ge(d_le, b + 1)
                        nc.scalar.activation(le[:, :], lg[:, :], ACT.Exp).then_inc(d_ex, 1)
                        root(act, d_var, d_sd, tmp, BT, b * 3 + 3)

                @block.tensor
                def _(pe):
                    pe.wait_ge(w_d, W_D)
                    with pe.Fori(0, NB) as b:
                        pe.wait_ge(d_cx, b * 16 + 16)

                        def turn_ctx(t):
                            if t >= 2:
                                pe.wait_ge(d_xt, b * 2 * BT + (t - 1))
                            for c in range(KC):
                                last = nc.tensor.transpose(psum[:, t % 2, c * P:(c + 1) * P],
                                                           ctxs[:, c, t, :], ident[:, :])
                            last.then_inc(d_tp, 1)

                        turn_ctx(0)
                        for t in range(BT):
                            if t + 1 < BT:
                                turn_ctx(t + 1)
                            pe.wait_ge(d_xt, b * 2 * BT + (t + 1))
                            if t >= 2:
                                pe.wait_ge(d_y, b * BT + (t - 1))
                            for c in range(KC):
                                last = nc.tensor.matmul(psum[:, 2 + t % 2, :], ct[:, t % 2, c, :], wo[:, c, :],
                                                        start=(c == 0), stop=(c == KC - 1))
                            last.then_inc(d_ou, 1)
                        for t in range(BT):
                            pe.wait_ge(d_xn, b * BT + (t + 1))
                            if t >= 2:
                                pe.wait_ge(d_xt, b * 2 * BT + (BT + t - 1))
                            for c in range(KC):
                                last = nc.tensor.transpose(psum[:, t % 2, c * P:(c + 1) * P],
                                                           rows[:, t, c * P:(c + 1) * P], ident[:, :])
                                if t == c == 0:
                                    last.then_inc(d_used, 1)
                            last.then_inc(d_tp, 1)
                            which = 0 if t == 0 else 2 if t == BT - 1 else 1
                            for c in range(KC):
                                last = nc.tensor.matmul(psum[:, 4 + c, 0:P], rows[:, t, c * P:(c + 1) * P],
                                                        counted[:, which, :], start=(t == 0), stop=(t == BT - 1))
                        last.then_inc(d_mn, 1)
                        pe.wait_ge(d_mt, b + 1)
                        for c in range(KC):
                            last = nc.tensor.matmul(psum[:, 2, 0:NEX], mt[:, c, :], route_w[:, c, :],
                                                    start=(c == 0), stop=(c == KC - 1))
                        last.then_inc(d_lg, 1)
                        pe.wait_ge(d_bs, b + 1)
                        for c in range(KC):
                            last = nc.tensor.matmul(psum[:, 4 + c, :], lora_a[:, c * P:(c + 1) * P], bs[:, :],
                                                    start=True, stop=True)
                        last.then_inc(d_we, 1)
                        pe.wait_ge(d_wf, b + 1)
                        pe.wait_ge(d_xt, b * 2 * BT + 2 * BT)
                        for t in range(BT):
                            if t >= 2:
                                pe.wait_ge(d_fy, b * BT + (t - 1))
                            for c in range(KC):
                                last = nc.tensor.matmul(psum[:, 2 + t % 2, :], xt[:, c, t * P:(t + 1) * P],
                                                        weff[:, c, :], start=(c == 0), stop=(c == KC - 1))
                            last.then_inc(d_f, 1)


def constants():
    half = HALF
    inv_freq = (np.float32(1.0) / np.float32(10000.0) ** (np.arange(half, dtype=np.float32) / np.float32(half)))
    ang = np.arange(S, dtype=np.float32)[:, None] * inv_freq.astype(np.float32)[None, :]
    cos, sin = np.cos(ang).astype(np.float32), np.sin(ang).astype(np.float32)
    causal = np.zeros((P, S), np.float32)
    causal[:, S - P:] = np.triu(np.full((P, P), MASK / SCALE3, np.float32), 1)
    own = np.zeros((P, NEX), np.float32)
    own[np.arange(P), np.arange(P) // RANK] = 2.0
    counted = np.ones((P, 3, P), np.float32)
    counted[:107, 0, :] = 0.0
    counted[P - 1:, 2, :] = 0.0
    return {"ident": np.eye(P, dtype=np.float32), "rope_c": np.concatenate([cos, cos], 1),
            "rope_s": np.concatenate([-sin, sin], 1), "causal": causal, "own": own,
            "counted": counted.reshape(P, 3 * P)}


def kernel(L0_attn_x, L0_attn_Wq, L0_attn_bq, L0_attn_Wk, L0_attn_bk, L0_attn_Wv, L0_attn_bv, L0_ffn_gate_w,
           L0_ffn_up_w, L0_ffn_down_w, L0_ffn_fc1_w, L0_ffn_fc2_w, L0_ffn_expert_w, L0_ffn_ln_gamma, L0_ffn_ln_beta,
           L1_attn_qkv_w, L1_attn_qkv_b, L1_attn_out_w, L1_attn_out_b, L1_ffn_W, L1_ffn_b, L1_ffn_A, L1_ffn_B,
           L1_ffn_router_W, L1_ffn_router_b):
    import concourse.bacc as bacc
    from concourse.bass_utils import run_bass_kernel_spmd

    arrays = {
        "x": np.reshape(L0_attn_x, (NB * S, E)),
        "wq0": np.reshape(L0_attn_Wq, (E, I0 * R0)), "bq0": np.reshape(L0_attn_bq, (I0 * R0,)),
        "wk0": np.reshape(L0_attn_Wk, (E, I0)), "bk0": np.reshape(L0_attn_bk, (I0,)),
        "wv0": np.reshape(L0_attn_Wv, (E, I0)), "bv0": np.reshape(L0_attn_bv, (I0,)),
        "gate": L0_ffn_gate_w, "up": L0_ffn_up_w, "down": L0_ffn_down_w, "fc1": L0_ffn_fc1_w, "fc2": L0_ffn_fc2_w,
        "expert_t": np.transpose(L0_ffn_expert_w), "gamma": L0_ffn_ln_gamma, "beta": L0_ffn_ln_beta,
        "w3": L1_attn_qkv_w, "b3": L1_attn_qkv_b, "wo": L1_attn_out_w, "bo": L1_attn_out_b,
        "w4": np.transpose(L1_ffn_W), "b4": L1_ffn_b,
        "lora_a": np.reshape(L1_ffn_A, (NEX * RANK, E)),
        "lora_b": np.reshape(np.transpose(L1_ffn_B, (0, 2, 1)), (NEX * RANK, E)),
        "route_w": np.transpose(L1_ffn_router_W), "route_b": L1_ffn_router_b,
    }
    arrays.update(constants())
    nc = bacc.Bacc("TRN2", target_bir_lowering=False, num_devices=1)
    fed, ins = {}, {}
    for name, a in arrays.items():
        a = np.ascontiguousarray(a)
        fed[f"in_{name}"] = a
        ins[name] = nc.dram_tensor(f"in_{name}", a.shape, mybir.dt.from_np(a.dtype), kind="ExternalInput").ap()
    out = nc.dram_tensor("out", (NB * S, E), F32, kind="ExternalOutput").ap()
    layers(nc, ins, out)
    got = run_bass_kernel_spmd(nc, [fed], core_ids=[0])
    return got.results[0]["out"].reshape(NB, S, E)
```

```python
from contextlib import ExitStack

import concourse.bass as bass
import numpy as np
from concourse import mybir

F32 = mybir.dt.float32
BF16 = mybir.dt.bfloat16
ALU = mybir.AluOpType
ACT = mybir.ActivationFunctionType
X_AXIS = mybir.AxisListType.X

P = 128
NB, S, E = 2, 1024, 512
TILES = NB * S // P
BT = S // P
KC = E // P
D0, G0, R0 = 16, 8, 4
I0 = D0 * G0
INT, LAT, NE = 1024, 256, 8
H, HD = 32, 16
HALF = HD // 2
VW = 32
QH = 4
QUADS = NB * H // QH
BQ = H // QH
NEX, RANK = 8, 16
EPS = 1e-5
MASK = -66504.0
SCALE3 = HD ** -0.5
GT = 4
GR = GT * P
CHAIN_B = 22
COPIES = 6
Q_PARTS = (0, 0, 0, 1, 1, 2)
K_PARTS = (0, 1, 2, 0, 1, 0)
KR = COPIES * HD
KM = KR + 3


class Chain:

    def __init__(self, eng, sem):
        self.eng, self.sem, self.base, self.k = eng, sem, 0, 0

    def begin(self, base):
        self.base, self.k = base, 0

    def mark(self, ins):
        ins.then_inc(self.sem, 1)
        self.k += 1
        return self.k

    def need(self, k=None):
        self.eng.wait_ge(self.sem, self.base + (self.k if k is None else k))

    def link(self, ins):
        self.mark(ins)
        self.need()

    def need_apart(self, passed):
        wait_apart(self.eng, self.sem, self.base + self.k, passed)


def wait_apart(eng, sem, count, passed):
    eng.wait_ge(sem, count)
    eng.sem_inc(passed, 1)


def layers(nc, ins, out):
    with ExitStack() as whole:
        def at(stack, make, name, shape, dt=F32):
            return stack.enter_context(make(name, shape, dt))

        def sem(name):
            return whole.enter_context(nc.semaphore(name))

        def sb(name, shape, dt=F32, stack=whole):
            return at(stack, nc.sbuf_tensor, name, shape, dt)

        xs = sb("xs", [P, TILES, E])
        ident = sb("ident", [P, P])
        psum = whole.enter_context(nc.psum_tensor("psum", [P, 8, 512], F32))

        q_scr = nc.dram_tensor("q_scr", [3, NB * E, S], BF16).ap()
        k_scr = nc.dram_tensor("k_scr", [3, NB * E, S], BF16).ap()
        v_scr = nc.dram_tensor("v_scr", [TILES, P, H * VW], F32).ap()

        x_in = [sem(f"x_in{c}") for c in range(4)]
        const_in = sem("const_in")
        passed_v = sem("passed_v")
        passed_p = sem("passed_p")

        def finish_stats(dve, act_var, act_sd, chain, st, tmp, n, count, var_at, sd_at):
            nc.vector.tensor_tensor(tmp[:, 0, 0:n], st[:, 0:n, 1], st[:, 0:n, 4], ALU.add)
            nc.vector.tensor_tensor(tmp[:, 1, 0:n], st[:, 0:n, 1], st[:, 0:n, 4], ALU.subtract)
            chain.link(nc.vector.tensor_tensor(tmp[:, 2, 0:n], st[:, 0:n, 2], st[:, 0:n, 5], ALU.add))
            nc.vector.tensor_scalar(tmp[:, 0, 0:n], tmp[:, 0, 0:n], 0.5, None, ALU.mult)
            chain.link(nc.vector.scalar_tensor_tensor(out=tmp[:, 3, 0:n], in0=tmp[:, 1, 0:n], scalar=0.25,
                                                      in1=tmp[:, 1, 0:n], op0=ALU.mult, op1=ALU.mult))
            nc.vector.scalar_tensor_tensor(out=tmp[:, 4, 0:n], in0=tmp[:, 2, 0:n], scalar=1.0 / count,
                                           in1=tmp[:, 3, 0:n], op0=ALU.mult, op1=ALU.add).then_inc(act_var, 1)
            dve.wait_ge(act_sd, sd_at)
            chain.link(nc.vector.reciprocal(tmp[:, 5, 0:n], tmp[:, 4, 0:n]))

        def root(act, act_var, act_sd, tmp, n, var_at):
            act.wait_ge(act_var, var_at)
            nc.scalar.activation(tmp[:, 4, 0:n], tmp[:, 4, 0:n], ACT.Sqrt,
                                 bias=eps[:, 0:1]).then_inc(act_sd, 1)

        eps = sb("eps", [P, 1])

        b_stack = whole.enter_context(ExitStack())
        mixed = sb("mixed", [P, TILES, I0], stack=b_stack)
        mixed_st = sb("mixed_st", [P, TILES, 6], stack=b_stack)
        up = sb("up", [P, KC, INT], stack=b_stack)
        down = sb("down", [P, INT // P, E], stack=b_stack)
        fc1 = sb("fc1", [P, KC, LAT], stack=b_stack)
        lat_out = sb("lat_out", [P, LAT // P, E], stack=b_stack)
        gate = sb("gate", [P, KC, NE], stack=b_stack)
        w3 = sb("w3", [P, KC, 3 * E], stack=b_stack)
        b3 = sb("b3", [P, 3 * E], stack=b_stack)
        gamma = sb("gamma", [P, E], stack=b_stack)
        beta = sb("beta", [P, E], stack=b_stack)
        rope_c = sb("rope_c", [P, BT, HD], stack=b_stack)
        rope_s = sb("rope_s", [P, BT, HD], stack=b_stack)
        w_b = sem("w_b")
        W_B = 16 * 10

        with ExitStack() as sa:
            wq0 = sb("wq0", [P, KC, I0 * R0], stack=sa)
            w0 = sb("w0", [P, KC, 3 * I0], stack=sa)
            bq0 = sb("bq0", [P, I0 * R0], stack=sa)
            b0 = sb("b0", [P, 3 * I0], stack=sa)
            expert_t = sb("expert_t", [P, LAT // P, LAT], stack=sa)
            fc2 = sb("fc2", [P, LAT // P, E], stack=sa)
            st = sb("a_st", [P, TILES, 6], stack=sa)
            tmp = sb("a_tmp", [P, 6, TILES], stack=sa)
            xn = sb("a_xn", [P, 2, E], stack=sa)
            xt = sb("a_xt", [P, 2, E], stack=sa)
            qkv = sb("a_qkv", [P, 2, 3 * I0], stack=sa)
            prod = sb("a_prod", [P, 2, D0 * D0 * G0], stack=sa)
            prov = sb("a_prov", [P, 2, D0 * D0 * G0], stack=sa)
            sc = sb("a_sc", [P, 2, D0 * D0], stack=sa)
            pr = sb("a_pr", [P, 2, D0 * D0], stack=sa)
            mx = sb("a_mx", [P, D0], stack=sa)
            ls = sb("a_ls", [P, 4, D0], stack=sa)
            av = sb("a_av", [P, I0], stack=sa)

            w_a = sem("w_a")
            a_w0 = sem("a_w0")
            a_var = sem("a_var")
            a_sd = sem("a_sd")
            a_xn = sem("a_xn")
            a_tp = sem("a_tp")
            a_xt = sem("a_xt")
            a_pq = sem("a_pq")
            a_qkv = sem("a_qkv")
            a_p1 = sem("a_p1")
            a_s = sem("a_s")
            a_p = sem("a_p")
            a_p2 = sem("a_p2")
            a_v = sem("a_v")
            a_ef = sem("a_ef")
            a_efc = sem("a_efc")
            DP = 4
            SPLIT = DP * D0 * G0

            with nc.Block() as block:
                @block.sync
                def _(sp):
                    for c in range(4):
                        sp.dma_start(xs[:, 4 * c:4 * c + 4, :],
                                     ins["x"][512 * c:512 * c + 512, :].rearrange("(t p) e -> p t e", p=P)
                                     ).then_inc(x_in[c], 16)
                        if c == 0:
                            sp.dma_start(ident[:, :], ins["ident"]).then_inc(const_in, 16)
                            sp.dma_start(wq0[:, :, :], ins["wq0"].rearrange("(k p) n -> p k n", p=P)).then_inc(w_a, 16)
                            sp.dma_start(w0[:, :, I0:2 * I0],
                                         ins["wk0"].rearrange("(k p) n -> p k n", p=P)).then_inc(w_a, 16)
                            sp.dma_start(w0[:, :, 2 * I0:3 * I0],
                                         ins["wv0"].rearrange("(k p) n -> p k n", p=P)).then_inc(w_a, 16)
                            sp.dma_start(bq0[:, :], ins["bq0"].partition_broadcast(P)).then_inc(w_a, 16)
                            sp.dma_start(b0[:, I0:2 * I0], ins["bk0"].partition_broadcast(P)).then_inc(w_a, 16)
                            sp.dma_start(b0[:, 2 * I0:3 * I0], ins["bv0"].partition_broadcast(P)).then_inc(w_a, 16)
                    sp.dma_start(expert_t[:, :, :],
                                 ins["expert_t"].rearrange("(k p) n -> p k n", p=P)).then_inc(w_a, 16)
                    sp.dma_start(fc2[:, :, :], ins["fc2"].rearrange("(k p) n -> p k n", p=P)).then_inc(w_a, 16)
                    for dst, name in ((up, "up"), (down, "down"), (fc1, "fc1"), (gate, "gate"), (w3, "w3"),
                                      (rope_c, "rope_c"), (rope_s, "rope_s")):
                        sp.dma_start(dst[:, :, :], ins[name].rearrange("(k p) n -> p k n", p=P)).then_inc(w_b, 16)
                    sp.dma_start(b3[:, :], ins["b3"].partition_broadcast(P)).then_inc(w_b, 16)
                    sp.dma_start(gamma[:, :], ins["gamma"].partition_broadcast(P)).then_inc(w_b, 16)
                    sp.dma_start(beta[:, :], ins["beta"].partition_broadcast(P)).then_inc(w_b, 16)

                @block.vector
                def _(dve):
                    ch = Chain(dve, a_v)
                    ch.link(nc.vector.memset(eps[:, :], EPS))
                    for c in range(4):
                        dve.wait_ge(x_in[c], 16)
                        for t in range(4 * c, 4 * c + 4):
                            i = nc.vector.bn_stats(st[:, t, :], xs[:, t, :])
                    ch.link(i)
                    dve.wait_ge(w_a, 16 * 8)
                    nc.vector.tensor_reduce(w0[:, :, 0:I0], wq0[:, :, :].rearrange("p k (i r) -> p k i r", r=R0),
                                            X_AXIS, ALU.add)
                    nc.vector.tensor_reduce(b0[:, 0:I0], bq0[:, :].rearrange("p (i r) -> p i r", r=R0),
                                            X_AXIS, ALU.add).then_inc(a_w0, 1)
                    finish_stats(dve, a_var, a_sd, ch, st, tmp, TILES, E, 1, 1)
                    head = ch.k

                    def normalise(n, u):
                        nc.vector.tensor_scalar(xn[:, u, :], tile_of(xs, n), col_of(tmp, 0, n), col_of(tmp, 5, n),
                                                ALU.subtract, ALU.mult).then_inc(a_xn, 1)

                    def tile_of(a, n):
                        return a[:, bass.ds(n, 1), :].rearrange("p o e -> p (o e)")

                    def col_of(a, row, n):
                        return a[:, row, bass.ds(n, 1)]

                    def evacuate(n, u):
                        dve.wait_ge(a_pq, n + 1)
                        nc.vector.tensor_tensor(qkv[:, u, :], psum[:, 2 + u, 0:3 * I0], b0[:, :],
                                                ALU.add).then_inc(a_qkv, 1)

                    def weigh(n, u):
                        dve.wait_ge(a_p1, n + 1)
                        s2 = sc[:, u, :].rearrange("p (d e) -> p d e", d=D0)
                        ch.link(nc.vector.tensor_reduce(sc[:, u, :], prod[:, u, :].rearrange("p (i g) -> p i g", g=G0),
                                                        X_AXIS, ALU.add))
                        ch.link(nc.vector.tensor_reduce(mx[:, :], s2, X_AXIS, ALU.max))
                        nc.vector.tensor_tensor(s2, s2, mx[:, :].rearrange("p (d o) -> p d o", o=1)
                                                .broadcast_to([P, D0, D0]), ALU.subtract).then_inc(a_s, 1)

                    def share(n, u):
                        dve.wait_ge(a_p, n + 1)
                        p2 = pr[:, u, :].rearrange("p (d e) -> p d e", d=D0)
                        ch.mark(nc.vector.tensor_reduce(ls[:, u, :], p2, X_AXIS, ALU.add))
                        v3 = qkv[:, u, 2 * I0:3 * I0].rearrange("p (e g) -> p g e", g=G0)
                        for d in range(DP):
                            last = nc.vector.tensor_tensor(
                                prov[:, u, d * D0 * G0:(d + 1) * D0 * G0].rearrange("p (g e) -> p g e", g=G0),
                                p2[:, d:d + 1, :].broadcast_to([P, G0, D0]), v3, ALU.mult)
                        ch.need()
                        ch.link(nc.vector.reciprocal(ls[:, 2 + u, :], ls[:, u, :]))

                    def collect(n, u):
                        dve.wait_ge(a_p2, n + 1)
                        ch.link(nc.vector.tensor_reduce(av[:, :], prov[:, u, :].rearrange("p (i e) -> p i e", e=D0),
                                                        X_AXIS, ALU.add))
                        o = tile_of(mixed, n)
                        ch.mark(nc.vector.tensor_tensor(
                            o.rearrange("p (d g) -> p d g", g=G0), av[:, :].rearrange("p (d g) -> p d g", g=G0),
                            ls[:, 2 + u, :].rearrange("p (d o) -> p d o", o=1).broadcast_to([P, D0, G0]), ALU.mult))
                        ch.need_apart(passed_v)
                        nc.vector.bn_stats(tile_of(mixed_st, n), o)

                    FIRST_LINKS, LINKS = 4, 6

                    def step(n, u):
                        left = TILES - n if isinstance(n, int) else TILES
                        ch.begin(head + FIRST_LINKS + n * LINKS)
                        if left > 3:
                            normalise(n + 3, 1 - u)
                        if left > 1:
                            weigh(n + 1, 1 - u)
                        collect(n, u)
                        if left > 2:
                            evacuate(n + 2, u)
                        if left > 1:
                            share(n + 1, 1 - u)
                            assert ch.k == LINKS, ch.k

                    normalise(0, 0)
                    normalise(1, 1)
                    ch.begin(head)
                    evacuate(0, 0)
                    normalise(2, 0)
                    weigh(0, 0)
                    evacuate(1, 1)
                    share(0, 0)
                    assert ch.k == FIRST_LINKS, ch.k
                    with dve.Fori(0, TILES // 2 - 2) as it:
                        for u in range(2):
                            step(it * 2 + u, u)
                    for n in range(TILES - 4, TILES):
                        step(n, n % 2)

                @block.gpsimd
                def _(pool):
                    def scores(n, u):
                        pool.wait_ge(a_qkv, n + 1)
                        q = qkv[:, u, 0:I0].rearrange("p (d o g) -> p d o g", d=D0, o=1).broadcast_to([P, D0, D0, G0])
                        k = qkv[:, u, I0:2 * I0].rearrange("p (o e g) -> p o e g", o=1, e=D0)\
                            .broadcast_to([P, D0, D0, G0])
                        nc.gpsimd.tensor_tensor(prod[:, u, :].rearrange("p (d e g) -> p d e g", d=D0, e=D0), q, k,
                                                ALU.mult).then_inc(a_p1, 1)

                    def context(n, u):
                        pool.wait_ge(a_p, n + 1)
                        n_d = D0 - DP
                        p = pr[:, u, DP * D0:].rearrange("p (d o e) -> p d o e", d=n_d, o=1)\
                            .broadcast_to([P, n_d, G0, D0])
                        v = qkv[:, u, 2 * I0:3 * I0].rearrange("p (o e g) -> p o g e", o=1, g=G0)\
                            .broadcast_to([P, n_d, G0, D0])
                        nc.gpsimd.tensor_tensor(prov[:, u, SPLIT:].rearrange("p (d g e) -> p d g e", d=n_d, g=G0), p, v,
                                                ALU.mult).then_inc(a_p2, 1)

                    scores(0, 0)
                    scores(1, 1)
                    context(0, 0)
                    with pool.Fori(0, TILES // 2 - 1) as it:
                        for u in range(2):
                            context(it * 2 + (u + 1), 1 - u)
                            scores(it * 2 + (u + 2), u)
                    context(TILES - 1, 1)

                @block.scalar
                def _(act):
                    root(act, a_var, a_sd, tmp, TILES, 1)

                    def copy_xt(n, u):
                        act.wait_ge(a_tp, n + 1)
                        nc.scalar.activation(xt[:, u, :], psum[:, u, :], ACT.Copy).then_inc(a_xt, 1)

                    def exps(n, u):
                        act.wait_ge(a_s, n + 1)
                        nc.scalar.activation(pr[:, u, :], sc[:, u, :], ACT.Exp,
                                             scale=D0 ** -0.5).then_inc(a_p, 1)

                    copy_xt(0, 0)
                    copy_xt(1, 1)
                    copy_xt(2, 0)
                    exps(0, 0)
                    with act.Fori(0, TILES // 2 - 2) as it:
                        for u in range(2):
                            copy_xt(it * 2 + (u + 3), 1 - u)
                            exps(it * 2 + (u + 1), 1 - u)
                    copy_xt(TILES - 1, 1)
                    for n in range(TILES - 3, TILES):
                        exps(n, n % 2)
                    act.wait_ge(a_ef, 1)
                    nc.scalar.activation(lat_out[:, :, :].rearrange("p k n -> p (k n)"),
                                         psum[:, 4:6, :].rearrange("p k n -> p (k n)"), ACT.Copy).then_inc(a_efc, 1)

                @block.tensor
                def _(pe):
                    pe.wait_ge(const_in, 16)
                    pe.wait_ge(a_w0, 1)

                    def project(n, u):
                        pe.wait_ge(a_xn, n + 1)
                        for c in range(KC):
                            last = nc.tensor.transpose(psum[:, u, c * P:(c + 1) * P], xn[:, u, c * P:(c + 1) * P],
                                                       ident[:, :])
                        last.then_inc(a_tp, 1)
                        pe.wait_ge(a_xt, n + 1)
                        for c in range(KC):
                            last = nc.tensor.matmul(psum[:, 2 + u, 0:3 * I0], xt[:, u, c * P:(c + 1) * P],
                                                    w0[:, c, :], start=(c == 0), stop=(c == KC - 1))
                        last.then_inc(a_pq, 1)

                    with pe.Fori(0, TILES // 2) as it:
                        for u in range(2):
                            project(it * 2 + u, u)
                    for lc in range(LAT // P):
                        for mc in range(LAT // P):
                            last = nc.tensor.matmul(psum[:, 4 + lc, :], expert_t[:, mc, lc * P:(lc + 1) * P],
                                                    fc2[:, mc, :], start=(mc == 0), stop=(mc == LAT // P - 1))
                    last.then_inc(a_ef, 1)

        with ExitStack() as sbk:
            mtmp = sb("b_mtmp", [P, 6, TILES], stack=sbk)
            x_st = sb("b_x_st", [P, TILES, 6], stack=sbk)
            x_tmp = sb("b_x_tmp", [P, 6, TILES], stack=sbk)
            st = sb("b_st", [P, GT, 6], stack=sbk)
            tmp = sb("b_tmp", [P, 6, GT], stack=sbk)
            ln = sb("b_ln", [P, 2, I0], stack=sbk)
            rows1 = sb("b_rows1", [P, GT, E], stack=sbk)
            rows2 = sb("b_rows2", [P, GT, E], stack=sbk)
            xt1 = sb("b_xt1", [P, KC, GR], stack=sbk)
            xt2 = sb("b_xt2", [P, KC, GR], stack=sbk)
            ht = sb("b_ht", [P, INT // P, GR], stack=sbk)
            lt = sb("b_lt", [P, LAT // P, GR], stack=sbk)
            sh = sb("b_sh", [P, 2, E], stack=sbk)
            top = sb("b_top", [P, GT, 8], stack=sbk)
            rw = sb("b_rw", [P, GT], stack=sbk)
            qk = sb("b_qk", [P, 2 * E], stack=sbk)
            rot = sb("b_rot", [P, 2 * E], stack=sbk)
            rest = sb("b_rest", [P, 2 * E], stack=sbk)
            parts = sb("b_parts", [P, 3, 2 * KC, 2 * P], BF16, stack=sbk)
            v32 = sb("b_v32", [P, H, VW], stack=sbk)

            b_v = sem("b_v")
            b_mv = sem("b_mv")
            b_ms = sem("b_ms")
            b_var = sem("b_var")
            b_sd = sem("b_sd")
            b_x1 = sem("b_x1")
            b_x2 = sem("b_x2")
            b_t1 = sem("b_t1")
            b_t2 = sem("b_t2")
            b_xt1 = sem("b_xt1")
            b_xt2 = sem("b_xt2")
            b_up = sem("b_up")
            b_hr = sem("b_hr")
            b_h = sem("b_h")
            b_gate = sem("b_gate")
            b_gs = sem("b_gs")
            b_dn = sem("b_dn")
            b_sh = sem("b_sh")
            b_y = sem("b_y")
            b_qkv = sem("b_qkv")
            b_ev = sem("b_ev")
            b_vs = sem("b_vs")
            b_rot = sem("b_rot")
            b_qk = sem("b_qk")
            b_tq = sem("b_tq")
            b_p1 = sem("b_p1")
            b_r = sem("b_r")
            b_p2 = sem("b_p2")
            b_p3 = sem("b_p3")
            b_vo = sem("b_vo")
            b_qo = sem("b_qo")
            b_c = sem("b_c")
            G = TILES // GT
            N_UP = INT // P
            N_U = N_UP + LAT // P
            T_BANK, U_BANK, R_BANK, G_BANK = 0, 2, 4, 6

            def this(g):
                return lambda per, k: g * per + k

            def after(g):
                return lambda per, k: g * per + (per + k)

            with nc.Block() as block:
                @block.sync
                def _(sp):
                    with sp.Fori(0, G) as g:
                        for t in range(GT):
                            sp.wait_ge(b_vs, g * GT + (t + 1))
                            sp.dma_start(v_scr[bass.ds(g * GT + t, 1), :, :].rearrange("o p n -> p (o n)"),
                                         v32[:, :, :].rearrange("p h w -> p (h w)")).then_inc(b_vo, 16)
                            if t % 2 == 1:
                                sp.wait_ge(b_p2, g * GT + (t + 1))
                                sp.wait_ge(b_p3, g * GT + (t + 1))
                                row = (g // 2) * E
                                col = (g % 2) * GR + (t // 2) * 2 * P
                                for j, scr in enumerate((q_scr, k_scr)):
                                    for part in range(3):
                                        sp.dma_start(
                                            scr[part, bass.ds(row, E), bass.ds(col, 2 * P)]
                                            .rearrange("(c p) n -> p c n", p=P),
                                            parts[:, part, j * KC:(j + 1) * KC, :]).then_inc(b_qo, 16)
                    sp.wait_ge(b_qo, TILES // 2 * 6 * 16 + 16)
                    sp.wait_ge(b_vo, (TILES + 1) * 16)

                @block.vector
                def _(dve):
                    ch = Chain(dve, b_v)

                    def tile_of(a, n):
                        return a[:, bass.ds(n, 1), :].rearrange("p o e -> p (o e)")

                    def after_block1(n, t):
                        ch.link(nc.vector.tensor_scalar(ln[:, t % 2, :], tile_of(mixed, n),
                                                        mtmp[:, 0, bass.ds(n, 1)], mtmp[:, 5, bass.ds(n, 1)],
                                                        ALU.subtract, ALU.mult))
                        x3 = tile_of(xs, n).rearrange("p (i r) -> p i r", r=R0)
                        ch.mark(nc.vector.tensor_tensor(
                            x3, x3, ln[:, t % 2, :].rearrange("p (i o) -> p i o", o=1).broadcast_to([P, I0, R0]),
                            ALU.add))
                        ch.need_apart(passed_v)
                        return nc.vector.bn_stats(tile_of(x_st, n), tile_of(xs, n))

                    def input2(c):
                        for t in range(GT):
                            n = c(GT, t)
                            nc.vector.tensor_scalar(rows1[:, t, :], tile_of(xs, n), x_tmp[:, 0, bass.ds(n, 1)],
                                                    x_tmp[:, 5, bass.ds(n, 1)], ALU.subtract,
                                                    ALU.mult).then_inc(b_x1, 1)

                    def gate_sums(c):
                        wait_apart(dve, b_gate, c(1, 1), passed_v)
                        for t in range(GT):
                            last = nc.vector.max(top[:, t, :], psum[:, G_BANK, t * NE:(t + 1) * NE])
                        last.then_inc(b_gs, 1)
                        dve.wait_ge(b_gs, c(1, 1))
                        ch.link(nc.vector.tensor_tensor(rw[:, :], top[:, :, 0], top[:, :, 1], ALU.add))

                    def output2(c, t):
                        dve.wait_ge(b_sh, c(GT, t + 1))
                        nc.vector.scalar_tensor_tensor(
                            out=rows2[:, t, :], in0=psum[:, R_BANK + t % 2, :], scalar=rw[:, t:t + 1],
                            in1=sh[:, t % 2, :], op0=ALU.mult, op1=ALU.add).then_inc(b_y, 1)
                        dve.wait_ge(b_y, c(GT, t + 1))
                        return nc.vector.bn_stats(st[:, t, :], rows2[:, t, :])

                    def scaled(dst, src, t):
                        return nc.vector.tensor_scalar(dst, src, tmp[:, 0, t:t + 1], tmp[:, 5, t:t + 1],
                                                       ALU.subtract, ALU.mult)

                    def norms(c):
                        def finish(k):
                            finish_stats(dve, b_var, b_sd, ch, st, tmp, GT, E, None, c(3, k + 3))

                        finish(0)
                        for t in range(GT):
                            last = scaled(rows2[:, t, :], rows2[:, t, :], t)
                        ch.link(last)
                        for t in range(GT):
                            last = nc.vector.tensor_tensor(rows2[:, t, :], rows2[:, t, :], gamma[:, :], ALU.mult)
                        ch.link(last)
                        for t in range(GT):
                            last = nc.vector.tensor_tensor(rows2[:, t, :], rows2[:, t, :], beta[:, :], ALU.add)
                        ch.link(last)
                        for t in range(GT):
                            last = nc.vector.bn_stats(st[:, t, :], rows2[:, t, :])
                        ch.link(last)
                        finish(1)
                        for t in range(GT):
                            last = scaled(rows2[:, t, :], rows2[:, t, :], t)
                        ch.link(last)
                        for t in range(GT):
                            x = tile_of(xs, c(GT, t))
                            last = nc.vector.tensor_tensor(x, x, rows2[:, t, :], ALU.add)
                        ch.mark(last)
                        ch.need_apart(passed_v)
                        for t in range(GT):
                            last = nc.vector.bn_stats(st[:, t, :], tile_of(xs, c(GT, t)))
                        ch.link(last)
                        finish(2)
                        for t in range(GT):
                            scaled(rows2[:, t, :], tile_of(xs, c(GT, t)), t).then_inc(b_x2, 1)

                    def evacuate(c, t):
                        qk_bank = (U_BANK, R_BANK)[t % 2]
                        dve.wait_ge(b_qkv, c(GT, t + 1))
                        dve.wait_ge(b_tq, c(GT, t + 1))
                        nc.vector.tensor_tensor(qk[:, :].rearrange("p (j n) -> p j n", j=2),
                                                psum[:, qk_bank:qk_bank + 2, :],
                                                b3[:, 0:2 * E].rearrange("p (j n) -> p j n", j=2),
                                                ALU.add).then_inc(b_ev, 1)
                        dve.wait_ge(b_vo, c(GT * 16, (t + 1) * 16))
                        if t == 0:
                            dve.wait_ge(b_c, 2)
                        nc.vector.tensor_tensor(v32[:, :, 0:HD],
                                                psum[:, G_BANK + t % 2, :].rearrange("p (h w) -> p h w", w=HD),
                                                b3[:, 2 * E:3 * E].rearrange("p (h w) -> p h w", w=HD),
                                                ALU.add).then_inc(b_vs, 1)

                    def rotate(g, c, t):
                        dve.wait_ge(b_rot, c(GT, t + 1))
                        q3 = qk[:, :].rearrange("p (h w) -> p h w", w=HD)
                        cos = rope_c[:, bass.ds((g % 2) * GT + t, 1), :].broadcast_to([P, 2 * H, HD])
                        ch.link(nc.vector.tensor_tensor(q3, q3, cos, ALU.mult))
                        nc.vector.tensor_tensor(qk[:, :], qk[:, :], rot[:, :], ALU.add).then_inc(b_qk, 1)

                    def split(c, t):
                        dve.wait_ge(b_p1, c(GT, t + 1))
                        half = slice((t % 2) * P, (t % 2 + 1) * P)
                        pt = psum[:, T_BANK:T_BANK + 2, :].rearrange("p b (c n) -> p (b c) n", n=P)
                        r3 = rest[:, :].rearrange("p (c n) -> p c n", n=P)
                        nc.vector.tensor_tensor(r3, pt, parts[:, 0, :, half], ALU.subtract).then_inc(b_r, 1)
                        dve.wait_ge(b_p2, c(GT, t + 1))
                        nc.vector.tensor_tensor(parts[:, 2, :, half], r3, parts[:, 1, :, half],
                                                ALU.subtract).then_inc(b_p3, 1)

                    dve.sem_inc(b_vo, 16)
                    dve.sem_inc(b_tq, 1)
                    dve.wait_ge(w_b, W_B)
                    finish_stats(dve, b_mv, b_ms, ch, mixed_st, mtmp, TILES, I0, 1, 1)
                    for t in range(GT):
                        last = after_block1(t, t)
                    ch.link(last)
                    finish_stats(dve, b_var, b_sd, ch, x_st, x_tmp, GT, E, None, 1)
                    input2(this(0))
                    head = ch.k
                    with dve.Fori(0, G - 1) as g:
                        ch.begin(g * (2 * GT + 1) + head)
                        for t in range(GT):
                            last = after_block1(g * GT + (GT + t), t)
                        ch.link(last)
                    ch.begin((G - 1) * (2 * GT + 1) + head)
                    finish_stats(dve, b_var, b_sd, ch, x_st[:, GT:TILES, :], x_tmp[:, :, GT:TILES], TILES - GT, E,
                                 None, 2)
                    gate_sums(this(0))
                    for t in range(GT - 1):
                        output2(this(0), t)
                    head = ch.base + ch.k

                    with dve.Fori(0, G - 1) as g:
                        mine, nxt = this(g), after(g)
                        ch.begin(g * CHAIN_B + head)
                        input2(nxt)
                        ch.link(output2(mine, GT - 1))
                        norms(mine)
                        gate_sums(nxt)
                        for t in range(GT):
                            evacuate(mine, t)
                            if t:
                                split(mine, t - 1)
                            rotate(g, mine, t)
                        output2(nxt, 0)
                        split(mine, GT - 1)
                        for t in range(1, GT - 1):
                            output2(nxt, t)
                        assert ch.k == CHAIN_B, ch.k
                    ch.begin((G - 1) * CHAIN_B + head)
                    mine = this(G - 1)
                    ch.link(output2(mine, GT - 1))
                    norms(mine)
                    for t in range(GT):
                        evacuate(mine, t)
                        if t:
                            split(mine, t - 1)
                        rotate(G - 1, mine, t)
                    split(mine, GT - 1)

                @block.gpsimd
                def _(pool):
                    def square(c):
                        for j in range(N_UP):
                            pool.wait_ge(b_hr, c(N_U, j + 1))
                            nc.gpsimd.tensor_tensor(ht[:, j, :], ht[:, j, :], ht[:, j, :],
                                                    ALU.mult).then_inc(b_h, 1)

                    def swapped(g, c):
                        for t in range(GT):
                            pool.wait_ge(b_ev, c(GT, t + 1))
                            q4 = qk[:, :].rearrange("p (h j w) -> p h j w", j=2, w=HALF)
                            r4 = rot[:, :].rearrange("p (h j w) -> p h j w", j=2, w=HALF)
                            s = rope_s[:, bass.ds((g % 2) * GT + t, 1), :]
                            nc.gpsimd.tensor_tensor(r4[:, :, 0, :], q4[:, :, 1, :],
                                                    s[:, :, 0:HALF].broadcast_to([P, 2 * H, HALF]), ALU.mult)
                            nc.gpsimd.tensor_tensor(r4[:, :, 1, :], q4[:, :, 0, :],
                                                    s[:, :, HALF:HD].broadcast_to([P, 2 * H, HALF]),
                                                    ALU.mult).then_inc(b_rot, 1)

                    nc.gpsimd.memset(v32[:, :, HD:VW], 0.0).then_inc(b_c, 1)
                    pool.wait_ge(b_c, 1)
                    nc.gpsimd.memset(v32[:, :, HD:HD + 1], 1.0).then_inc(b_c, 1)
                    square(this(0))
                    with pool.Fori(0, G - 1) as g:
                        square(after(g))
                        swapped(g, this(g))
                    swapped(G - 1, this(G - 1))

                @block.scalar
                def _(act):
                    def copy_input2(c):
                        for t in range(GT):
                            act.wait_ge(b_t1, c(GT, t + 1))
                            nc.scalar.activation(xt1[:, :, t * P:(t + 1) * P],
                                                 psum[:, T_BANK + t % 2, :].rearrange("p (c n) -> p c n", n=P),
                                                 ACT.Copy).then_inc(b_xt1, 1)

                    def copy_input3(c, tiles):
                        for t in tiles:
                            act.wait_ge(b_t2, c(GT, t + 1))
                            nc.scalar.activation(xt2[:, :, t * P:(t + 1) * P],
                                                 psum[:, T_BANK + t % 2, :].rearrange("p (c n) -> p c n", n=P),
                                                 ACT.Copy).then_inc(b_xt2, 1)

                    def read_up(c, js):
                        for j in js:
                            act.wait_ge(b_up, c(N_U, j + 1))
                            if j < N_UP:
                                nc.scalar.activation(ht[:, j, :], psum[:, U_BANK + j % 2, :],
                                                     ACT.Relu).then_inc(b_hr, 1)
                            else:
                                nc.scalar.activation(lt[:, j - N_UP, :], psum[:, U_BANK + j % 2, :],
                                                     ACT.Copy).then_inc(b_hr, 1)

                    def read_shared(c, t, again=True):
                        act.wait_ge(b_dn, c(GT, t + 1))
                        if again or t >= 2:
                            act.wait_ge(b_y, c(GT, t - 1))
                        nc.scalar.activation(sh[:, t % 2, :], psum[:, U_BANK + t % 2, :], ACT.Copy).then_inc(b_sh, 1)

                    def two_parts(c, t):
                        half = slice((t % 2) * P, (t % 2 + 1) * P)
                        act.wait_ge(b_tq, c(GT, t + 2))
                        if t % 2 == 0:
                            act.wait_ge(b_qo, c(GT * 3 * 16, t * 3 * 16 + 16))
                        nc.scalar.activation(parts[:, 0, :, half],
                                             psum[:, T_BANK:T_BANK + 2, :].rearrange("p b (c n) -> p (b c) n", n=P),
                                             ACT.Copy).then_inc(b_p1, 1)
                        act.wait_ge(b_r, c(GT, t + 1))
                        nc.scalar.activation(parts[:, 1, :, half], rest[:, :].rearrange("p (c n) -> p c n", n=P),
                                             ACT.Copy).then_inc(b_p2, 1)

                    act.sem_inc(b_qo, 16)
                    root(act, b_mv, b_ms, mtmp, TILES, 1)
                    root(act, b_var, b_sd, x_tmp, GT, 1)
                    copy_input2(this(0))
                    read_up(this(0), range(0, 7))
                    root(act, b_var, b_sd, x_tmp[:, :, GT:TILES], TILES - GT, 2)
                    read_up(this(0), range(7, N_U))
                    for t in range(GT):
                        read_shared(this(0), t, again=False)
                    with act.Fori(0, G - 1) as g:
                        mine, nxt = this(g), after(g)
                        copy_input2(nxt)
                        root(act, b_var, b_sd, tmp, GT, mine(3, 3))
                        read_up(nxt, range(0, 3))
                        root(act, b_var, b_sd, tmp, GT, mine(3, 4))
                        read_up(nxt, range(3, 5))
                        root(act, b_var, b_sd, tmp, GT, mine(3, 5))
                        read_up(nxt, range(5, 7))
                        copy_input3(mine, range(0, 2))
                        read_up(nxt, range(7, 8))
                        copy_input3(mine, range(2, GT))
                        read_up(nxt, range(8, N_U))
                        for t in range(GT - 1):
                            two_parts(mine, t)
                        read_shared(nxt, 0)
                        two_parts(mine, GT - 1)
                        for t in range(1, GT):
                            read_shared(nxt, t)
                    mine = this(G - 1)
                    for k in range(3):
                        root(act, b_var, b_sd, tmp, GT, mine(3, 3 + k))
                    copy_input3(mine, range(GT))
                    for t in range(GT):
                        two_parts(mine, t)

                @block.tensor
                def _(pe):
                    def turn(src, t, done):
                        for c in range(KC):
                            last = nc.tensor.transpose(psum[:, T_BANK + t % 2, c * P:(c + 1) * P],
                                                       src[:, t, c * P:(c + 1) * P], ident[:, :])
                        last.then_inc(done, 1)

                    def turn_input2(c):
                        for t in range(GT):
                            pe.wait_ge(b_x1, c(GT, t + 1))
                            if t >= 2:
                                pe.wait_ge(b_xt1, c(GT, t - 1))
                            turn(rows1, t, b_t1)

                    def turn_input3(c, tiles):
                        for t in tiles:
                            pe.wait_ge(b_x2, c(GT, t + 1))
                            if t >= 2:
                                pe.wait_ge(b_xt2, c(GT, t - 1))
                            turn(rows2, t, b_t2)

                    def up_and_fc1(c, js, before=None):
                        for j in js:
                            if j >= 2:
                                pe.wait_ge(b_hr, c(N_U, j - 1))
                            elif before is not None:
                                pe.wait_ge(b_sh, before(GT, j + 3))
                            w = up[:, :, j * P:(j + 1) * P] if j < N_UP else fc1[:, :, (j - N_UP) * P:(j - N_UP + 1) * P]
                            for k in range(KC):
                                last = nc.tensor.matmul(psum[:, U_BANK + j % 2, :], w[:, k, :], xt1[:, k, :],
                                                        start=(k == 0), stop=(k == KC - 1))
                            last.then_inc(b_up, 1)

                    def gate_logits():
                        for t in range(GT):
                            for k in range(KC):
                                last = nc.tensor.matmul(psum[:, G_BANK, t * NE:(t + 1) * NE],
                                                        xt1[:, k, t * P:(t + 1) * P], gate[:, k, :],
                                                        start=(k == 0), stop=(k == KC - 1))
                        last.then_inc(b_gate, 1)

                    def shared(t):
                        for k in range(N_UP):
                            nc.tensor.matmul(psum[:, U_BANK + t % 2, :], ht[:, k, t * P:(t + 1) * P], down[:, k, :],
                                             start=(k == 0), stop=(k == N_UP - 1))

                    def routed(t):
                        for k in range(LAT // P):
                            last = nc.tensor.matmul(psum[:, R_BANK + t % 2, :], lt[:, k, t * P:(t + 1) * P],
                                                    lat_out[:, k, :], start=(k == 0), stop=(k == LAT // P - 1))
                        last.then_inc(b_dn, 1)

                    def qkv(c, t):
                        if t >= 2:
                            pe.wait_ge(b_ev, c(GT, t - 1))
                            pe.wait_ge(b_vs, c(GT, t - 1))
                        elif t == 1:
                            pe.wait_ge(b_y, c(GT, GT))
                        for j in range(3):
                            bank = (U_BANK, R_BANK)[t % 2] + j if j < 2 else G_BANK + t % 2
                            for k in range(KC):
                                last = nc.tensor.matmul(psum[:, bank, :], xt2[:, k, t * P:(t + 1) * P],
                                                        w3[:, k, j * E:(j + 1) * E],
                                                        start=(k == 0), stop=(k == KC - 1))
                        last.then_inc(b_qkv, 1)

                    def turn_qk(c, t):
                        pe.wait_ge(b_qk, c(GT, t + 1))
                        if t:
                            pe.wait_ge(b_r, c(GT, t))
                        for k in range(2 * KC):
                            last = nc.tensor.transpose(psum[:, T_BANK + k // KC, (k % KC) * P:(k % KC + 1) * P],
                                                       qk[:, k * P:(k + 1) * P], ident[:, :])
                        last.then_inc(b_tq, 1)

                    pe.wait_ge(w_b, W_B)
                    turn_input2(this(0))
                    pe.wait_ge(b_xt1, GT)
                    up_and_fc1(this(0), range(N_U))
                    gate_logits()
                    pe.wait_ge(b_hr, N_U)
                    pe.wait_ge(b_h, N_UP)
                    for t in range(GT):
                        if t >= 2:
                            pe.wait_ge(b_y, t - 1)
                        shared(t)
                        routed(t)
                    with pe.Fori(0, G - 1) as g:
                        mine, nxt = this(g), after(g)
                        turn_input2(nxt)
                        pe.wait_ge(b_xt1, nxt(GT, GT))
                        up_and_fc1(nxt, range(0, 7), mine)
                        turn_input3(mine, range(0, 2))
                        up_and_fc1(nxt, range(7, 8))
                        turn_input3(mine, range(2, GT))
                        up_and_fc1(nxt, range(8, N_U))
                        gate_logits()
                        pe.wait_ge(b_xt2, mine(GT, GT))
                        pe.wait_ge(b_hr, nxt(N_U, N_U))
                        pe.wait_ge(b_gs, nxt(1, 1))
                        for t in range(GT):
                            qkv(mine, t)
                            if t:
                                turn_qk(mine, t - 1)
                        pe.wait_ge(b_h, nxt(N_UP, N_UP))
                        pe.wait_ge(b_ev, mine(GT, GT - 1))
                        shared(0)
                        pe.wait_ge(b_ev, mine(GT, GT))
                        pe.wait_ge(b_vs, mine(GT, GT))
                        routed(0)
                        turn_qk(mine, GT - 1)
                        for t in range(1, GT):
                            if t >= 2:
                                pe.wait_ge(b_y, nxt(GT, t - 1))
                            shared(t)
                            routed(t)
                        pe.wait_ge(b_r, mine(GT, GT))
                    mine = this(G - 1)
                    turn_input3(mine, range(GT))
                    pe.wait_ge(b_xt2, mine(GT, GT))
                    pe.wait_ge(b_sh, mine(GT, GT))
                    for t in range(GT):
                        qkv(mine, t)
                        if t:
                            turn_qk(mine, t - 1)
                    turn_qk(mine, GT - 1)
        b_stack.close()

        wo = sb("wo", [P, KC, E])
        bo = sb("bo", [P, E])
        w4 = sb("w4", [P, KC, E])
        b4 = sb("b4", [P, E])
        lora_a = sb("lora_a", [P, E])
        lora_b = sb("lora_b", [P, E])
        route_w = sb("route_w", [P, KC, NEX])
        route_b = sb("route_b", [P, NEX])
        own = sb("own", [P, NEX])
        counted = sb("counted", [P, 3, P])
        ctx = sb("ctx", [P, QUADS // 2, BT, P])
        w_d = sem("w_d")
        W_D = 16 * 10

        batches = [(0, 0), (1, 0), (0, 1), (1, 1), (0, 2), (0, 3), (1, 2), (1, 4), (1, 5), (1, 6), (1, 7), (1, 3)]
        NBATCH = len(batches)
        HALF0 = batches.index((0, 3))
        PIECES = NBATCH * QH
        DIAG = BT * QH

        def span(half, j):
            q0 = max(half * 512, j * P)
            return q0, half * 512 + 512 - q0

        def units(heads):
            return [(h, i, lo, min((i + 1) * P, lo + 512)) for h in heads for i in (7, 0, 6, 1, 5, 2, 4, 3)
                    for lo in range(0, (i + 1) * P, 512)]

        FIRST = len(units(range(QH + 1))) + 1
        RING = len(units(range(QH))) + 3
        SLOTS = 3
        assert RING % SLOTS == 0

        def schedule(ahead, beyond):
            feed = []
            if ahead:
                feed = [("unit", u) for u in units(range(1, QH))] + [("join", 0)]
                more = [("next", u) for u in units(range(1))] if beyond else []
                feed += more[:3] + [("peak", 0)] + more[3:]

            def cost(item):
                return 100 + item[1][3] - item[1][2] if item[1] else 100

            total, fed, done = sum(cost(f) for f in feed), 0, 0
            pieces = sum(QH * (span(*b)[1] + 100) for b in batches)
            for m in range(NBATCH):
                for h in range(QH):
                    yield "piece", m * QH + h
                    done += span(*batches[m])[1] + 100
                    while len(feed) > TAIL and fed * pieces <= done * total * 0.97:
                        fed += cost(feed[0])
                        yield feed.pop(0)
                if m:
                    yield "pv", m - 1
                if m == HALF0 + 3:
                    yield "turn", 0
            while len(feed) > TAIL // 2:
                yield feed.pop(0)
            yield "pv", NBATCH - 1
            while feed:
                yield feed.pop(0)
            yield "turn", 1

        TAIL = 4

        with ExitStack() as sc_:
            q_stack = sb("q_stack", [P, 4, QH * BT, P], BF16, stack=sc_)
            qs = q_stack[:, :, :, :].rearrange("p u (h t) q -> p u h (t q)", h=QH)
            ks = sb("ks", [P, 4, QH, S], BF16, stack=sc_)
            vs = sb("vs", [P, 4, BT, QH * VW], stack=sc_)
            pt = sb("c_pt", [P, 2 * QH, 512], stack=sc_)
            junk = sb("c_junk", [P, 3, 512], BF16, stack=sc_)
            causal = sb("c_causal", [P, 512], stack=sc_)
            mx = sb("c_mx", [P, 2, 2, QH * BT], stack=sc_)
            peak_in = sb("c_peak_in", [P, QH * BT], stack=sc_)
            mp = sb("c_mp", [QH * BT, 3, P], BF16, stack=sc_)
            mr = sb("c_mr", [QH * BT, P], stack=sc_)
            ot = sb("c_ot", [P, S], stack=sc_)
            rec = sb("c_rec", [P, 2, BT // 2 * QH], stack=sc_)

            c_in = sem("c_in")
            c_ld = [sem(f"c_ld{u}") for u in range(4)]
            c_one = sem("c_one")
            c_ap = sem("c_ap")
            c_ac = sem("c_ac")
            c_mp = sem("c_mp")
            c_mrow = sem("c_mrow")
            c_j = sem("c_j")
            c_m = sem("c_m")
            c_v = sem("c_v")
            c_sb = sem("c_sb")
            c_ex = sem("c_ex")
            c_af = sem("c_af")
            c_o = sem("c_o")
            c_oe = sem("c_oe")
            LOADS = 2 * COPIES + 1

            with nc.Block() as block:
                @block.sync
                def _(sp):
                    def load(n, u):
                        for scr, dst, parts_ in ((k_scr, ks, K_PARTS), (q_scr, qs, Q_PARTS)):
                            for c, part in enumerate(parts_):
                                sp.dma_start(dst[c * HD:(c + 1) * HD, u, :, :],
                                             scr[part, bass.ds(n * QH * HD, QH * HD), :]
                                             .rearrange("(h d) s -> d h s", d=HD)).then_inc(c_ld[u], 16)
                        sp.dma_start(vs[:, u, :, :],
                                     v_scr[bass.ds((n // BQ) * BT, BT), :, bass.ds((n % BQ) * QH * VW, QH * VW)]
                                     .rearrange("t p n -> p t n")).then_inc(c_ld[u], 16)

                    load(0, 0)
                    sp.dma_start(causal[:, :], ins["causal"]).then_inc(c_in, 16)
                    for u in range(1, 4):
                        load(u, u)
                    for dst, name in ((wo, "wo"), (w4, "w4"), (route_w, "route_w")):
                        sp.dma_start(dst[:, :, :], ins[name].rearrange("(k p) n -> p k n", p=P)).then_inc(w_d, 16)
                    for dst, name in ((bo, "bo"), (b4, "b4"), (route_b, "route_b")):
                        sp.dma_start(dst[:, :], ins[name].partition_broadcast(P)).then_inc(w_d, 16)
                    for dst, name in ((lora_a, "lora_a"), (lora_b, "lora_b"), (own, "own")):
                        sp.dma_start(dst[:, :], ins[name]).then_inc(w_d, 16)
                    sp.dma_start(counted[:, :, :], ins["counted"].rearrange("p (a n) -> p a n", a=3)).then_inc(w_d, 16)

                    def peaks(n, u):
                        sp.wait_ge(c_mp, n + 1)
                        for j in range(3):
                            sp.dma_start(q_stack[KR + j:KR + j + 1, u, :, :],
                                         mp[:, j, :]).then_inc(c_mrow, 16)

                    peaks(0, 0)
                    with sp.Fori(0, QUADS // 4 - 1) as it:
                        for u in range(4):
                            n = it * 4 + u
                            peaks(n + 1, (u + 1) % 4)
                            sp.wait_ge(c_o, n * 2 + 2)
                            load(n + 4, u)
                    for u in range(3):
                        peaks(QUADS - 4 + u + 1, u + 1)
                    sp.wait_ge(c_mrow, QUADS * 48)

                @block.gpsimd
                def _(pool):
                    nc.gpsimd.memset(ks[KR:KM, :, :, :], 1.0).then_inc(c_one, 1)

                    def mask(n, u):
                        d = 0
                        for m, (half, j) in enumerate(batches):
                            if span(half, j)[0] != j * P:
                                continue
                            for h in range(QH):
                                p = m * QH + h
                                wait_apart(pool, c_ex, n * PIECES + (p + 1), passed_p)
                                blk = pt[:, p % (2 * QH), 0:P]
                                nc.gpsimd.affine_select(out=blk, in_=blk, compare_op=ALU.is_ge, fill=0.0, base=0,
                                                        pattern=[[1, P]], channel_multiplier=-1).then_inc(c_af, 1)
                                d += 1
                        assert d == DIAG

                    with pool.Fori(0, QUADS) as n:
                        mask(n, 0)

                @block.scalar
                def _(act):
                    with act.Fori(0, QUADS) as n:
                        for m, (half, j) in enumerate(batches):
                            w = span(half, j)[1]
                            for h in range(QH):
                                p = m * QH + h
                                act.wait_ge(c_sb, n * PIECES + (p + 1))
                                nc.scalar.activation(pt[:, p % (2 * QH), 0:w], psum[:, SLOTS + p % 3, 0:w], ACT.Exp,
                                                     scale=SCALE3).then_inc(c_ex, 1)
                            if m == HALF0 + 2 or m == NBATCH - 1:
                                b = int(m == NBATCH - 1)
                                act.wait_ge(c_o, n * 2 + (b + 1))
                                nc.scalar.activation(ot[:, b * 512:(b + 1) * 512], psum[:, 6 + b, :],
                                                     ACT.Copy).then_inc(c_oe, 1)

                @block.vector
                def _(dve):
                    ch = Chain(dve, c_v)
                    dve.wait_ge(c_in, 16)

                    def unit_max(unit, slot, par, used):
                        h, i, lo, hi = unit
                        w, s = hi - lo, h * BT + i
                        wait_apart(dve, c_ap, used + 1, passed_v)
                        most = mx[:, par, lo // 512, s:s + 1]
                        if hi == (i + 1) * P:
                            nc.vector.tensor_tensor_reduce(
                                out=junk[:, slot, 0:w], in0=psum[:, slot, 0:w], in1=causal[:, 512 - w:512], scale=1.0,
                                scalar=-3.4e38, op0=ALU.add, op1=ALU.max, accum_out=most).then_inc(c_ac, 1)
                        else:
                            nc.vector.tensor_reduce(most, psum[:, slot, 0:w], X_AXIS, ALU.max).then_inc(c_ac, 1)

                    def join(n, par, used):
                        dve.wait_ge(c_ac, used)
                        nc.vector.tensor_tensor(peak_in[:, :], mx[:, par, 0, :], mx[:, par, 1, :],
                                                ALU.max).then_inc(c_j, 1)

                    def peak_parts(slot, used):
                        dve.wait_ge(c_ap, used + 1)
                        t = psum[0:QH * BT, slot, 0:P]
                        ch.link(nc.vector.tensor_scalar(mp[:, 0, :], t, -1.0, None, ALU.mult))
                        nc.vector.scalar_tensor_tensor(out=mr[:, :], in0=t, scalar=-1.0, in1=mp[:, 0, :],
                                                       op0=ALU.mult, op1=ALU.subtract).then_inc(c_ac, 1)
                        dve.wait_ge(c_ac, used + 1)
                        ch.link(nc.vector.tensor_copy(mp[:, 1, :], mr[:, :]))
                        nc.vector.tensor_tensor(mp[:, 2, :], mr[:, :], mp[:, 1, :], ALU.subtract).then_inc(c_mp, 1)

                    def context(pair, i, half, slot, used):
                        dve.wait_ge(c_ap, used + 1)
                        c4 = psum[:, slot, :].rearrange("p (t h w) -> p t h w", h=QH, w=VW)
                        r4 = rec[:, half, :].rearrange("p (t h o) -> p t h o", h=QH, o=1)
                        ch.link(nc.vector.reciprocal(r4, c4[:, :, :, HD:HD + 1]))
                        o = ctx[:, bass.ds(pair, 1), half * 4:half * 4 + 4, i * QH * HD:(i + 1) * QH * HD]\
                            .rearrange("p o t (h d) -> p (o t) h d", d=HD)
                        nc.vector.tensor_tensor(o, c4[:, :, :, 0:HD], r4.broadcast_to([P, 4, QH, HD]),
                                                ALU.mult).then_inc(c_ac, 1)

                    def step(n, u, pair, ahead, beyond):
                        ch.begin(CH0 + n * CHN)
                        k = 0
                        for what, a in schedule(ahead, beyond):
                            slot = (FIRST + k) % SLOTS
                            used = n * RING + (FIRST + k)
                            if n is last_n:
                                used -= len(units(range(1)))
                            if what == "unit":
                                unit_max(a, slot, (u + 1) % 2, used)
                            elif what == "next":
                                unit_max(a, slot, u % 2, used)
                            elif what == "peak":
                                peak_parts(slot, used)
                            elif what == "turn":
                                context(pair, u % 2, a, slot, used)
                            else:
                                if what == "join":
                                    join(n, (u + 1) % 2, used)
                                continue
                            k += 1
                        assert ch.k == (CHN if ahead else 2), ch.k

                    CH0, CHN, last_n = 2, 4, QUADS - 1
                    nc.vector.memset(mx[:, :, 1, :], -3.4e38).then_inc(c_m, 1)
                    dve.wait_ge(c_m, 1)
                    for k, unit in enumerate(units(range(QH))):
                        unit_max(unit, k % SLOTS, 0, k)
                    join(0, 0, RING - 3)
                    peak_parts((RING - 3) % SLOTS, RING - 3)
                    for k, unit in enumerate(units(range(1))):
                        unit_max(unit, (RING - 2 + k) % SLOTS, 1, RING - 2 + k)
                    with dve.Fori(0, QUADS // 4 - 1) as it:
                        for u in range(4):
                            step(it * 4 + u, u, it * 2 + u // 2, True, True)
                    for u in range(4):
                        n = QUADS - 4 + u
                        step(n, u, n // 2, u < 3, u < 2)

                @block.tensor
                def _(pe):
                    def score_unit(unit, slot, u, used):
                        h, i, lo, hi = unit
                        if not isinstance(used, int) or used >= SLOTS:
                            pe.wait_ge(c_ac, used - (SLOTS - 1))
                        nc.tensor.matmul(psum[:, slot, 0:hi - lo], qs[0:KR, u, h, i * P:(i + 1) * P],
                                         ks[0:KR, u, h, lo:hi], start=True, stop=True).then_inc(c_ap, 1)

                    def peak(n, slot, used):
                        pe.wait_ge(c_ac, used - (SLOTS - 1))
                        pe.wait_ge(c_j, n + 1)
                        nc.tensor.transpose(psum[0:QH * BT, slot, 0:P], peak_in[:, :], ident[:, :]).then_inc(c_ap, 1)

                    def turn(n, half, slot, used):
                        pe.wait_ge(c_ac, used - (SLOTS - 1))
                        pe.wait_ge(c_oe, n * 2 + (half + 1))
                        for t in range(4):
                            at_ = (half * 4 + t) * P
                            last = nc.tensor.transpose(psum[:, slot, t * P:(t + 1) * P], ot[:, at_:at_ + P], ident[:, :])
                        last.then_inc(c_ap, 1)

                    def piece(n, p, u):
                        m, h = divmod(p, QH)
                        half, j = batches[m]
                        q0, w = span(half, j)
                        if p >= 3:
                            pe.wait_ge(c_ex, n * PIECES + (p - 2))
                        nc.tensor.matmul(psum[:, SLOTS + p % 3, 0:w], ks[0:KM, u, h, j * P:(j + 1) * P],
                                         qs[0:KM, u, h, q0:q0 + w], start=True, stop=True).then_inc(c_sb, 1)

                    diags = [m for m, (half, j) in enumerate(batches) if span(half, j)[0] == j * P]

                    def values(n, m, u):
                        half, j = batches[m]
                        q0, w = span(half, j)
                        pe.wait_ge(c_ex, n * PIECES + (m + 1) * QH)
                        if m in diags:
                            pe.wait_ge(c_af, n * DIAG + (diags.index(m) + 1) * QH)
                        mine = [b for b in batches if b[0] == half]
                        for h in range(QH):
                            last = nc.tensor.matmul(psum[h * VW:(h + 1) * VW, 6 + half, q0 - half * 512:q0 - half * 512 + w],
                                                    vs[:, u, j, h * VW:(h + 1) * VW], pt[:, (m * QH + h) % (2 * QH), 0:w],
                                                    start=(batches[m] == mine[0]), stop=(batches[m] == mine[-1]),
                                                    skip_group_check=True)
                        if batches[m] == mine[-1]:
                            last.then_inc(c_o, 1)

                    def step(n, u, ahead, beyond, loaded):
                        pe.wait_ge(c_mrow, n * 48 + 48)
                        k = 0
                        for what, a in schedule(ahead, beyond):
                            slot = (FIRST + k) % SLOTS
                            used = n * RING + (FIRST + k)
                            if n is last_n:
                                used -= len(units(range(1)))
                            if what == "piece":
                                piece(n, a, u)
                            elif what == "pv":
                                values(n, a, u)
                            elif what != "join":
                                if what == "unit":
                                    score_unit(a, slot, (u + 1) % 4, used)
                                elif what == "next":
                                    if a == units(range(1))[0]:
                                        pe.wait_ge(c_ld[(u + 2) % 4], loaded)
                                    score_unit(a, slot, (u + 2) % 4, used)
                                elif what == "peak":
                                    peak(n + 1, slot, used)
                                else:
                                    turn(n, a, slot, used)
                                k += 1

                    last_n = QUADS - 1
                    pe.wait_ge(c_ld[0], LOADS * 16)
                    for k, unit in enumerate(units(range(QH))):
                        score_unit(unit, k % SLOTS, 0, k)
                    peak(0, (RING - 3) % SLOTS, RING - 3)
                    pe.wait_ge(c_ld[1], LOADS * 16)
                    for k, unit in enumerate(units(range(1))):
                        score_unit(unit, (RING - 2 + k) % SLOTS, 1, RING - 2 + k)
                    pe.wait_ge(c_one, 1)
                    with pe.Fori(0, QUADS // 4 - 1) as it:
                        for u in range(4):
                            step(it * 4 + u, u, True, True, (it + (1 if u < 2 else 2)) * (LOADS * 16))
                    for u in range(4):
                        step(QUADS - 4 + u, u, u < 3, u < 2, QUADS // 4 * LOADS * 16)

        with ExitStack() as sd:
            ctxs = sb("d_ctxs", [P, BQ // 2, BT, P], stack=sd)
            ct = sb("d_ct", [P, 2, KC, P], stack=sd)
            rows = sb("d_rows", [P, BT, E], stack=sd)
            xt = sb("d_xt", [P, KC, S], stack=sd)
            st = sb("d_st", [P, BT, 6], stack=sd)
            tmp = sb("d_tmp", [P, 6, BT], stack=sd)
            mt = sb("d_mt", [P, KC, P], stack=sd)
            lg = sb("d_lg", [P, NEX], stack=sd)
            le = sb("d_le", [P, NEX], stack=sd)
            one = sb("d_one", [P, 8], stack=sd)
            bs = sb("d_bs", [P, E], stack=sd)
            weff = sb("d_weff", [P, KC, E], stack=sd)

            d_cx = sem("d_cx")
            d_tp = sem("d_tp")
            d_xt = sem("d_xt")
            d_ou = sem("d_ou")
            d_used = sem("d_used")
            d_y = sem("d_y")
            d_var = sem("d_var")
            d_sd = sem("d_sd")
            d_xn = sem("d_xn")
            d_mn = sem("d_mn")
            d_mt = sem("d_mt")
            d_lg = sem("d_lg")
            d_le = sem("d_le")
            d_ex = sem("d_ex")
            d_bs = sem("d_bs")
            d_we = sem("d_we")
            d_wf = sem("d_wf")
            d_f = sem("d_f")
            d_fy = sem("d_fy")
            d_o = sem("d_o")
            d_out = sem("d_out")
            d_v = sem("d_v")
            MEAN_ROWS = S - 1 - 107
            CHD = 22

            with nc.Block() as block:
                @block.sync
                def _(sp):
                    sp.sem_inc(d_used, 1)
                    with sp.Fori(0, NB) as b:
                        sp.wait_ge(d_used, b + 1)
                        sp.dma_start(ctxs[:, :, :, :], ctx[:, bass.ds(b * KC, KC), :, :]).then_inc(d_cx, 16)
                        for t in range(BT):
                            sp.wait_ge(d_o, b * BT + (t + 1))
                            sp.dma_start(out[bass.ds(b * S + t * P, P), :], rows[:, t, :]).then_inc(d_out, 16)
                    sp.wait_ge(d_out, TILES * 16 + 16)

                @block.vector
                def _(dve):
                    ch = Chain(dve, d_v)
                    dve.sem_inc(d_out, 16)
                    dve.wait_ge(w_d, W_D)

                    def tile_of(a, n):
                        return a[:, bass.ds(n, 1), :].rearrange("p o e -> p (o e)")

                    with dve.Fori(0, NB) as b:
                        ch.begin(b * CHD)

                        def scaled(dst, src, t):
                            return nc.vector.tensor_scalar(dst, src, tmp[:, 0, t:t + 1], tmp[:, 5, t:t + 1],
                                                           ALU.subtract, ALU.mult)

                        dve.wait_ge(d_out, b * (BT * 16) + 16)
                        for t in range(BT):
                            dve.wait_ge(d_ou, b * BT + (t + 1))
                            nc.vector.tensor_tensor(rows[:, t, :], psum[:, 2 + t % 2, :], bo[:, :],
                                                    ALU.add).then_inc(d_y, 1)
                            dve.wait_ge(d_y, b * BT + (t + 1))
                            last = nc.vector.bn_stats(st[:, t, :], rows[:, t, :])
                        ch.link(last)
                        finish_stats(dve, d_var, d_sd, ch, st, tmp, BT, E, None, b * 3 + 1)
                        for t in range(BT):
                            last = scaled(rows[:, t, :], rows[:, t, :], t)
                        ch.link(last)
                        for t in range(BT):
                            last = nc.vector.tensor_tensor(tile_of(xs, b * BT + t), tile_of(xs, b * BT + t),
                                                           rows[:, t, :], ALU.add)
                        ch.mark(last)
                        ch.need_apart(passed_v)
                        for t in range(BT):
                            last = nc.vector.bn_stats(st[:, t, :], tile_of(xs, b * BT + t))
                        ch.link(last)
                        finish_stats(dve, d_var, d_sd, ch, st, tmp, BT, E, None, b * 3 + 2)
                        for t in range(BT):
                            scaled(rows[:, t, :], tile_of(xs, b * BT + t), t).then_inc(d_xn, 1)
                        dve.wait_ge(d_lg, b + 1)
                        ch.link(nc.vector.tensor_tensor(lg[:, :], psum[:, 2, 0:NEX], route_b[:, :], ALU.add))
                        ch.link(nc.vector.tensor_reduce(one[:, 0:1], lg[:, :], X_AXIS, ALU.max))
                        nc.vector.tensor_scalar(lg[:, :], lg[:, :], one[:, 0:1], None, ALU.subtract).then_inc(d_le, 1)
                        dve.wait_ge(d_ex, b + 1)
                        ch.link(nc.vector.tensor_reduce(one[:, 1:2], le[:, :], X_AXIS, ALU.add))
                        ch.link(nc.vector.reciprocal(one[:, 2:3], one[:, 1:2]))
                        ch.link(nc.vector.tensor_scalar(le[:, :], le[:, :], one[:, 2:3], None, ALU.mult))
                        ch.link(nc.vector.tensor_tensor(lg[:, :], le[:, :], own[:, :], ALU.mult))
                        ch.link(nc.vector.tensor_reduce(one[:, 3:4], lg[:, :], X_AXIS, ALU.add))
                        nc.vector.tensor_scalar(bs[:, :], lora_b[:, :], one[:, 3:4], None, ALU.mult).then_inc(d_bs, 1)
                        dve.wait_ge(d_we, b + 1)
                        for c in range(KC):
                            last = nc.vector.tensor_tensor(weff[:, c, :], psum[:, 4 + c, :], w4[:, c, :], ALU.add)
                        last.then_inc(d_wf, 1)
                        for t in range(BT):
                            dve.wait_ge(d_f, b * BT + (t + 1))
                            nc.vector.tensor_tensor(rows[:, t, :], psum[:, 2 + t % 2, :], b4[:, :],
                                                    ALU.add).then_inc(d_fy, 1)
                            dve.wait_ge(d_fy, b * BT + (t + 1))
                            last = nc.vector.bn_stats(st[:, t, :], rows[:, t, :])
                        ch.link(last)
                        finish_stats(dve, d_var, d_sd, ch, st, tmp, BT, E, None, b * 3 + 3)
                        for t in range(BT):
                            last = scaled(rows[:, t, :], rows[:, t, :], t)
                        ch.link(last)
                        for t in range(BT):
                            nc.vector.tensor_tensor(rows[:, t, :], tile_of(xs, b * BT + t), rows[:, t, :],
                                                    ALU.add).then_inc(d_o, 1)
                        assert ch.k == CHD, ch.k

                @block.scalar
                def _(act):
                    with act.Fori(0, NB) as b:
                        for t in range(BT):
                            act.wait_ge(d_tp, b * 2 * BT + (t + 1))
                            nc.scalar.activation(ct[:, t % 2, :, :].rearrange("p c n -> p (c n)"), psum[:, t % 2, :],
                                                 ACT.Copy).then_inc(d_xt, 1)
                        root(act, d_var, d_sd, tmp, BT, b * 3 + 1)
                        root(act, d_var, d_sd, tmp, BT, b * 3 + 2)
                        for t in range(BT):
                            act.wait_ge(d_tp, b * 2 * BT + (BT + t + 1))
                            nc.scalar.activation(xt[:, :, t * P:(t + 1) * P],
                                                 psum[:, t % 2, :].rearrange("p (c n) -> p c n", n=P),
                                                 ACT.Copy).then_inc(d_xt, 1)
                        act.wait_ge(d_mn, b + 1)
                        for c in range(KC):
                            last = nc.scalar.activation(mt[:, c, :], psum[:, 4 + c, 0:P], ACT.Copy,
                                                        scale=1.0 / MEAN_ROWS)
                        last.then_inc(d_mt, 1)
                        act.wait_ge(d_le, b + 1)
                        nc.scalar.activation(le[:, :], lg[:, :], ACT.Exp).then_inc(d_ex, 1)
                        root(act, d_var, d_sd, tmp, BT, b * 3 + 3)

                @block.tensor
                def _(pe):
                    pe.wait_ge(w_d, W_D)
                    with pe.Fori(0, NB) as b:
                        pe.wait_ge(d_cx, b * 16 + 16)

                        def turn_ctx(t):
                            if t >= 2:
                                pe.wait_ge(d_xt, b * 2 * BT + (t - 1))
                            for c in range(KC):
                                last = nc.tensor.transpose(psum[:, t % 2, c * P:(c + 1) * P],
                                                           ctxs[:, c, t, :], ident[:, :])
                            last.then_inc(d_tp, 1)

                        turn_ctx(0)
                        for t in range(BT):
                            if t + 1 < BT:
                                turn_ctx(t + 1)
                            pe.wait_ge(d_xt, b * 2 * BT + (t + 1))
                            if t >= 2:
                                pe.wait_ge(d_y, b * BT + (t - 1))
                            for c in range(KC):
                                last = nc.tensor.matmul(psum[:, 2 + t % 2, :], ct[:, t % 2, c, :], wo[:, c, :],
                                                        start=(c == 0), stop=(c == KC - 1))
                            last.then_inc(d_ou, 1)
                        for t in range(BT):
                            pe.wait_ge(d_xn, b * BT + (t + 1))
                            if t >= 2:
                                pe.wait_ge(d_xt, b * 2 * BT + (BT + t - 1))
                            for c in range(KC):
                                last = nc.tensor.transpose(psum[:, t % 2, c * P:(c + 1) * P],
                                                           rows[:, t, c * P:(c + 1) * P], ident[:, :])
                                if t == c == 0:
                                    last.then_inc(d_used, 1)
                            last.then_inc(d_tp, 1)
                            which = 0 if t == 0 else 2 if t == BT - 1 else 1
                            for c in range(KC):
                                last = nc.tensor.matmul(psum[:, 4 + c, 0:P], rows[:, t, c * P:(c + 1) * P],
                                                        counted[:, which, :], start=(t == 0), stop=(t == BT - 1))
                        last.then_inc(d_mn, 1)
                        pe.wait_ge(d_mt, b + 1)
                        for c in range(KC):
                            last = nc.tensor.matmul(psum[:, 2, 0:NEX], mt[:, c, :], route_w[:, c, :],
                                                    start=(c == 0), stop=(c == KC - 1))
                        last.then_inc(d_lg, 1)
                        pe.wait_ge(d_bs, b + 1)
                        for c in range(KC):
                            last = nc.tensor.matmul(psum[:, 4 + c, :], lora_a[:, c * P:(c + 1) * P], bs[:, :],
                                                    start=True, stop=True)
                        last.then_inc(d_we, 1)
                        pe.wait_ge(d_wf, b + 1)
                        pe.wait_ge(d_xt, b * 2 * BT + 2 * BT)
                        for t in range(BT):
                            if t >= 2:
                                pe.wait_ge(d_fy, b * BT + (t - 1))
                            for c in range(KC):
                                last = nc.tensor.matmul(psum[:, 2 + t % 2, :], xt[:, c, t * P:(t + 1) * P],
                                                        weff[:, c, :], start=(c == 0), stop=(c == KC - 1))
                            last.then_inc(d_f, 1)


def constants():
    half = HALF
    inv_freq = (np.float32(1.0) / np.float32(10000.0) ** (np.arange(half, dtype=np.float32) / np.float32(half)))
    ang = np.arange(S, dtype=np.float32)[:, None] * inv_freq.astype(np.float32)[None, :]
    cos, sin = np.cos(ang).astype(np.float32), np.sin(ang).astype(np.float32)
    causal = np.zeros((P, 512), np.float32)
    causal[:, 512 - P:] = np.triu(np.full((P, P), MASK / SCALE3, np.float32), 1)
    own = np.zeros((P, NEX), np.float32)
    own[np.arange(P), np.arange(P) // RANK] = 2.0
    counted = np.ones((P, 3, P), np.float32)
    counted[:107, 0, :] = 0.0
    counted[P - 1:, 2, :] = 0.0
    return {"ident": np.eye(P, dtype=np.float32), "rope_c": np.concatenate([cos, cos], 1),
            "rope_s": np.concatenate([-sin, sin], 1), "causal": causal, "own": own,
            "counted": counted.reshape(P, 3 * P)}


def kernel(L0_attn_x, L0_attn_Wq, L0_attn_bq, L0_attn_Wk, L0_attn_bk, L0_attn_Wv, L0_attn_bv, L0_ffn_gate_w,
           L0_ffn_up_w, L0_ffn_down_w, L0_ffn_fc1_w, L0_ffn_fc2_w, L0_ffn_expert_w, L0_ffn_ln_gamma, L0_ffn_ln_beta,
           L1_attn_qkv_w, L1_attn_qkv_b, L1_attn_out_w, L1_attn_out_b, L1_ffn_W, L1_ffn_b, L1_ffn_A, L1_ffn_B,
           L1_ffn_router_W, L1_ffn_router_b):
    import concourse.bacc as bacc
    from concourse.bass_utils import run_bass_kernel_spmd

    arrays = {
        "x": np.reshape(L0_attn_x, (NB * S, E)),
        "wq0": np.reshape(L0_attn_Wq, (E, I0 * R0)), "bq0": np.reshape(L0_attn_bq, (I0 * R0,)),
        "wk0": np.reshape(L0_attn_Wk, (E, I0)), "bk0": np.reshape(L0_attn_bk, (I0,)),
        "wv0": np.reshape(L0_attn_Wv, (E, I0)), "bv0": np.reshape(L0_attn_bv, (I0,)),
        "gate": L0_ffn_gate_w, "up": L0_ffn_up_w, "down": L0_ffn_down_w, "fc1": L0_ffn_fc1_w, "fc2": L0_ffn_fc2_w,
        "expert_t": np.transpose(L0_ffn_expert_w), "gamma": L0_ffn_ln_gamma, "beta": L0_ffn_ln_beta,
        "w3": L1_attn_qkv_w, "b3": L1_attn_qkv_b, "wo": L1_attn_out_w, "bo": L1_attn_out_b,
        "w4": np.transpose(L1_ffn_W), "b4": L1_ffn_b,
        "lora_a": np.reshape(L1_ffn_A, (NEX * RANK, E)),
        "lora_b": np.reshape(np.transpose(L1_ffn_B, (0, 2, 1)), (NEX * RANK, E)),
        "route_w": np.transpose(L1_ffn_router_W), "route_b": L1_ffn_router_b,
    }
    arrays.update(constants())
    nc = bacc.Bacc("TRN2", target_bir_lowering=False, num_devices=1)
    fed, ins = {}, {}
    for name, a in arrays.items():
        a = np.ascontiguousarray(a)
        fed[f"in_{name}"] = a
        ins[name] = nc.dram_tensor(f"in_{name}", a.shape, mybir.dt.from_np(a.dtype), kind="ExternalInput").ap()
    out = nc.dram_tensor("out", (NB * S, E), F32, kind="ExternalOutput").ap()
    layers(nc, ins, out)
    got = run_bass_kernel_spmd(nc, [fed], core_ids=[0])
    return got.results[0]["out"].reshape(NB, S, E)
```

```python
from contextlib import ExitStack

import concourse.bass as bass
import numpy as np
from concourse import mybir

F32 = mybir.dt.float32
BF16 = mybir.dt.bfloat16
ALU = mybir.AluOpType
ACT = mybir.ActivationFunctionType
X_AXIS = mybir.AxisListType.X

P = 128
NB, S, E = 2, 1024, 512
TILES = NB * S // P
BT = S // P
KC = E // P
D0, G0, R0 = 16, 8, 4
I0 = D0 * G0
INT, LAT, NE = 1024, 256, 8
H, HD = 32, 16
HALF = HD // 2
VW = 32
QH = 4
QUADS = NB * H // QH
BQ = H // QH
NEX, RANK = 8, 16
EPS = 1e-5
MASK = -66504.0
SCALE3 = HD ** -0.5
GT = 4
GR = GT * P
CHAIN_B = 22
COPIES = 6
Q_PARTS = (0, 0, 0, 1, 1, 2)
K_PARTS = (0, 1, 2, 0, 1, 0)
KR = COPIES * HD
KM = KR + 3


class Chain:

    def __init__(self, eng, sem):
        self.eng, self.sem, self.base, self.k = eng, sem, 0, 0

    def begin(self, base):
        self.base, self.k = base, 0

    def mark(self, ins):
        ins.then_inc(self.sem, 1)
        self.k += 1
        return self.k

    def need(self, k=None):
        self.eng.wait_ge(self.sem, self.base + (self.k if k is None else k))

    def link(self, ins):
        self.mark(ins)
        self.need()

    def need_apart(self, passed):
        wait_apart(self.eng, self.sem, self.base + self.k, passed)


def wait_apart(eng, sem, count, passed):
    eng.wait_ge(sem, count)
    eng.sem_inc(passed, 1)


def layers(nc, ins, out):
    with ExitStack() as whole:
        def at(stack, make, name, shape, dt=F32):
            return stack.enter_context(make(name, shape, dt))

        def sem(name):
            return whole.enter_context(nc.semaphore(name))

        def sb(name, shape, dt=F32, stack=whole):
            return at(stack, nc.sbuf_tensor, name, shape, dt)

        xs = sb("xs", [P, TILES, E])
        ident = sb("ident", [P, P])
        psum = whole.enter_context(nc.psum_tensor("psum", [P, 8, 512], F32))

        q_scr = nc.dram_tensor("q_scr", [3, NB * E, S], BF16).ap()
        k_scr = nc.dram_tensor("k_scr", [3, NB * E, S], BF16).ap()
        v_scr = nc.dram_tensor("v_scr", [TILES, P, H * VW], F32).ap()

        x_in = [sem(f"x_in{c}") for c in range(4)]
        const_in = sem("const_in")
        passed_v = sem("passed_v")
        passed_p = sem("passed_p")

        def finish_stats(dve, act_var, act_sd, chain, st, tmp, n, count, var_at, sd_at):
            nc.vector.tensor_tensor(tmp[:, 0, 0:n], st[:, 0:n, 1], st[:, 0:n, 4], ALU.add)
            nc.vector.tensor_tensor(tmp[:, 1, 0:n], st[:, 0:n, 1], st[:, 0:n, 4], ALU.subtract)
            chain.link(nc.vector.tensor_tensor(tmp[:, 2, 0:n], st[:, 0:n, 2], st[:, 0:n, 5], ALU.add))
            nc.vector.tensor_scalar(tmp[:, 0, 0:n], tmp[:, 0, 0:n], 0.5, None, ALU.mult)
            chain.link(nc.vector.scalar_tensor_tensor(out=tmp[:, 3, 0:n], in0=tmp[:, 1, 0:n], scalar=0.25,
                                                      in1=tmp[:, 1, 0:n], op0=ALU.mult, op1=ALU.mult))
            nc.vector.scalar_tensor_tensor(out=tmp[:, 4, 0:n], in0=tmp[:, 2, 0:n], scalar=1.0 / count,
                                           in1=tmp[:, 3, 0:n], op0=ALU.mult, op1=ALU.add).then_inc(act_var, 1)
            dve.wait_ge(act_sd, sd_at)
            chain.link(nc.vector.reciprocal(tmp[:, 5, 0:n], tmp[:, 4, 0:n]))

        def root(act, act_var, act_sd, tmp, n, var_at):
            act.wait_ge(act_var, var_at)
            nc.scalar.activation(tmp[:, 4, 0:n], tmp[:, 4, 0:n], ACT.Sqrt,
                                 bias=eps[:, 0:1]).then_inc(act_sd, 1)

        eps = sb("eps", [P, 1])
        row_mx = sb("row_mx", [P, 2, 2, QH * BT])

        quad0_k = sb("quad0_k", [P, TILES * I0])
        quad0_q = sb("quad0_q", [P, GT * E])
        mixed = quad0_k[:, :].rearrange("p (t e) -> p t e", e=I0)
        block2_in = quad0_q[:, :].rearrange("p (t e) -> p t e", e=E)
        quad0_k = quad0_k[:, :].bitcast(BF16).rearrange("p (h s) -> p h s", s=S)
        quad0_q = quad0_q[:, :].bitcast(BF16).rearrange("p (a q) -> p a q", q=P)
        EARLY = 2

        def units(heads):
            return [(h, i, lo, min((i + 1) * P, lo + 512)) for h in heads for i in (7, 0, 6, 1, 5, 2, 4, 3)
                    for lo in range(0, (i + 1) * P, 512)]

        def unit_scores(psum_part, q, k, unit):
            h, i, lo, hi = unit
            return nc.tensor.matmul(psum_part[:, 0:hi - lo], q[0:KR, h * BT + i, :], k[0:KR, h, lo:hi],
                                    start=True, stop=True)

        def unit_max(psum_part, unit, par, causal, junk):
            h, i, lo, hi = unit
            w, s = hi - lo, h * BT + i
            most = row_mx[:, par, lo // 512, s:s + 1]
            if hi == (i + 1) * P:
                return nc.vector.tensor_tensor_reduce(out=junk[:, 0:w], in0=psum_part[:, 0:w],
                                                      in1=causal[:, 512 - w:512], scale=1.0, scalar=-3.4e38,
                                                      op0=ALU.add, op1=ALU.max, accum_out=most)
            return nc.vector.tensor_reduce(most, psum_part[:, 0:w], X_AXIS, ALU.max)

        def load_stacks(sp, n, q, k, done):
            for scr, dst, parts_ in ((k_scr, k, K_PARTS), (q_scr, q, Q_PARTS)):
                for c, part in enumerate(parts_):
                    sp.dma_start(dst[c * HD:(c + 1) * HD, :, :].rearrange("d a b -> d (a b)")
                                 .rearrange("d (h s) -> d h s", s=S),
                                 scr[part, bass.ds(n * QH * HD, QH * HD), :]
                                 .rearrange("(h d) s -> d h s", d=HD)).then_inc(done, 16)

        b_stack = whole.enter_context(ExitStack())
        mixed_st = sb("mixed_st", [P, TILES, 6], stack=b_stack)
        up = sb("up", [P, KC, INT], stack=b_stack)
        down = sb("down", [P, INT // P, E], stack=b_stack)
        fc1 = sb("fc1", [P, KC, LAT], stack=b_stack)
        lat_out = sb("lat_out", [P, LAT // P, E], stack=b_stack)
        gate = sb("gate", [P, KC, NE], stack=b_stack)
        w3 = sb("w3", [P, KC, 3 * E], stack=b_stack)
        b3 = sb("b3", [P, 3 * E], stack=b_stack)
        gamma = sb("gamma", [P, E], stack=b_stack)
        beta = sb("beta", [P, E], stack=b_stack)
        rope_c = sb("rope_c", [P, BT, HD], stack=b_stack)
        rope_s = sb("rope_s", [P, BT, HD], stack=b_stack)
        w_b = sem("w_b")
        W_B = 16 * 10

        with ExitStack() as sa:
            wq0 = sb("wq0", [P, KC, I0 * R0], stack=sa)
            w0 = sb("w0", [P, KC, 3 * I0], stack=sa)
            bq0 = sb("bq0", [P, I0 * R0], stack=sa)
            b0 = sb("b0", [P, 3 * I0], stack=sa)
            expert_t = sb("expert_t", [P, LAT // P, LAT], stack=sa)
            fc2 = sb("fc2", [P, LAT // P, E], stack=sa)
            st = sb("a_st", [P, TILES, 6], stack=sa)
            tmp = sb("a_tmp", [P, 6, TILES], stack=sa)
            xn = sb("a_xn", [P, 2, E], stack=sa)
            xt = sb("a_xt", [P, 2, E], stack=sa)
            qkv = sb("a_qkv", [P, 2, 3 * I0], stack=sa)
            prod = sb("a_prod", [P, 2, D0 * D0 * G0], stack=sa)
            prov = sb("a_prov", [P, 2, D0 * D0 * G0], stack=sa)
            sc = sb("a_sc", [P, 2, D0 * D0], stack=sa)
            pr = sb("a_pr", [P, 2, D0 * D0], stack=sa)
            mx = sb("a_mx", [P, D0], stack=sa)
            ls = sb("a_ls", [P, 4, D0], stack=sa)
            av = sb("a_av", [P, I0], stack=sa)

            w_a = sem("w_a")
            w_e = sem("w_e")
            a_w0 = sem("a_w0")
            a_var = sem("a_var")
            a_sd = sem("a_sd")
            a_xn = sem("a_xn")
            a_tp = sem("a_tp")
            a_xt = sem("a_xt")
            a_pq = sem("a_pq")
            a_qk = sem("a_qk")
            a_p1 = sem("a_p1")
            a_s = sem("a_s")
            a_p = sem("a_p")
            a_p2 = sem("a_p2")
            a_v = sem("a_v")
            a_ef = sem("a_ef")
            a_efc = sem("a_efc")
            DP = 4
            SPLIT = DP * D0 * G0

            with nc.Block() as block:
                @block.sync
                def _(sp):
                    def load_x(c):
                        sp.dma_start(xs[:, 4 * c:4 * c + 4, :],
                                     ins["x"][512 * c:512 * c + 512, :].rearrange("(t p) e -> p t e", p=P)
                                     ).then_inc(x_in[c], 16)

                    load_x(0)
                    sp.dma_start(wq0[:, :, :], ins["wq0"].rearrange("(k p) n -> p k n", p=P)).then_inc(w_a, 16)
                    sp.dma_start(bq0[:, :], ins["bq0"].partition_broadcast(P)).then_inc(w_a, 16)
                    sp.dma_start(ident[:, :], ins["ident"]).then_inc(const_in, 16)
                    for j, (w, b) in enumerate((("wk0", "bk0"), ("wv0", "bv0"))):
                        cols = slice((j + 1) * I0, (j + 2) * I0)
                        sp.dma_start(w0[:, :, cols], ins[w].rearrange("(k p) n -> p k n", p=P)).then_inc(w_a, 16)
                        sp.dma_start(b0[:, cols], ins[b].partition_broadcast(P)).then_inc(w_a, 16)
                    for c in range(1, 4):
                        load_x(c)
                    sp.dma_start(expert_t[:, :, :],
                                 ins["expert_t"].rearrange("(k p) n -> p k n", p=P)).then_inc(w_e, 16)
                    sp.dma_start(fc2[:, :, :], ins["fc2"].rearrange("(k p) n -> p k n", p=P)).then_inc(w_e, 16)
                    for dst, name in ((up, "up"), (down, "down"), (fc1, "fc1"), (gate, "gate"), (w3, "w3"),
                                      (rope_c, "rope_c"), (rope_s, "rope_s")):
                        sp.dma_start(dst[:, :, :], ins[name].rearrange("(k p) n -> p k n", p=P)).then_inc(w_b, 16)
                    sp.dma_start(b3[:, :], ins["b3"].partition_broadcast(P)).then_inc(w_b, 16)
                    sp.dma_start(gamma[:, :], ins["gamma"].partition_broadcast(P)).then_inc(w_b, 16)
                    sp.dma_start(beta[:, :], ins["beta"].partition_broadcast(P)).then_inc(w_b, 16)

                @block.vector
                def _(dve):
                    ch = Chain(dve, a_v)
                    ch.link(nc.vector.memset(eps[:, :], EPS))
                    def statistics(c):
                        part = slice(4 * c, 4 * c + 4)
                        dve.wait_ge(x_in[c], 16)
                        for t in range(4 * c, 4 * c + 4):
                            i = nc.vector.bn_stats(st[:, t, :], xs[:, t, :])
                        ch.link(i)
                        finish_stats(dve, a_var, a_sd, ch, st[:, part, :], tmp[:, :, part], 4, E, c + 1, c + 1)

                    statistics(0)
                    dve.wait_ge(w_a, 16 * 6)
                    nc.vector.tensor_reduce(w0[:, :, 0:I0], wq0[:, :, :].rearrange("p k (i r) -> p k i r", r=R0),
                                            X_AXIS, ALU.add)
                    nc.vector.tensor_reduce(b0[:, 0:I0], bq0[:, :].rearrange("p (i r) -> p i r", r=R0),
                                            X_AXIS, ALU.add).then_inc(a_w0, 1)

                    def normalise(n, u):
                        nc.vector.tensor_scalar(xn[:, u, :], tile_of(xs, n), col_of(tmp, 0, n), col_of(tmp, 5, n),
                                                ALU.subtract, ALU.mult).then_inc(a_xn, 1)

                    def tile_of(a, n):
                        return a[:, bass.ds(n, 1), :].rearrange("p o e -> p (o e)")

                    def col_of(a, row, n):
                        return a[:, row, bass.ds(n, 1)]

                    def queries_keys(n, u):
                        dve.wait_ge(a_pq, n + 1)
                        nc.vector.tensor_tensor(qkv[:, u, 0:2 * I0], psum[:, 2 + u, 0:2 * I0], b0[:, 0:2 * I0],
                                                ALU.add).then_inc(a_qk, 1)

                    def values(n, u):
                        nc.vector.tensor_tensor(qkv[:, u, 2 * I0:3 * I0], psum[:, 2 + u, 2 * I0:3 * I0],
                                                b0[:, 2 * I0:3 * I0], ALU.add)

                    def weigh(n, u):
                        dve.wait_ge(a_p1, n + 1)
                        s2 = sc[:, u, :].rearrange("p (d e) -> p d e", d=D0)
                        ch.link(nc.vector.tensor_reduce(sc[:, u, :], prod[:, u, :].rearrange("p (i g) -> p i g", g=G0),
                                                        X_AXIS, ALU.add))
                        ch.link(nc.vector.tensor_reduce(mx[:, :], s2, X_AXIS, ALU.max))
                        nc.vector.tensor_tensor(s2, s2, mx[:, :].rearrange("p (d o) -> p d o", o=1)
                                                .broadcast_to([P, D0, D0]), ALU.subtract).then_inc(a_s, 1)

                    def share(n, u):
                        dve.wait_ge(a_p, n + 1)
                        p2 = pr[:, u, :].rearrange("p (d e) -> p d e", d=D0)
                        ch.mark(nc.vector.tensor_reduce(ls[:, u, :], p2, X_AXIS, ALU.add))
                        v3 = qkv[:, u, 2 * I0:3 * I0].rearrange("p (e g) -> p g e", g=G0)
                        for d in range(DP):
                            last = nc.vector.tensor_tensor(
                                prov[:, u, d * D0 * G0:(d + 1) * D0 * G0].rearrange("p (g e) -> p g e", g=G0),
                                p2[:, d:d + 1, :].broadcast_to([P, G0, D0]), v3, ALU.mult)
                        ch.need()
                        ch.link(nc.vector.reciprocal(ls[:, 2 + u, :], ls[:, u, :]))

                    def collect(n, u):
                        dve.wait_ge(a_p2, n + 1)
                        ch.link(nc.vector.tensor_reduce(av[:, :], prov[:, u, :].rearrange("p (i e) -> p i e", e=D0),
                                                        X_AXIS, ALU.add))
                        o = tile_of(mixed, n)
                        ch.mark(nc.vector.tensor_tensor(
                            o.rearrange("p (d g) -> p d g", g=G0), av[:, :].rearrange("p (d g) -> p d g", g=G0),
                            ls[:, 2 + u, :].rearrange("p (d o) -> p d o", o=1).broadcast_to([P, D0, G0]), ALU.mult))
                        ch.need_apart(passed_v)
                        nc.vector.bn_stats(tile_of(mixed_st, n), o)

                    LINKS = 6

                    def step(n, u):
                        left = TILES - n if isinstance(n, int) else TILES
                        ch.begin(head + n * LINKS)
                        if left > 1:
                            weigh(n + 1, 1 - u)
                        collect(n, u)
                        if left > 2:
                            values(n + 2, u)
                        if left > 4:
                            normalise(n + 4, u)
                        if left > 3:
                            queries_keys(n + 3, 1 - u)
                        if left > 1:
                            share(n + 1, 1 - u)
                            assert ch.k == LINKS, ch.k

                    normalise(0, 0)
                    normalise(1, 1)
                    statistics(1)
                    for n in range(2):
                        queries_keys(n, n)
                        values(n, n)
                        normalise(n + 2, n)
                    statistics(2)
                    statistics(3)
                    weigh(0, 0)
                    share(0, 0)
                    queries_keys(2, 0)
                    head = ch.k
                    with dve.Fori(0, TILES // 2 - 2) as it:
                        for u in range(2):
                            step(it * 2 + u, u)
                    for n in range(TILES - 4, TILES):
                        step(n, n % 2)

                @block.gpsimd
                def _(pool):
                    def scores(n, u):
                        pool.wait_ge(a_qk, n + 1)
                        q = qkv[:, u, 0:I0].rearrange("p (d o g) -> p d o g", d=D0, o=1).broadcast_to([P, D0, D0, G0])
                        k = qkv[:, u, I0:2 * I0].rearrange("p (o e g) -> p o e g", o=1, e=D0)\
                            .broadcast_to([P, D0, D0, G0])
                        nc.gpsimd.tensor_tensor(prod[:, u, :].rearrange("p (d e g) -> p d e g", d=D0, e=D0), q, k,
                                                ALU.mult).then_inc(a_p1, 1)

                    def context(n, u):
                        pool.wait_ge(a_p, n + 1)
                        n_d = D0 - DP
                        p = pr[:, u, DP * D0:].rearrange("p (d o e) -> p d o e", d=n_d, o=1)\
                            .broadcast_to([P, n_d, G0, D0])
                        v = qkv[:, u, 2 * I0:3 * I0].rearrange("p (o e g) -> p o g e", o=1, g=G0)\
                            .broadcast_to([P, n_d, G0, D0])
                        nc.gpsimd.tensor_tensor(prov[:, u, SPLIT:].rearrange("p (d g e) -> p d g e", d=n_d, g=G0), p, v,
                                                ALU.mult).then_inc(a_p2, 1)

                    scores(0, 0)
                    scores(1, 1)
                    with pool.Fori(0, TILES // 2 - 1) as it:
                        for u in range(2):
                            context(it * 2 + u, u)
                            scores(it * 2 + (u + 2), u)
                    context(TILES - 2, 0)
                    context(TILES - 1, 1)

                @block.scalar
                def _(act):
                    def copy_xt(n, u):
                        act.wait_ge(a_tp, n + 1)
                        nc.scalar.activation(xt[:, u, :], psum[:, u, :], ACT.Copy).then_inc(a_xt, 1)

                    def exps(n, u):
                        act.wait_ge(a_s, n + 1)
                        nc.scalar.activation(pr[:, u, :], sc[:, u, :], ACT.Exp,
                                             scale=D0 ** -0.5).then_inc(a_p, 1)

                    def norm(c):
                        root(act, a_var, a_sd, tmp[:, :, 4 * c:4 * c + 4], 4, c + 1)

                    norm(0)
                    copy_xt(0, 0)
                    copy_xt(1, 1)
                    norm(1)
                    copy_xt(2, 0)
                    copy_xt(3, 1)
                    norm(2)
                    norm(3)
                    exps(0, 0)
                    with act.Fori(0, TILES // 2 - 2) as it:
                        for u in range(2):
                            exps(it * 2 + (u + 1), 1 - u)
                            copy_xt(it * 2 + (u + 4), u)
                    for n in range(TILES - 3, TILES):
                        exps(n, n % 2)
                    act.wait_ge(a_ef, 1)
                    nc.scalar.activation(lat_out[:, :, :].rearrange("p k n -> p (k n)"),
                                         psum[:, 4:6, :].rearrange("p k n -> p (k n)"), ACT.Copy).then_inc(a_efc, 1)

                @block.tensor
                def _(pe):
                    pe.wait_ge(const_in, 16)
                    pe.wait_ge(a_w0, 1)

                    def project(n, u):
                        pe.wait_ge(a_xn, n + 1)
                        for c in range(KC):
                            last = nc.tensor.transpose(psum[:, u, c * P:(c + 1) * P], xn[:, u, c * P:(c + 1) * P],
                                                       ident[:, :])
                        last.then_inc(a_tp, 1)
                        pe.wait_ge(a_xt, n + 1)
                        for c in range(KC):
                            last = nc.tensor.matmul(psum[:, 2 + u, 0:3 * I0], xt[:, u, c * P:(c + 1) * P],
                                                    w0[:, c, :], start=(c == 0), stop=(c == KC - 1))
                        last.then_inc(a_pq, 1)

                    with pe.Fori(0, TILES // 2) as it:
                        for u in range(2):
                            project(it * 2 + u, u)
                    pe.wait_ge(w_e, 16 * 2)
                    for lc in range(LAT // P):
                        for mc in range(LAT // P):
                            last = nc.tensor.matmul(psum[:, 4 + lc, :], expert_t[:, mc, lc * P:(lc + 1) * P],
                                                    fc2[:, mc, :], start=(mc == 0), stop=(mc == LAT // P - 1))
                    last.then_inc(a_ef, 1)

        with ExitStack() as sbk:
            mtmp = sb("b_mtmp", [P, 6, TILES], stack=sbk)
            x_st = sb("b_x_st", [P, TILES, 6], stack=sbk)
            x_tmp = sb("b_x_tmp", [P, 6, TILES], stack=sbk)
            st = sb("b_st", [P, GT, 6], stack=sbk)
            tmp = sb("b_tmp", [P, 6, GT], stack=sbk)
            ln = sb("b_ln", [P, 2, I0], stack=sbk)
            rows1 = block2_in
            rows2 = sb("b_rows2", [P, GT, E], stack=sbk)
            xt1 = sb("b_xt1", [P, KC, GR], stack=sbk)
            xt2 = sb("b_xt2", [P, KC, GR], stack=sbk)
            ht = sb("b_ht", [P, INT // P, GR], stack=sbk)
            lt = sb("b_lt", [P, LAT // P, GR], stack=sbk)
            sh = sb("b_sh", [P, 2, E], stack=sbk)
            top = sb("b_top", [P, GT, 8], stack=sbk)
            rw = sb("b_rw", [P, GT], stack=sbk)
            qk = sb("b_qk", [P, 2 * E], stack=sbk)
            rot = sb("b_rot", [P, 2 * E], stack=sbk)
            rest = sb("b_rest", [P, 2 * E], stack=sbk)
            parts = sb("b_parts", [P, 3, 2 * KC, 2 * P], BF16, stack=sbk)
            v32 = sb("b_v32", [P, H, VW], stack=sbk)

            b_v = sem("b_v")
            b_mv = sem("b_mv")
            b_ms = sem("b_ms")
            b_var = sem("b_var")
            b_sd = sem("b_sd")
            b_x1 = sem("b_x1")
            b_x2 = sem("b_x2")
            b_t1 = sem("b_t1")
            b_t2 = sem("b_t2")
            b_xt1 = sem("b_xt1")
            b_xt2 = sem("b_xt2")
            b_up = sem("b_up")
            b_hr = sem("b_hr")
            b_h = sem("b_h")
            b_gate = sem("b_gate")
            b_gs = sem("b_gs")
            b_dn = sem("b_dn")
            b_sh = sem("b_sh")
            b_y = sem("b_y")
            b_qkv = sem("b_qkv")
            b_ev = sem("b_ev")
            b_vs = sem("b_vs")
            b_rot = sem("b_rot")
            b_qk = sem("b_qk")
            b_tq = sem("b_tq")
            b_p1 = sem("b_p1")
            b_r = sem("b_r")
            b_p2 = sem("b_p2")
            b_p3 = sem("b_p3")
            b_vo = sem("b_vo")
            b_qo = sem("b_qo")
            b_c = sem("b_c")
            b_q0 = sem("b_q0")
            b_ap = sem("b_ap")
            b_ac = sem("b_ac")
            early = units(range(EARLY))
            G = TILES // GT
            N_UP = INT // P
            N_U = N_UP + LAT // P
            EARLY_BANKS = (2, 3, 6)
            T_BANK, U_BANK, R_BANK, G_BANK = 0, 2, 4, 6

            def this(g):
                return lambda per, k: g * per + k

            def after(g):
                return lambda per, k: g * per + (per + k)

            with nc.Block() as block:
                @block.sync
                def _(sp):
                    def store(g):
                        for t in range(GT):
                            sp.wait_ge(b_vs, g * GT + (t + 1))
                            sp.dma_start(v_scr[bass.ds(g * GT + t, 1), :, :].rearrange("o p n -> p (o n)"),
                                         v32[:, :, :].rearrange("p h w -> p (h w)")).then_inc(b_vo, 16)
                            if t % 2 == 1:
                                sp.wait_ge(b_p2, g * GT + (t + 1))
                                sp.wait_ge(b_p3, g * GT + (t + 1))
                                row = (g // 2) * E
                                col = (g % 2) * GR + (t // 2) * 2 * P
                                for j, scr in enumerate((q_scr, k_scr)):
                                    for part in range(3):
                                        sp.dma_start(
                                            scr[part, bass.ds(row, E), bass.ds(col, 2 * P)]
                                            .rearrange("(c p) n -> p c n", p=P),
                                            parts[:, part, j * KC:(j + 1) * KC, :]).then_inc(b_qo, 16)

                    with sp.Fori(0, G // NB) as g:
                        store(g)
                    sp.wait_ge(b_t1, TILES)
                    sp.wait_ge(b_qo, TILES // 2 // NB * 6 * 16 + 16)
                    load_stacks(sp, 0, quad0_q, quad0_k, b_q0)
                    sp.wait_ge(b_dn, TILES)
                    sp.dma_start(lt[:, 0, :], ins["causal"]).then_inc(b_q0, 16)
                    with sp.Fori(0, G // NB) as g:
                        store(g + G // NB)
                    sp.wait_ge(b_qo, TILES // 2 * 6 * 16 + 16)
                    sp.wait_ge(b_vo, (TILES + 1) * 16)

                @block.vector
                def _(dve):
                    ch = Chain(dve, b_v)

                    def tile_of(a, n):
                        return a[:, bass.ds(n, 1), :].rearrange("p o e -> p (o e)")

                    def after_block1(n, t):
                        ch.link(nc.vector.tensor_scalar(ln[:, t % 2, :], tile_of(mixed, n),
                                                        mtmp[:, 0, bass.ds(n, 1)], mtmp[:, 5, bass.ds(n, 1)],
                                                        ALU.subtract, ALU.mult))
                        x3 = tile_of(xs, n).rearrange("p (i r) -> p i r", r=R0)
                        ch.mark(nc.vector.tensor_tensor(
                            x3, x3, ln[:, t % 2, :].rearrange("p (i o) -> p i o", o=1).broadcast_to([P, I0, R0]),
                            ALU.add))
                        ch.need_apart(passed_v)
                        return nc.vector.bn_stats(tile_of(x_st, n), tile_of(xs, n))

                    def input2(c):
                        for t in range(GT):
                            n = c(GT, t)
                            nc.vector.tensor_scalar(rows1[:, t, :], tile_of(xs, n), x_tmp[:, 0, bass.ds(n, 1)],
                                                    x_tmp[:, 5, bass.ds(n, 1)], ALU.subtract,
                                                    ALU.mult).then_inc(b_x1, 1)

                    def gate_sums(c):
                        wait_apart(dve, b_gate, c(1, 1), passed_v)
                        for t in range(GT):
                            last = nc.vector.max(top[:, t, :], psum[:, G_BANK, t * NE:(t + 1) * NE])
                        last.then_inc(b_gs, 1)
                        dve.wait_ge(b_gs, c(1, 1))
                        ch.link(nc.vector.tensor_tensor(rw[:, :], top[:, :, 0], top[:, :, 1], ALU.add))

                    def output2(c, t):
                        dve.wait_ge(b_sh, c(GT, t + 1))
                        nc.vector.scalar_tensor_tensor(
                            out=rows2[:, t, :], in0=psum[:, R_BANK + t % 2, :], scalar=rw[:, t:t + 1],
                            in1=sh[:, t % 2, :], op0=ALU.mult, op1=ALU.add).then_inc(b_y, 1)
                        dve.wait_ge(b_y, c(GT, t + 1))
                        return nc.vector.bn_stats(st[:, t, :], rows2[:, t, :])

                    def scaled(dst, src, t):
                        return nc.vector.tensor_scalar(dst, src, tmp[:, 0, t:t + 1], tmp[:, 5, t:t + 1],
                                                       ALU.subtract, ALU.mult)

                    def finish(c, k):
                        finish_stats(dve, b_var, b_sd, ch, st, tmp, GT, E, None, c(3, k + 3))

                    def own_norm(c):
                        finish(c, 0)
                        for t in range(GT):
                            last = scaled(rows2[:, t, :], rows2[:, t, :], t)
                        ch.link(last)
                        for t in range(GT):
                            last = nc.vector.tensor_tensor(rows2[:, t, :], rows2[:, t, :], gamma[:, :], ALU.mult)
                        ch.link(last)

                    def own_beta(c):
                        for t in range(GT):
                            last = nc.vector.tensor_tensor(rows2[:, t, :], rows2[:, t, :], beta[:, :], ALU.add)
                        ch.link(last)
                        for t in range(GT):
                            last = nc.vector.bn_stats(st[:, t, :], rows2[:, t, :])
                        ch.link(last)
                        finish(c, 1)

                    def add_block2(c):
                        for t in range(GT):
                            last = scaled(rows2[:, t, :], rows2[:, t, :], t)
                        ch.link(last)
                        for t in range(GT):
                            x = tile_of(xs, c(GT, t))
                            last = nc.vector.tensor_tensor(x, x, rows2[:, t, :], ALU.add)
                        ch.mark(last)
                        ch.need_apart(passed_v)
                        for t in range(GT):
                            last = nc.vector.bn_stats(st[:, t, :], tile_of(xs, c(GT, t)))
                        ch.link(last)

                    def input3(c):
                        finish(c, 2)
                        for t in range(GT):
                            scaled(rows2[:, t, :], tile_of(xs, c(GT, t)), t).then_inc(b_x2, 1)

                    def evacuate(c, t):
                        qk_bank = (U_BANK, R_BANK)[t % 2]
                        dve.wait_ge(b_qkv, c(GT, t + 1))
                        dve.wait_ge(b_tq, c(GT, t + 1))
                        nc.vector.tensor_tensor(qk[:, :].rearrange("p (j n) -> p j n", j=2),
                                                psum[:, qk_bank:qk_bank + 2, :],
                                                b3[:, 0:2 * E].rearrange("p (j n) -> p j n", j=2),
                                                ALU.add).then_inc(b_ev, 1)
                        dve.wait_ge(b_vo, c(GT * 16, (t + 1) * 16))
                        if t == 0:
                            dve.wait_ge(b_c, 2)
                        nc.vector.tensor_tensor(v32[:, :, 0:HD],
                                                psum[:, G_BANK + t % 2, :].rearrange("p (h w) -> p h w", w=HD),
                                                b3[:, 2 * E:3 * E].rearrange("p (h w) -> p h w", w=HD),
                                                ALU.add).then_inc(b_vs, 1)

                    def rotate(g, c, t):
                        dve.wait_ge(b_rot, c(GT, t + 1))
                        q3 = qk[:, :].rearrange("p (h w) -> p h w", w=HD)
                        cos = rope_c[:, bass.ds((g % 2) * GT + t, 1), :].broadcast_to([P, 2 * H, HD])
                        ch.link(nc.vector.tensor_tensor(q3, q3, cos, ALU.mult))
                        nc.vector.tensor_tensor(qk[:, :], qk[:, :], rot[:, :], ALU.add).then_inc(b_qk, 1)

                    def split(c, t):
                        dve.wait_ge(b_p1, c(GT, t + 1))
                        half = slice((t % 2) * P, (t % 2 + 1) * P)
                        pt = psum[:, T_BANK:T_BANK + 2, :].rearrange("p b (c n) -> p (b c) n", n=P)
                        r3 = rest[:, :].rearrange("p (c n) -> p c n", n=P)
                        nc.vector.tensor_tensor(r3, pt, parts[:, 0, :, half], ALU.subtract).then_inc(b_r, 1)
                        dve.wait_ge(b_p2, c(GT, t + 1))
                        nc.vector.tensor_tensor(parts[:, 2, :, half], r3, parts[:, 1, :, half],
                                                ALU.subtract).then_inc(b_p3, 1)

                    dve.sem_inc(b_vo, 16)
                    dve.sem_inc(b_tq, 1)
                    ch.link(nc.vector.memset(row_mx[:, :, 1, :], -3.4e38))
                    dve.wait_ge(w_b, W_B)
                    finish_stats(dve, b_mv, b_ms, ch, mixed_st, mtmp, TILES, I0, 1, 1)
                    for t in range(GT):
                        last = after_block1(t, t)
                    ch.link(last)
                    finish_stats(dve, b_var, b_sd, ch, x_st, x_tmp, GT, E, None, 1)
                    input2(this(0))
                    head = ch.k
                    with dve.Fori(0, G - 1) as g:
                        ch.begin(g * (2 * GT + 1) + head)
                        for t in range(GT):
                            last = after_block1(g * GT + (GT + t), t)
                        ch.link(last)
                    ch.begin((G - 1) * (2 * GT + 1) + head)
                    finish_stats(dve, b_var, b_sd, ch, x_st[:, GT:TILES, :], x_tmp[:, :, GT:TILES], TILES - GT, E,
                                 None, 2)
                    gate_sums(this(0))
                    for t in range(GT - 1):
                        output2(this(0), t)
                    head = ch.base + ch.k

                    with dve.Fori(0, G - 2) as g:
                        mine, nxt = this(g), after(g)
                        ch.begin(g * CHAIN_B + head)
                        input2(nxt)
                        ch.link(output2(mine, GT - 1))
                        for part in (own_norm, own_beta, add_block2, input3):
                            part(mine)
                        gate_sums(nxt)
                        for t in range(GT):
                            evacuate(mine, t)
                            if t:
                                split(mine, t - 1)
                            rotate(g, mine, t)
                        output2(nxt, 0)
                        split(mine, GT - 1)
                        for t in range(1, GT - 1):
                            output2(nxt, t)
                        assert ch.k == CHAIN_B, ch.k
                    ch.begin((G - 2) * CHAIN_B + head)
                    mine, nxt = this(G - 2), this(G - 1)
                    input2(nxt)
                    ch.link(output2(mine, GT - 1))
                    for part in (own_norm, own_beta, add_block2, input3):
                        part(mine)
                    gate_sums(nxt)
                    for t in range(GT):
                        last = output2(nxt, t)
                    ch.link(last)
                    own_norm(nxt)
                    own_beta(nxt)
                    for t in range(GT):
                        evacuate(mine, t)
                        if t:
                            split(mine, t - 1)
                        rotate(G - 2, mine, t)
                        if t < 2:
                            (add_block2, input3)[t](nxt)

                    def maxima(lo, hi):
                        for e in range(lo, hi):
                            wait_apart(dve, b_ap, e + 1, passed_v)
                            unit_max(psum[:, EARLY_BANKS[e % 3], :], early[e], 0, lt[:, 0, :],
                                     sh[:, :, :].rearrange("p a b -> p (a b)").bitcast(BF16)
                                     .rearrange("p (a b) -> p a b", b=512)[:, e % 3, :]).then_inc(b_ac, 1)

                    for t in range(GT):
                        evacuate(nxt, t)
                        split(*((nxt, t - 1) if t else (mine, GT - 1)))
                        if t == GT - 1:
                            dve.wait_ge(b_q0, 13 * 16)
                            maxima(0, 3)
                        rotate(G - 1, nxt, t)
                    maxima(3, 8)
                    split(nxt, GT - 1)
                    maxima(8, len(early))

                @block.gpsimd
                def _(pool):
                    def square(c):
                        for j in range(N_UP):
                            pool.wait_ge(b_hr, c(N_U, j + 1))
                            nc.gpsimd.tensor_tensor(ht[:, j, :], ht[:, j, :], ht[:, j, :],
                                                    ALU.mult).then_inc(b_h, 1)

                    def swapped(g, c):
                        for t in range(GT):
                            pool.wait_ge(b_ev, c(GT, t + 1))
                            q4 = qk[:, :].rearrange("p (h j w) -> p h j w", j=2, w=HALF)
                            r4 = rot[:, :].rearrange("p (h j w) -> p h j w", j=2, w=HALF)
                            s = rope_s[:, bass.ds((g % 2) * GT + t, 1), :]
                            nc.gpsimd.tensor_tensor(r4[:, :, 0, :], q4[:, :, 1, :],
                                                    s[:, :, 0:HALF].broadcast_to([P, 2 * H, HALF]), ALU.mult)
                            nc.gpsimd.tensor_tensor(r4[:, :, 1, :], q4[:, :, 0, :],
                                                    s[:, :, HALF:HD].broadcast_to([P, 2 * H, HALF]),
                                                    ALU.mult).then_inc(b_rot, 1)

                    nc.gpsimd.memset(v32[:, :, HD:VW], 0.0).then_inc(b_c, 1)
                    pool.wait_ge(b_c, 1)
                    nc.gpsimd.memset(v32[:, :, HD:HD + 1], 1.0).then_inc(b_c, 1)
                    square(this(0))
                    with pool.Fori(0, G - 1) as g:
                        square(after(g))
                        swapped(g, this(g))
                    swapped(G - 1, this(G - 1))

                @block.scalar
                def _(act):
                    def copy_input2(c):
                        for t in range(GT):
                            act.wait_ge(b_t1, c(GT, t + 1))
                            nc.scalar.activation(xt1[:, :, t * P:(t + 1) * P],
                                                 psum[:, T_BANK + t % 2, :].rearrange("p (c n) -> p c n", n=P),
                                                 ACT.Copy).then_inc(b_xt1, 1)

                    def copy_input3(c, tiles, dst=xt2):
                        for t in tiles:
                            act.wait_ge(b_t2, c(GT, t + 1))
                            nc.scalar.activation(dst[:, :, t * P:(t + 1) * P],
                                                 psum[:, T_BANK + t % 2, :].rearrange("p (c n) -> p c n", n=P),
                                                 ACT.Copy).then_inc(b_xt2, 1)

                    def read_up(c, js):
                        for j in js:
                            act.wait_ge(b_up, c(N_U, j + 1))
                            if j < N_UP:
                                nc.scalar.activation(ht[:, j, :], psum[:, U_BANK + j % 2, :],
                                                     ACT.Relu).then_inc(b_hr, 1)
                            else:
                                nc.scalar.activation(lt[:, j - N_UP, :], psum[:, U_BANK + j % 2, :],
                                                     ACT.Copy).then_inc(b_hr, 1)

                    def read_shared(c, t, again=True):
                        act.wait_ge(b_dn, c(GT, t + 1))
                        if again or t >= 2:
                            act.wait_ge(b_y, c(GT, t - 1))
                        nc.scalar.activation(sh[:, t % 2, :], psum[:, U_BANK + t % 2, :], ACT.Copy).then_inc(b_sh, 1)

                    def two_parts(c, t):
                        half = slice((t % 2) * P, (t % 2 + 1) * P)
                        act.wait_ge(b_tq, c(GT, t + 2))
                        if t % 2 == 0:
                            act.wait_ge(b_qo, c(GT * 3 * 16, t * 3 * 16 + 16))
                        nc.scalar.activation(parts[:, 0, :, half],
                                             psum[:, T_BANK:T_BANK + 2, :].rearrange("p b (c n) -> p (b c) n", n=P),
                                             ACT.Copy).then_inc(b_p1, 1)
                        act.wait_ge(b_r, c(GT, t + 1))
                        nc.scalar.activation(parts[:, 1, :, half], rest[:, :].rearrange("p (c n) -> p c n", n=P),
                                             ACT.Copy).then_inc(b_p2, 1)

                    act.sem_inc(b_qo, 16)
                    root(act, b_mv, b_ms, mtmp, TILES, 1)
                    root(act, b_var, b_sd, x_tmp, GT, 1)
                    copy_input2(this(0))
                    read_up(this(0), range(0, 7))
                    root(act, b_var, b_sd, x_tmp[:, :, GT:TILES], TILES - GT, 2)
                    read_up(this(0), range(7, N_U))
                    for t in range(GT):
                        read_shared(this(0), t, again=False)

                    def up_beside_norms(mine, nxt):
                        copy_input2(nxt)
                        root(act, b_var, b_sd, tmp, GT, mine(3, 3))
                        read_up(nxt, range(0, 3))
                        root(act, b_var, b_sd, tmp, GT, mine(3, 4))
                        read_up(nxt, range(3, 5))
                        root(act, b_var, b_sd, tmp, GT, mine(3, 5))
                        read_up(nxt, range(5, 7))
                        copy_input3(mine, range(0, 2))
                        read_up(nxt, range(7, 8))
                        copy_input3(mine, range(2, GT))
                        read_up(nxt, range(8, N_U))

                    with act.Fori(0, G - 2) as g:
                        mine, nxt = this(g), after(g)
                        up_beside_norms(mine, nxt)
                        for t in range(GT - 1):
                            two_parts(mine, t)
                        read_shared(nxt, 0)
                        two_parts(mine, GT - 1)
                        for t in range(1, GT):
                            read_shared(nxt, t)
                    mine, nxt = this(G - 2), this(G - 1)
                    up_beside_norms(mine, nxt)
                    for t in range(GT):
                        read_shared(nxt, t)
                    root(act, b_var, b_sd, tmp, GT, nxt(3, 3))
                    root(act, b_var, b_sd, tmp, GT, nxt(3, 4))
                    two_parts(mine, 0)
                    root(act, b_var, b_sd, tmp, GT, nxt(3, 5))
                    two_parts(mine, 1)
                    copy_input3(nxt, range(GT), xt1)
                    for t in range(2, GT):
                        two_parts(mine, t)
                    for t in range(GT):
                        two_parts(nxt, t)

                @block.tensor
                def _(pe):
                    def turn(src, t, done):
                        for c in range(KC):
                            last = nc.tensor.transpose(psum[:, T_BANK + t % 2, c * P:(c + 1) * P],
                                                       src[:, t, c * P:(c + 1) * P], ident[:, :])
                        last.then_inc(done, 1)

                    def turn_input2(c):
                        for t in range(GT):
                            pe.wait_ge(b_x1, c(GT, t + 1))
                            if t >= 2:
                                pe.wait_ge(b_xt1, c(GT, t - 1))
                            turn(rows1, t, b_t1)

                    def turn_input3(c, tiles):
                        for t in tiles:
                            pe.wait_ge(b_x2, c(GT, t + 1))
                            if t >= 2:
                                pe.wait_ge(b_xt2, c(GT, t - 1))
                            turn(rows2, t, b_t2)

                    def up_and_fc1(c, js, before=None):
                        for j in js:
                            if j >= 2:
                                pe.wait_ge(b_hr, c(N_U, j - 1))
                            elif before is not None:
                                pe.wait_ge(b_sh, before(GT, j + 3))
                            w = up[:, :, j * P:(j + 1) * P] if j < N_UP else fc1[:, :, (j - N_UP) * P:(j - N_UP + 1) * P]
                            for k in range(KC):
                                last = nc.tensor.matmul(psum[:, U_BANK + j % 2, :], w[:, k, :], xt1[:, k, :],
                                                        start=(k == 0), stop=(k == KC - 1))
                            last.then_inc(b_up, 1)

                    def gate_logits():
                        for t in range(GT):
                            for k in range(KC):
                                last = nc.tensor.matmul(psum[:, G_BANK, t * NE:(t + 1) * NE],
                                                        xt1[:, k, t * P:(t + 1) * P], gate[:, k, :],
                                                        start=(k == 0), stop=(k == KC - 1))
                        last.then_inc(b_gate, 1)

                    def shared(t):
                        for k in range(N_UP):
                            nc.tensor.matmul(psum[:, U_BANK + t % 2, :], ht[:, k, t * P:(t + 1) * P], down[:, k, :],
                                             start=(k == 0), stop=(k == N_UP - 1))

                    def routed(t):
                        for k in range(LAT // P):
                            last = nc.tensor.matmul(psum[:, R_BANK + t % 2, :], lt[:, k, t * P:(t + 1) * P],
                                                    lat_out[:, k, :], start=(k == 0), stop=(k == LAT // P - 1))
                        last.then_inc(b_dn, 1)

                    def qkv(c, t, xt=xt2, again=False):
                        if t >= 2 or again:
                            pe.wait_ge(b_ev, c(GT, t - 1))
                            pe.wait_ge(b_vs, c(GT, t - 1))
                        elif t == 1:
                            pe.wait_ge(b_y, c(GT, GT))
                        for j in range(3):
                            bank = (U_BANK, R_BANK)[t % 2] + j if j < 2 else G_BANK + t % 2
                            for k in range(KC):
                                last = nc.tensor.matmul(psum[:, bank, :], xt[:, k, t * P:(t + 1) * P],
                                                        w3[:, k, j * E:(j + 1) * E],
                                                        start=(k == 0), stop=(k == KC - 1))
                        last.then_inc(b_qkv, 1)

                    def turn_qk(c, t, again=False):
                        pe.wait_ge(b_qk, c(GT, t + 1))
                        if t or again:
                            pe.wait_ge(b_r, c(GT, t))
                        for k in range(2 * KC):
                            last = nc.tensor.transpose(psum[:, T_BANK + k // KC, (k % KC) * P:(k % KC + 1) * P],
                                                       qk[:, k * P:(k + 1) * P], ident[:, :])
                        last.then_inc(b_tq, 1)

                    pe.wait_ge(w_b, W_B)
                    turn_input2(this(0))
                    pe.wait_ge(b_xt1, GT)
                    up_and_fc1(this(0), range(N_U))
                    gate_logits()
                    pe.wait_ge(b_hr, N_U)
                    pe.wait_ge(b_h, N_UP)
                    for t in range(GT):
                        if t >= 2:
                            pe.wait_ge(b_y, t - 1)
                        shared(t)
                        routed(t)

                    def up_beside_norms(mine, nxt):
                        turn_input2(nxt)
                        pe.wait_ge(b_xt1, nxt(GT, GT))
                        up_and_fc1(nxt, range(0, 7), mine)
                        turn_input3(mine, range(0, 2))
                        up_and_fc1(nxt, range(7, 8))
                        turn_input3(mine, range(2, GT))
                        up_and_fc1(nxt, range(8, N_U))
                        gate_logits()
                        pe.wait_ge(b_xt2, mine(GT, GT))
                        pe.wait_ge(b_hr, nxt(N_U, N_U))

                    with pe.Fori(0, G - 2) as g:
                        mine, nxt = this(g), after(g)
                        up_beside_norms(mine, nxt)
                        pe.wait_ge(b_gs, nxt(1, 1))
                        for t in range(GT):
                            qkv(mine, t)
                            if t:
                                turn_qk(mine, t - 1)
                        pe.wait_ge(b_h, nxt(N_UP, N_UP))
                        pe.wait_ge(b_ev, mine(GT, GT - 1))
                        shared(0)
                        pe.wait_ge(b_ev, mine(GT, GT))
                        pe.wait_ge(b_vs, mine(GT, GT))
                        routed(0)
                        turn_qk(mine, GT - 1)
                        for t in range(1, GT):
                            if t >= 2:
                                pe.wait_ge(b_y, nxt(GT, t - 1))
                            shared(t)
                            routed(t)
                        pe.wait_ge(b_r, mine(GT, GT))
                    mine, nxt = this(G - 2), this(G - 1)
                    up_beside_norms(mine, nxt)
                    pe.wait_ge(b_h, nxt(N_UP, N_UP))
                    pe.wait_ge(b_y, mine(GT, GT))
                    for t in range(GT):
                        if t >= 2:
                            pe.wait_ge(b_y, nxt(GT, t - 1))
                        shared(t)
                        routed(t)
                    pe.wait_ge(b_gs, nxt(1, 1))
                    pe.wait_ge(b_sh, nxt(GT, GT))
                    for t in range(GT):
                        if t == 1:
                            pe.wait_ge(b_y, nxt(GT, GT))
                        qkv(mine, t)
                        if t in (1, 2):
                            turn_qk(mine, t - 1)
                    pe.wait_ge(b_r, mine(GT, 2))
                    turn_input3(nxt, range(GT))
                    pe.wait_ge(b_xt2, nxt(GT, GT))
                    turn_qk(mine, 2)
                    for t in range(GT):
                        qkv(nxt, t, xt1, again=True)
                        if t:
                            turn_qk(nxt, t - 1, again=True)
                        else:
                            turn_qk(mine, GT - 1)

                    def scores(lo, hi):
                        for e in range(lo, hi):
                            if e >= 3:
                                pe.wait_ge(b_ac, e - 2)
                            unit_scores(psum[:, EARLY_BANKS[e % 3], :], quad0_q, quad0_k, early[e]).then_inc(b_ap, 1)

                    pe.wait_ge(b_q0, 13 * 16)
                    pe.wait_ge(b_ev, nxt(GT, GT - 1))
                    pe.wait_ge(b_vs, nxt(GT, GT - 1))
                    scores(0, 6)
                    turn_qk(nxt, GT - 1)
                    scores(6, len(early))
        b_stack.close()

        wo = sb("wo", [P, KC, E])
        bo = sb("bo", [P, E])
        w4 = sb("w4", [P, KC, E])
        b4 = sb("b4", [P, E])
        lora_a = sb("lora_a", [P, E])
        lora_b = sb("lora_b", [P, E])
        route_w = sb("route_w", [P, KC, NEX])
        route_b = sb("route_b", [P, NEX])
        own = sb("own", [P, NEX])
        counted = sb("counted", [P, 3, 8])
        ctx = sb("ctx", [P, QUADS // 2, BT, P])
        w_d = sem("w_d")
        W_D = 16 * 10

        batches = [(0, 0), (1, 0), (0, 1), (1, 1), (0, 2), (0, 3), (1, 2), (1, 4), (1, 5), (1, 6), (1, 7), (1, 3)]
        NBATCH = len(batches)
        HALF0 = batches.index((0, 3))
        PIECES = NBATCH * QH
        DIAG = BT * QH

        def span(half, j):
            q0 = max(half * 512, j * P)
            return q0, half * 512 + 512 - q0

        LATE = len(units(range(EARLY, QH)))
        FIRST = LATE + 1 + len(units(range(1)))
        RING = len(units(range(QH))) + 3
        SLOTS = 3
        assert RING % SLOTS == 0

        def schedule(ahead, beyond, behind=True):
            feed = []
            if ahead:
                feed = [("unit", u) for u in units(range(1, QH))] + [("join", 0)]
                more = [("next", u) for u in units(range(1))] if beyond else []
                feed += more[:3] + [("peak", 0)] + more[3:]

            def on_vector(item):
                return 100 + item[1][3] - item[1][2] if item[1] else 100

            def on_scalar(m):
                return span(*batches[m])[1] + 100

            total, fed, done = sum(on_vector(f) for f in feed), 0, 0
            pace = 1.0 if beyond else 1.2
            pieces = sum(QH * on_scalar(m) for m in range(NBATCH))
            for m in range(NBATCH):
                for h in range(QH):
                    yield "piece", m * QH + h
                    done += on_scalar(m)
                    while feed and fed * pieces <= done * total * pace:
                        fed += on_vector(feed[0])
                        yield feed.pop(0)
                if m == 0 and behind:
                    yield "last pv", NBATCH - 1
                if m == 2 and behind:
                    yield "last turn", 1
                if m:
                    yield "pv", m - 1
                if m == HALF0 + 3:
                    yield "turn", 0
            yield from feed

        def before_step(n, behind):
            shorter = len(units(range(1))) if isinstance(n, int) and n == QUADS - 1 else 0
            return n * RING + (FIRST - behind - shorter)

        with ExitStack() as sc_:
            qs = [quad0_q] + [sb(f"qs{u}", [P, QH * BT, P], BF16, stack=sc_)[:, :, :] for u in range(1, 4)]
            ks = [quad0_k] + [sb(f"ks{u}", [P, QH, S], BF16, stack=sc_)[:, :, :] for u in range(1, 4)]
            vs = sb("vs", [P, 4, BT, QH * VW], stack=sc_)
            pt = sb("c_pt", [P, 2 * QH, 512], stack=sc_)
            junk = sb("c_junk", [P, 3, 512], BF16, stack=sc_)
            causal = sb("c_causal", [P, 512], stack=sc_)
            peak_in = sb("c_peak_in", [P, QH * BT], stack=sc_)
            mp = sb("c_mp", [QH * BT, 3, P], BF16, stack=sc_)
            mr = sb("c_mr", [QH * BT, P], stack=sc_)
            ot = sb("c_ot", [P, S], stack=sc_)
            rec = sb("c_rec", [P, 2, BT // 2 * QH], stack=sc_)

            c_in = sem("c_in")
            c_ld = [sem(f"c_ld{u}") for u in range(4)]
            c_one = sem("c_one")
            c_ap = sem("c_ap")
            c_ac = sem("c_ac")
            c_mp = sem("c_mp")
            c_mrow = sem("c_mrow")
            c_j = sem("c_j")
            c_v = sem("c_v")
            c_sb = sem("c_sb")
            c_ex = sem("c_ex")
            c_af = sem("c_af")
            c_o = sem("c_o")
            c_oe = sem("c_oe")
            LOADS = 2 * COPIES + 1

            with nc.Block() as block:
                @block.sync
                def _(sp):
                    def load_values(n, u):
                        sp.dma_start(vs[:, u, :, :],
                                     v_scr[bass.ds((n // BQ) * BT, BT), :, bass.ds((n % BQ) * QH * VW, QH * VW)]
                                     .rearrange("t p n -> p t n")).then_inc(c_ld[u], 16)

                    def load(n, u):
                        load_stacks(sp, n, qs[u], ks[u], c_ld[u])
                        load_values(n, u)

                    sp.dma_start(causal[:, :], ins["causal"]).then_inc(c_in, 16)
                    sp.sem_inc(c_ld[0], 2 * COPIES * 16)

                    def peaks(n, u):
                        sp.wait_ge(c_mp, n + 1)
                        for j in range(3):
                            sp.dma_start(qs[u][KR + j:KR + j + 1, :, :],
                                         mp[:, j, :]).then_inc(c_mrow, 16)

                    load(1, 1)
                    load_values(0, 0)
                    peaks(0, 0)
                    for u in range(2, 4):
                        load(u, u)
                    for dst, name in ((wo, "wo"), (w4, "w4"), (route_w, "route_w")):
                        sp.dma_start(dst[:, :, :], ins[name].rearrange("(k p) n -> p k n", p=P)).then_inc(w_d, 16)
                    for dst, name in ((bo, "bo"), (b4, "b4"), (route_b, "route_b")):
                        sp.dma_start(dst[:, :], ins[name].partition_broadcast(P)).then_inc(w_d, 16)
                    for dst, name in ((lora_a, "lora_a"), (lora_b, "lora_b"), (own, "own")):
                        sp.dma_start(dst[:, :], ins[name]).then_inc(w_d, 16)
                    sp.dma_start(counted[:, :, :], ins["counted"].rearrange("p (a n) -> p a n", a=3)).then_inc(w_d, 16)
                    with sp.Fori(0, QUADS // 4 - 1) as it:
                        for u in range(4):
                            n = it * 4 + u
                            peaks(n + 1, (u + 1) % 4)
                            sp.wait_ge(c_o, n * 2 + 2)
                            load(n + 4, u)
                    for u in range(3):
                        peaks(QUADS - 4 + u + 1, u + 1)
                    sp.wait_ge(c_mrow, QUADS * 48)

                @block.gpsimd
                def _(pool):
                    for u in range(4):
                        nc.gpsimd.memset(ks[u][KR:KM, :, :], 1.0).then_inc(c_one, 1)

                    def mask(n, u):
                        d = 0
                        for m, (half, j) in enumerate(batches):
                            if span(half, j)[0] != j * P:
                                continue
                            for h in range(QH):
                                p = m * QH + h
                                wait_apart(pool, c_ex, n * PIECES + (p + 1), passed_p)
                                blk = pt[:, p % (2 * QH), 0:P]
                                nc.gpsimd.affine_select(out=blk, in_=blk, compare_op=ALU.is_ge, fill=0.0, base=0,
                                                        pattern=[[1, P]], channel_multiplier=-1).then_inc(c_af, 1)
                                d += 1
                        assert d == DIAG

                    with pool.Fori(0, QUADS) as n:
                        mask(n, 0)

                @block.scalar
                def _(act):
                    def contexts(n, half):
                        act.wait_ge(c_o, n * 2 + (half + 1))
                        nc.scalar.activation(ot[:, half * 512:(half + 1) * 512], psum[:, 6 + half, :],
                                             ACT.Copy).then_inc(c_oe, 1)

                    def step(n, last=None):
                        for m, (half, j) in enumerate(batches):
                            w = span(half, j)[1]
                            for h in range(QH):
                                p = m * QH + h
                                act.wait_ge(c_sb, n * PIECES + (p + 1))
                                nc.scalar.activation(pt[:, p % (2 * QH), 0:w], psum[:, SLOTS + p % 3, 0:w], ACT.Exp,
                                                     scale=SCALE3).then_inc(c_ex, 1)
                            if m == 1 and last is not None:
                                contexts(last, 1)
                            if m == HALF0 + 2:
                                contexts(n, 0)

                    step(0)
                    with act.Fori(0, QUADS - 1) as n:
                        step(n + 1, n)
                    contexts(QUADS - 1, 1)

                @block.vector
                def _(dve):
                    ch = Chain(dve, c_v)
                    dve.wait_ge(c_in, 16)

                    def slot_max(unit, slot, par, used):
                        wait_apart(dve, c_ap, used + 1, passed_v)
                        unit_max(psum[:, slot, :], unit, par, causal, junk[:, slot, :]).then_inc(c_ac, 1)

                    def join(n, par, used):
                        dve.wait_ge(c_ac, used)
                        nc.vector.tensor_tensor(peak_in[:, :], row_mx[:, par, 0, :], row_mx[:, par, 1, :],
                                                ALU.max).then_inc(c_j, 1)

                    def peak_parts(slot, used):
                        dve.wait_ge(c_ap, used + 1)
                        t = psum[0:QH * BT, slot, 0:P]
                        ch.link(nc.vector.tensor_scalar(mp[:, 0, :], t, -1.0, None, ALU.mult))
                        nc.vector.scalar_tensor_tensor(out=mr[:, :], in0=t, scalar=-1.0, in1=mp[:, 0, :],
                                                       op0=ALU.mult, op1=ALU.subtract).then_inc(c_ac, 1)
                        dve.wait_ge(c_ac, used + 1)
                        ch.link(nc.vector.tensor_copy(mp[:, 1, :], mr[:, :]))
                        nc.vector.tensor_tensor(mp[:, 2, :], mr[:, :], mp[:, 1, :], ALU.subtract).then_inc(c_mp, 1)

                    def context(pair, i, half, slot, used):
                        dve.wait_ge(c_ap, used + 1)
                        c4 = psum[:, slot, :].rearrange("p (t h w) -> p t h w", h=QH, w=VW)
                        r4 = rec[:, half, :].rearrange("p (t h o) -> p t h o", h=QH, o=1)
                        ch.link(nc.vector.reciprocal(r4, c4[:, :, :, HD:HD + 1]))
                        o = ctx[:, bass.ds(pair, 1), half * 4:half * 4 + 4, i * QH * HD:(i + 1) * QH * HD]\
                            .rearrange("p o t (h d) -> p (o t) h d", d=HD)
                        nc.vector.tensor_tensor(o, c4[:, :, :, 0:HD], r4.broadcast_to([P, 4, QH, HD]),
                                                ALU.mult).then_inc(c_ac, 1)

                    def step(n, u, pair, pair_last, ahead=True, beyond=True):
                        behind = pair_last is not None
                        ch.begin(n * CHN + (CH0 - behind))
                        k = 0
                        for what, a in schedule(ahead, beyond, behind):
                            slot = (FIRST - behind + k) % SLOTS
                            used = before_step(n, behind) + k
                            if what == "unit":
                                slot_max(a, slot, (u + 1) % 2, used)
                            elif what == "next":
                                slot_max(a, slot, u % 2, used)
                            elif what == "peak":
                                peak_parts(slot, used)
                            elif what == "turn":
                                context(pair, u % 2, a, slot, used)
                            elif what == "last turn":
                                context(pair_last, (u - 1) % 2, a, slot, used)
                            else:
                                if what == "join":
                                    join(n, (u + 1) % 2, used)
                                continue
                            k += 1

                    CH0, CHN = 2, 4
                    for k, unit in enumerate(units(range(EARLY, QH))):
                        slot_max(unit, k % SLOTS, 0, k)
                    join(0, 0, LATE)
                    peak_parts(LATE % SLOTS, LATE)
                    for k, unit in enumerate(units(range(1))):
                        slot_max(unit, (LATE + 1 + k) % SLOTS, 1, LATE + 1 + k)
                    step(0, 0, 0, None)
                    with dve.Fori(0, QUADS // 4 - 1) as it:
                        for u in range(1, 5):
                            step(it * 4 + u, u % 4, it * 2 + u // 2, it * 2 + (u - 1) // 2)
                    for n in range(QUADS - 3, QUADS):
                        step(n, n % 4, n // 2, (n - 1) // 2, n < QUADS - 1, n < QUADS - 2)
                    used = before_step(QUADS - 1, True) + 2
                    context(QUADS // 2 - 1, 1, 1, used % SLOTS, used)

                @block.tensor
                def _(pe):
                    def score_unit(unit, slot, u, used):
                        if not isinstance(used, int) or used >= SLOTS:
                            pe.wait_ge(c_ac, used - (SLOTS - 1))
                        unit_scores(psum[:, slot, :], qs[u], ks[u], unit).then_inc(c_ap, 1)

                    def peak(n, slot, used):
                        pe.wait_ge(c_ac, used - (SLOTS - 1))
                        pe.wait_ge(c_j, n + 1)
                        nc.tensor.transpose(psum[0:QH * BT, slot, 0:P], peak_in[:, :], ident[:, :]).then_inc(c_ap, 1)

                    def turn(n, half, slot, used):
                        pe.wait_ge(c_ac, used - (SLOTS - 1))
                        pe.wait_ge(c_oe, n * 2 + (half + 1))
                        for t in range(4):
                            at_ = (half * 4 + t) * P
                            last = nc.tensor.transpose(psum[:, slot, t * P:(t + 1) * P], ot[:, at_:at_ + P], ident[:, :])
                        last.then_inc(c_ap, 1)

                    def piece(n, p, u, behind):
                        m, h = divmod(p, QH)
                        half, j = batches[m]
                        q0, w = span(half, j)
                        if p >= 3 or behind:
                            pe.wait_ge(c_ex, n * PIECES + (p - 2))
                        nc.tensor.matmul(psum[:, SLOTS + p % 3, 0:w], ks[u][0:KM, h, j * P:(j + 1) * P],
                                         qs[u][0:KM, h * BT + q0 // P:h * BT + (q0 + w) // P, :].rearrange("p a b -> p (a b)"), start=True, stop=True).then_inc(c_sb, 1)

                    diags = [m for m, (half, j) in enumerate(batches) if span(half, j)[0] == j * P]

                    def values(n, m, u):
                        half, j = batches[m]
                        q0, w = span(half, j)
                        pe.wait_ge(c_ex, n * PIECES + (m + 1) * QH)
                        if m in diags:
                            pe.wait_ge(c_af, n * DIAG + (diags.index(m) + 1) * QH)
                        mine = [b for b in batches if b[0] == half]
                        for h in range(QH):
                            last = nc.tensor.matmul(psum[h * VW:(h + 1) * VW, 6 + half, q0 - half * 512:q0 - half * 512 + w],
                                                    vs[:, u, j, h * VW:(h + 1) * VW], pt[:, (m * QH + h) % (2 * QH), 0:w],
                                                    start=(batches[m] == mine[0]), stop=(batches[m] == mine[-1]),
                                                    skip_group_check=True)
                        if batches[m] == mine[-1]:
                            last.then_inc(c_o, 1)

                    def step(n, last, u, loaded, ahead=True, beyond=True):
                        behind = last is not None
                        pe.wait_ge(c_mrow, n * 48 + 48)
                        k = 0
                        for what, a in schedule(ahead, beyond, behind):
                            slot = (FIRST - behind + k) % SLOTS
                            used = before_step(n, behind) + k
                            if what == "piece":
                                piece(n, a, u, behind)
                            elif what == "pv":
                                values(n, a, u)
                            elif what == "last pv":
                                values(last, a, (u - 1) % 4)
                            elif what != "join":
                                if what == "unit":
                                    score_unit(a, slot, (u + 1) % 4, used)
                                elif what == "next":
                                    if a == units(range(1))[0]:
                                        pe.wait_ge(c_ld[(u + 2) % 4], loaded)
                                    score_unit(a, slot, (u + 2) % 4, used)
                                elif what == "peak":
                                    peak(n + 1, slot, used)
                                elif what == "turn":
                                    turn(n, a, slot, used)
                                else:
                                    turn(last, a, slot, used)
                                k += 1

                    for k, unit in enumerate(units(range(EARLY, QH))):
                        score_unit(unit, k % SLOTS, 0, k)
                    peak(0, LATE % SLOTS, LATE)
                    pe.wait_ge(c_ld[1], LOADS * 16)
                    for k, unit in enumerate(units(range(1))):
                        score_unit(unit, (LATE + 1 + k) % SLOTS, 1, LATE + 1 + k)
                    pe.wait_ge(c_ld[0], LOADS * 16)
                    pe.wait_ge(c_one, 4)
                    step(0, None, 0, LOADS * 16)
                    with pe.Fori(0, QUADS // 4 - 1) as it:
                        for u in range(1, 5):
                            step(it * 4 + u, it * 4 + (u - 1), u % 4, (it + (1 + (u + 2) // 4)) * (LOADS * 16))
                    for n in range(QUADS - 3, QUADS):
                        step(n, n - 1, n % 4, QUADS // 4 * LOADS * 16, n < QUADS - 1, n < QUADS - 2)
                    values(QUADS - 1, NBATCH - 1, (QUADS - 1) % 4)
                    used = before_step(QUADS - 1, True) + 2
                    turn(QUADS - 1, 1, used % SLOTS, used)

        with ExitStack() as sd:
            ct = sb("d_ct", [P, 2, KC, P], stack=sd)
            rows = sb("d_rows", [P, TILES, E], stack=sd)
            xt = sb("d_xt", [P, KC, NB * S], stack=sd)
            st = sb("d_st", [P, TILES, 6], stack=sd)
            tmp = sb("d_tmp", [P, 6, TILES], stack=sd)
            mt = sb("d_mt", [P, KC, P], stack=sd)
            lg = sb("d_lg", [P, NEX], stack=sd)
            le = sb("d_le", [P, NEX], stack=sd)
            one = sb("d_one", [P, 8], stack=sd)
            bs = sb("d_bs", [P, E], stack=sd)
            weff = sb("d_weff", [P, NB, KC, E], stack=sd)

            d_tp = sem("d_tp")
            d_xt = sem("d_xt")
            d_p = sem("d_p")
            d_y = sem("d_y")
            d_var = sem("d_var")
            d_sd = sem("d_sd")
            d_xn = sem("d_xn")
            acc = sb("d_acc", [P, NB, E], stack=sd)
            acc_last = sb("d_acc_last", [P, E], stack=sd)
            d_a = sem("d_a")
            d_sum = sem("d_sum")
            d_mn = sem("d_mn")
            d_mt = sem("d_mt")
            d_lg = sem("d_lg")
            d_le = sem("d_le")
            d_ex = sem("d_ex")
            d_bs = sem("d_bs")
            d_we = sem("d_we")
            d_wf = sem("d_wf")
            d_o = sem("d_o")
            d_out = sem("d_out")
            d_v = sem("d_v")
            MEAN_ROWS = S - 1 - 107
            NG = TILES // GT
            SG = BT // GT
            Y_BANK, Y_RING, M_BANK, L_BANK = 2, 4, 6, 7
            turns = [("ctx", t) for t in range(3 * GT + 1)] + [("rows", t) for t in range(2 * GT)] \
                + [("ctx", t) for t in range(3 * GT + 1, TILES)] + [("rows", t) for t in range(2 * GT, TILES)]

            def roots(g, k):
                order = [(0, 0), (0, 1), (1, 0), (1, 1), (2, 0), (2, 1), (3, 0), (3, 1), (0, 2), (1, 2), (2, 2),
                         (3, 2), (3, 3)]
                return order.index((g, k)) + 1

            with nc.Block() as block:
                @block.sync
                def _(sp):
                    for t in range(TILES):
                        sp.wait_ge(d_o, t + 1)
                        sp.dma_start(out[t * P:(t + 1) * P, :], rows[:, t, :]).then_inc(d_out, 16)
                    sp.wait_ge(d_out, TILES * 16)

                @block.vector
                def _(dve):
                    ch = Chain(dve, d_v)
                    dve.wait_ge(w_d, W_D)

                    def finish(g, k, tiles=None):
                        tiles = tiles or range(g * GT, (g + 1) * GT)
                        part = slice(tiles[0], tiles[-1] + 1)
                        finish_stats(dve, d_var, d_sd, ch, st[:, part, :], tmp[:, :, part], len(tiles), E, None,
                                     roots(g, k))

                    def scaled(dst, src, t):
                        return nc.vector.tensor_scalar(dst, src, tmp[:, 0, t:t + 1], tmp[:, 5, t:t + 1],
                                                       ALU.subtract, ALU.mult)

                    def take(g, bias, first, tiles=None):
                        for t in tiles or range(g * GT, (g + 1) * GT):
                            n = first + t
                            dve.wait_ge(d_p, n + 1)
                            nc.vector.tensor_tensor(rows[:, t, :], psum[:, Y_BANK + n % Y_RING, :], bias[:, :],
                                                    ALU.add).then_inc(d_y, 1)
                            dve.wait_ge(d_y, n + 1)
                            last = nc.vector.bn_stats(st[:, t, :], rows[:, t, :])
                        ch.link(last)

                    def norms(g):
                        tiles = range(g * GT, (g + 1) * GT)
                        finish(g, 0)
                        for t in tiles:
                            last = scaled(rows[:, t, :], rows[:, t, :], t)
                        ch.link(last)
                        for t in tiles:
                            last = nc.vector.tensor_tensor(xs[:, t, :], xs[:, t, :], rows[:, t, :], ALU.add)
                        ch.link(last)
                        for t in tiles:
                            last = nc.vector.bn_stats(st[:, t, :], xs[:, t, :])
                        ch.link(last)
                        finish(g, 1)
                        for t in tiles:
                            scaled(rows[:, t, :], xs[:, t, :], t).then_inc(d_xn, 1)

                    def routing(b):
                        dve.wait_ge(d_lg, b + 1)
                        ch.link(nc.vector.tensor_tensor(lg[:, :], psum[:, L_BANK, 0:NEX], route_b[:, :], ALU.add))
                        ch.link(nc.vector.tensor_reduce(one[:, 0:1], lg[:, :], X_AXIS, ALU.max))
                        nc.vector.tensor_scalar(lg[:, :], lg[:, :], one[:, 0:1], None, ALU.subtract).then_inc(d_le, 1)
                        dve.wait_ge(d_ex, b + 1)
                        ch.link(nc.vector.tensor_reduce(one[:, 1:2], le[:, :], X_AXIS, ALU.add))
                        ch.link(nc.vector.reciprocal(one[:, 2:3], one[:, 1:2]))
                        ch.link(nc.vector.tensor_scalar(le[:, :], le[:, :], one[:, 2:3], None, ALU.mult))
                        ch.link(nc.vector.tensor_tensor(lg[:, :], le[:, :], own[:, :], ALU.mult))
                        ch.link(nc.vector.tensor_reduce(one[:, 3:4], lg[:, :], X_AXIS, ALU.add))
                        nc.vector.tensor_scalar(bs[:, :], lora_b[:, :], one[:, 3:4], None, ALU.mult).then_inc(d_bs, 1)

                    def weights(b):
                        for c in range(KC):
                            dve.wait_ge(d_we, b * KC + c + 1)
                            nc.vector.tensor_tensor(weff[:, b, c, :], psum[:, M_BANK + c % 2, :], w4[:, c, :],
                                                    ALU.add).then_inc(d_wf, 1)

                    def result(g, k=2, tiles=None):
                        tiles = tiles or range(g * GT, (g + 1) * GT)
                        finish(g, k, tiles)
                        for t in tiles:
                            last = scaled(rows[:, t, :], rows[:, t, :], t)
                        ch.link(last)
                        for t in tiles:
                            nc.vector.tensor_tensor(rows[:, t, :], xs[:, t, :], rows[:, t, :],
                                                    ALU.add).then_inc(d_o, 1)

                    for g in range(3):
                        take(g, bo, 0)
                        norms(g)
                    routing(0)
                    take(3, bo, 0)
                    weights(0)
                    norms(3)
                    take(0, b4, TILES)
                    result(0)
                    routing(1)
                    take(1, b4, TILES)
                    weights(1)
                    result(1)
                    take(2, b4, TILES)
                    result(2)
                    for k, tiles in ((2, range(TILES - 4, TILES - 2)), (3, range(TILES - 2, TILES))):
                        take(3, b4, TILES, tiles)
                        result(3, k, tiles)

                @block.gpsimd
                def _(pool):
                    k = 0
                    for b in range(NB):
                        for t in range(BT):
                            row = rows[:, b * BT + t, :]
                            pool.wait_ge(d_xn, b * BT + t + 1)
                            if t == 0:
                                last = nc.gpsimd.tensor_tensor(acc[:, b, :], row,
                                                               counted[:, 0, 0:1].broadcast_to([P, E]), ALU.mult)
                            elif t < BT - 1:
                                last = nc.gpsimd.tensor_tensor(acc[:, b, :], acc[:, b, :], row, ALU.add)
                            else:
                                nc.gpsimd.tensor_tensor(acc_last[:, :], row,
                                                        counted[:, 2, 0:1].broadcast_to([P, E]),
                                                        ALU.mult).then_inc(d_a, 1)
                                k += 1
                                pool.wait_ge(d_a, k)
                                nc.gpsimd.tensor_tensor(acc[:, b, :], acc[:, b, :], acc_last[:, :],
                                                        ALU.add).then_inc(d_sum, 1)
                                continue
                            last.then_inc(d_a, 1)
                            k += 1
                            pool.wait_ge(d_a, k)

                @block.scalar
                def _(act):
                    def copy(what, t):
                        r = turns.index((what, t))
                        act.wait_ge(d_tp, r + 1)
                        src = psum[:, r % 2, :].rearrange("p (c n) -> p c n", n=P)
                        dst = ct[:, t % 2, :, :] if what == "ctx" else xt[:, :, t * P:(t + 1) * P]
                        nc.scalar.activation(dst, src, ACT.Copy).then_inc(d_xt, 1)

                    def norm(g, k, lo=0, hi=GT):
                        root(act, d_var, d_sd, tmp[:, :, g * GT + lo:g * GT + hi], hi - lo, roots(g, k))

                    def mean(b):
                        act.wait_ge(d_mn, b + 1)
                        for c in range(KC):
                            last = nc.scalar.activation(mt[:, c, :],
                                                        psum[:, M_BANK, c * 8:c * 8 + 1].broadcast_to([P, P]),
                                                        ACT.Copy, scale=1.0 / MEAN_ROWS)
                        last.then_inc(d_mt, 1)

                    def exps(b):
                        act.wait_ge(d_le, b + 1)
                        nc.scalar.activation(le[:, :], lg[:, :], ACT.Exp).then_inc(d_ex, 1)

                    for t in range(6):
                        copy("ctx", t)
                    norm(0, 0)
                    copy("ctx", 6)
                    copy("ctx", 7)
                    norm(0, 1)
                    copy("ctx", 8)
                    copy("ctx", 9)
                    norm(1, 0)
                    copy("ctx", 10)
                    copy("ctx", 11)
                    norm(1, 1)
                    copy("ctx", 12)
                    for t in range(4):
                        copy("rows", t)
                    norm(2, 0)
                    for t in range(4, 8):
                        copy("rows", t)
                    mean(0)
                    copy("ctx", 13)
                    norm(2, 1)
                    exps(0)
                    for t in range(14, 16):
                        copy("ctx", t)
                    norm(3, 0)
                    norm(3, 1)
                    for t in range(8, 12):
                        copy("rows", t)
                    norm(0, 2)
                    for t in range(12, 16):
                        copy("rows", t)
                    mean(1)
                    exps(1)
                    norm(1, 2)
                    norm(2, 2)
                    norm(3, 2, 0, 2)
                    norm(3, 3, 2, 4)

                @block.tensor
                def _(pe):
                    def turn(what, t):
                        r = turns.index((what, t))
                        if what == "rows":
                            pe.wait_ge(d_xn, t + 1)
                        if r >= 2:
                            pe.wait_ge(d_xt, r - 1)
                        for c in range(KC):
                            src = ctx[:, (t // BT) * KC + c, t % BT, :] if what == "ctx" \
                                else rows[:, t, c * P:(c + 1) * P]
                            last = nc.tensor.transpose(psum[:, r % 2, c * P:(c + 1) * P], src, ident[:, :])
                        last.then_inc(d_tp, 1)

                    def product(n, lhs, w):
                        if n >= Y_RING:
                            pe.wait_ge(d_y, n - Y_RING + 1)
                        for c in range(KC):
                            last = nc.tensor.matmul(psum[:, Y_BANK + n % Y_RING, :], lhs(c), w[:, c, :],
                                                    start=(c == 0), stop=(c == KC - 1))
                        last.then_inc(d_p, 1)

                    def project(tiles):
                        for t in tiles:
                            if t + 1 < TILES:
                                turn("ctx", t + 1)
                            pe.wait_ge(d_xt, turns.index(("ctx", t)) + 1)
                            product(t, lambda c: ct[:, t % 2, c, :], wo)

                    def mean(b):
                        pe.wait_ge(d_sum, b + 1)
                        for c in range(KC):
                            last = nc.tensor.matmul(psum[:, M_BANK, c * 8:c * 8 + 8], acc[:, b, c * P:(c + 1) * P],
                                                    counted[:, 1, :], start=True, stop=True)
                        last.then_inc(d_mn, 1)

                    def logits(b):
                        pe.wait_ge(d_mt, b + 1)
                        for c in range(KC):
                            last = nc.tensor.matmul(psum[:, L_BANK, 0:NEX], mt[:, c, :], route_w[:, c, :],
                                                    start=(c == 0), stop=(c == KC - 1))
                        last.then_inc(d_lg, 1)

                    def low_rank(b):
                        pe.wait_ge(d_bs, b + 1)
                        for c in range(KC):
                            if c >= 2:
                                pe.wait_ge(d_wf, b * KC + c - 1)
                            nc.tensor.matmul(psum[:, M_BANK + c % 2, :], lora_a[:, c * P:(c + 1) * P], bs[:, :],
                                             start=True, stop=True).then_inc(d_we, 1)

                    def block4(g, tiles=None):
                        pe.wait_ge(d_wf, (g // SG + 1) * KC)
                        pe.wait_ge(d_xt, turns.index(("rows", (g + 1) * GT - 1)) + 1)
                        for t in tiles or range(g * GT, (g + 1) * GT):
                            product(TILES + t, lambda c: xt[:, c, t * P:(t + 1) * P], weff[:, g // SG, :, :])

                    pe.wait_ge(w_d, W_D)
                    turn("ctx", 0)
                    project(range(3 * GT))
                    for t in range(BT):
                        turn("rows", t)
                    mean(0)
                    project(range(3 * GT, 3 * GT + 1))
                    logits(0)
                    project(range(3 * GT + 1, TILES))
                    low_rank(0)
                    block4(0)
                    for t in range(BT, TILES):
                        turn("rows", t)
                    mean(1)
                    block4(1, range(GT, GT + 1))
                    logits(1)
                    block4(1, range(GT + 1, 2 * GT))
                    low_rank(1)
                    block4(2)
                    block4(3)


def constants():
    half = HALF
    inv_freq = (np.float32(1.0) / np.float32(10000.0) ** (np.arange(half, dtype=np.float32) / np.float32(half)))
    ang = np.arange(S, dtype=np.float32)[:, None] * inv_freq.astype(np.float32)[None, :]
    cos, sin = np.cos(ang).astype(np.float32), np.sin(ang).astype(np.float32)
    causal = np.zeros((P, 512), np.float32)
    causal[:, 512 - P:] = np.triu(np.full((P, P), MASK / SCALE3, np.float32), 1)
    own = np.zeros((P, NEX), np.float32)
    own[np.arange(P), np.arange(P) // RANK] = 2.0
    counted = np.ones((P, 3, 8), np.float32)
    counted[:107, 0, :] = 0.0
    counted[P - 1:, 2, :] = 0.0
    return {"ident": np.eye(P, dtype=np.float32), "rope_c": np.concatenate([cos, cos], 1),
            "rope_s": np.concatenate([-sin, sin], 1), "causal": causal, "own": own,
            "counted": counted.reshape(P, 3 * 8)}


def kernel(L0_attn_x, L0_attn_Wq, L0_attn_bq, L0_attn_Wk, L0_attn_bk, L0_attn_Wv, L0_attn_bv, L0_ffn_gate_w,
           L0_ffn_up_w, L0_ffn_down_w, L0_ffn_fc1_w, L0_ffn_fc2_w, L0_ffn_expert_w, L0_ffn_ln_gamma, L0_ffn_ln_beta,
           L1_attn_qkv_w, L1_attn_qkv_b, L1_attn_out_w, L1_attn_out_b, L1_ffn_W, L1_ffn_b, L1_ffn_A, L1_ffn_B,
           L1_ffn_router_W, L1_ffn_router_b):
    import concourse.bacc as bacc
    from concourse.bass_utils import run_bass_kernel_spmd

    arrays = {
        "x": np.reshape(L0_attn_x, (NB * S, E)),
        "wq0": np.reshape(L0_attn_Wq, (E, I0 * R0)), "bq0": np.reshape(L0_attn_bq, (I0 * R0,)),
        "wk0": np.reshape(L0_attn_Wk, (E, I0)), "bk0": np.reshape(L0_attn_bk, (I0,)),
        "wv0": np.reshape(L0_attn_Wv, (E, I0)), "bv0": np.reshape(L0_attn_bv, (I0,)),
        "gate": L0_ffn_gate_w, "up": L0_ffn_up_w, "down": L0_ffn_down_w, "fc1": L0_ffn_fc1_w, "fc2": L0_ffn_fc2_w,
        "expert_t": np.transpose(L0_ffn_expert_w), "gamma": L0_ffn_ln_gamma, "beta": L0_ffn_ln_beta,
        "w3": L1_attn_qkv_w, "b3": L1_attn_qkv_b, "wo": L1_attn_out_w, "bo": L1_attn_out_b,
        "w4": np.transpose(L1_ffn_W), "b4": L1_ffn_b,
        "lora_a": np.reshape(L1_ffn_A, (NEX * RANK, E)),
        "lora_b": np.reshape(np.transpose(L1_ffn_B, (0, 2, 1)), (NEX * RANK, E)),
        "route_w": np.transpose(L1_ffn_router_W), "route_b": L1_ffn_router_b,
    }
    arrays.update(constants())
    nc = bacc.Bacc("TRN2", target_bir_lowering=False, num_devices=1)
    fed, ins = {}, {}
    for name, a in arrays.items():
        a = np.ascontiguousarray(a)
        fed[f"in_{name}"] = a
        ins[name] = nc.dram_tensor(f"in_{name}", a.shape, mybir.dt.from_np(a.dtype), kind="ExternalInput").ap()
    out = nc.dram_tensor("out", (NB * S, E), F32, kind="ExternalOutput").ap()
    layers(nc, ins, out)
    got = run_bass_kernel_spmd(nc, [fed], core_ids=[0])
    return got.results[0]["out"].reshape(NB, S, E)
```
